# Optimizing a Trainium2 kernel written in Bass

```python
import numpy as np
import jax
import jax.numpy as jnp

def _softmax(x, axis=-1):
    return jax.nn.softmax(x, axis=axis)

def _gelu(x):
    return jax.nn.gelu(x, approximate=True)

def _silu(x):
    return jax.nn.silu(x)

def _sigmoid(x):
    return jax.nn.sigmoid(x)

def _layernorm(x, axis=-1, eps=1e-05):
    m = jnp.mean(x, axis=axis, keepdims=True)
    v = jnp.var(x, axis=axis, keepdims=True)
    return (x - m) / jnp.sqrt(v + eps)

def _scatter_add(tgt, idx, src, axis=0):
    return tgt.at[idx].add(src)

def _segment_sum(src, seg, n):
    return jax.ops.segment_sum(src, seg, n)
kernel_name = 'mk_decoder_postln_d2_seqx_r4_be6184'

def setup_inputs(seed: int=0):
    np.random.seed(seed)
    _w = jnp.asarray

    def _rec_inputs():
        import jax
        import jax.numpy as jnp
        _rk = jax.random.key(seed)
        x = -0.0002928 + 1 * jax.random.normal(jax.random.fold_in(_rk, 1), (32, 256, 256), jnp.float32)
        _lenS = 256 - jax.random.randint(jax.random.fold_in(_rk, 7), (32,), 0, max(1, 256 // 4) + 1, jnp.int32)
        _lenS2 = 77 - jax.random.randint(jax.random.fold_in(_rk, 8), (32,), 0, max(1, 77 // 4) + 1, jnp.int32)
        _ctx_512P = jax.random.normal(jax.random.fold_in(_rk, 11), (32, 16, 128), jnp.float32)
        _ctx_512c = jax.random.dirichlet(jax.random.fold_in(_rk, 511), 0.3 * jnp.ones((16,), jnp.float32), (32, 77))
        _ctx_512t = jnp.einsum('bsk,bkd->bsd', _ctx_512c, _ctx_512P)
        _ctx_512t = _ctx_512t * jax.lax.rsqrt(jnp.mean(jnp.square(_ctx_512t)) + 1e-12) * 0.953939
        ctx_512 = -1.52775e-05 + 0.999936 * (_ctx_512t + 0.3 * jax.random.normal(jax.random.fold_in(_rk, 611), (32, 77, 128), jnp.float32))
        return (x, ctx_512)
    x, ctx_512 = _rec_inputs()

    def _L0_attn_setup():
        import jax, jax.numpy as jnp
        import numpy as np
        import math
        IN_DIM = 256
        LATENT_DIM = 64
        OUT_DIM = 256

        def _kaiming(key, fan_out, fan_in):
            std = math.sqrt(2.0 / fan_in)
            return jax.random.normal(key, (fan_out, fan_in), dtype=jnp.float32) * std
        key = jax.random.key(seed)
        kx, kt, kp, kg = jax.random.split(key, 4)
        x = jax.random.normal(kx, (8, 1024, IN_DIM), dtype=jnp.float32)
        W_theta = _kaiming(kt, LATENT_DIM, IN_DIM)
        W_phi = _kaiming(kp, LATENT_DIM, IN_DIM)
        W_g = _kaiming(kg, OUT_DIM, IN_DIM)
        return {'x': x, 'W_theta': W_theta, 'W_phi': W_phi, 'W_g': W_g}
    _L0_attn_all = _L0_attn_setup()
    _L0_attn_in = {k: v for k, v in _L0_attn_all.items() if k in ('W_theta', 'W_phi', 'W_g')}
    del _L0_attn_all

    def _L0_xattn_setup():
        import jax, jax.numpy as jnp
        import numpy as np
        NUM_HEADS = 16
        HEAD_DIM = 64
        Q_DIM = 256
        KV_DIM = 128
        INNER = NUM_HEADS * HEAD_DIM
        key = jax.random.key(seed)
        ks = jax.random.split(key, 7)
        B, N, M = (32, 128, 512)
        q = jax.random.normal(ks[0], (B, N, Q_DIM), dtype=jnp.float32)
        kv = jax.random.normal(ks[1], (B, M, KV_DIM), dtype=jnp.float32)
        Wq = jax.random.normal(ks[2], (Q_DIM, INNER), dtype=jnp.float32) / np.sqrt(Q_DIM)
        Wk = jax.random.normal(ks[3], (KV_DIM, INNER), dtype=jnp.float32) / np.sqrt(KV_DIM)
        Wv = jax.random.normal(ks[4], (KV_DIM, INNER), dtype=jnp.float32) / np.sqrt(KV_DIM)
        Wo = jax.random.normal(ks[5], (INNER, Q_DIM), dtype=jnp.float32) / np.sqrt(INNER)
        bo = jax.random.normal(ks[6], (Q_DIM,), dtype=jnp.float32) * 0.01
        return {'q': q, 'kv': kv, 'Wq': Wq, 'Wk': Wk, 'Wv': Wv, 'Wo': Wo, 'bo': bo}
    _L0_xattn_all = _L0_xattn_setup()
    _L0_xattn_in = {k: v for k, v in _L0_xattn_all.items() if k in ('Wq', 'Wk', 'Wv', 'Wo', 'bo')}
    del _L0_xattn_all

    def _L0_ffn_setup():
        import jax, jax.numpy as jnp
        import numpy as np
        NUM_EXPERTS = 8
        HIDDEN = 256
        INTER = 256
        BATCH = 2
        SEQ = 256
        TOP_K = 2
        SWIGLU_ALPHA = 1.702
        LIMIT = 7.0

        def _grouped_mm(x, w, expert_ids):
            onehot = jax.nn.one_hot(expert_ids, w.shape[0], dtype=x.dtype)
            y_all = jnp.einsum('tk,ekn->etn', x, w)
            return jnp.einsum('te,etn->tn', onehot, y_all)

        def _gpt_oss_swiglu(x):
            gate = jnp.minimum(x[..., ::2], LIMIT)
            up = jnp.clip(x[..., 1::2], -LIMIT, LIMIT)
            glu = gate * jax.nn.sigmoid(gate * SWIGLU_ALPHA)
            return (up + 1.0) * glu
        key = jax.random.key(seed)
        ks = jax.random.split(key, 7)
        hidden_states = jax.random.normal(ks[0], (BATCH, SEQ, HIDDEN), jnp.float32)
        router_indices = jax.random.randint(ks[1], (BATCH * SEQ, TOP_K), 0, NUM_EXPERTS)
        routing_weights = jax.nn.softmax(jax.random.normal(ks[2], (BATCH * SEQ, NUM_EXPERTS), jnp.float32), axis=-1)
        scale = 0.02
        gate_up_proj = jax.random.normal(ks[3], (NUM_EXPERTS, HIDDEN, 2 * INTER), jnp.float32) * scale
        gate_up_proj_bias = jax.random.normal(ks[4], (NUM_EXPERTS, 2 * INTER), jnp.float32) * scale
        down_proj = jax.random.normal(ks[5], (NUM_EXPERTS, INTER, HIDDEN), jnp.float32) * scale
        down_proj_bias = jax.random.normal(ks[6], (NUM_EXPERTS, HIDDEN), jnp.float32) * scale
        return {'hidden_states': hidden_states, 'router_indices': router_indices, 'routing_weights': routing_weights, 'gate_up_proj': gate_up_proj, 'gate_up_proj_bias': gate_up_proj_bias, 'down_proj': down_proj, 'down_proj_bias': down_proj_bias}
    _L0_ffn_all = _L0_ffn_setup()
    _L0_ffn_in = {k: v for k, v in _L0_ffn_all.items() if k in ('router_indices', 'routing_weights', 'gate_up_proj', 'gate_up_proj_bias', 'down_proj', 'down_proj_bias')}
    del _L0_ffn_all

    def _L1_attn_setup():
        import jax, jax.numpy as jnp
        import numpy as np
        EPS = 1e-06
        CHUNK = 64
        N_HEADS = 16
        GATE_NORM = 16.0

        def rmsnorm(x, eps=EPS):
            return x * jax.lax.rsqrt(jnp.mean(x * x, axis=-1, keepdims=True) + eps)

        def chunk_gate_retention(q, k, v, gt, chunk_size):
            b, h, t, d = q.shape
            c = chunk_size
            n = t // c
            scale = d ** (-0.5)
            q = q.reshape(b, h, n, c, d) * scale
            k = k.reshape(b, h, n, c, d)
            v = v.reshape(b, h, n, c, d)
            g = gt.reshape(b, h, n, c)
            bc = jnp.cumsum(g, axis=-1)
            B = bc[..., -1:]
            decay = jnp.exp(bc[..., :, None] - bc[..., None, :])
            mask = jnp.tril(jnp.ones((c, c), dtype=bool))
            A = jnp.einsum('bhnid,bhnjd->bhnij', q, k) * jnp.where(mask, decay, 0.0)
            o_intra = jnp.einsum('bhnij,bhnjd->bhnid', A, v)
            kd = k * jnp.exp(B - bc)[..., None]
            kv = jnp.einsum('bhncd,bhnce->bhnde', kd, v)
            qd = q * jnp.exp(bc)[..., None]

            def step(S, inp):
                qd_n, kv_n, B_n = inp
                o_cross = jnp.einsum('bhcd,bhde->bhce', qd_n, S)
                S_new = jnp.exp(B_n)[..., None] * S + kv_n
                return (S_new, o_cross)
            S0 = jnp.zeros((b, h, d, d), dtype=q.dtype)
            inps = (jnp.moveaxis(qd, 2, 0), jnp.moveaxis(kv, 2, 0), jnp.moveaxis(B, 2, 0))
            S_last, o_cross = jax.lax.scan(step, S0, inps)
            o_cross = jnp.moveaxis(o_cross, 0, 2)
            o = (o_intra + o_cross).reshape(b, h, t, d)
            return (o, S_last)
        key = jax.random.key(seed)
        ks = jax.random.split(key, 7)
        dim, nh = (256, N_HEADS)
        s = 0.03
        return {'x': jax.random.normal(ks[0], (2, 2048, dim), dtype=jnp.float32), 'Wq': jax.random.normal(ks[1], (dim, dim), dtype=jnp.float32) * s, 'Wk': jax.random.normal(ks[2], (dim, dim), dtype=jnp.float32) * s, 'Wv': jax.random.normal(ks[3], (dim, dim), dtype=jnp.float32) * s, 'Wg': jax.random.normal(ks[4], (dim, dim), dtype=jnp.float32) * s, 'Wgt': jax.random.normal(ks[5], (dim, nh), dtype=jnp.float32) * s, 'Wo': jax.random.normal(ks[6], (dim, dim), dtype=jnp.float32) * s}
    _L1_attn_all = _L1_attn_setup()
    _L1_attn_in = {k: v for k, v in _L1_attn_all.items() if k in ('Wq', 'Wk', 'Wv', 'Wg', 'Wgt', 'Wo')}
    del _L1_attn_all

    def _L1_xattn_setup():
        import jax, jax.numpy as jnp
        import numpy as np
        B, LQ, LK = (8, 512, 512)
        QD, KD, VD = (256, 128, 128)
        key = jax.random.key(seed)
        ks = jax.random.split(key, 9)
        s = 0.02
        return {'query': jax.random.normal(ks[0], (B, LQ, QD), jnp.float32), 'key': jax.random.normal(ks[1], (B, LK, KD), jnp.float32), 'value': jax.random.normal(ks[2], (B, LK, VD), jnp.float32), 'Wq': jax.random.normal(ks[3], (QD, QD), jnp.float32) * s, 'bq': jnp.zeros((QD,), jnp.float32), 'Wk': jax.random.normal(ks[4], (KD, QD), jnp.float32) * s, 'bk': jnp.zeros((QD,), jnp.float32), 'Wv': jax.random.normal(ks[5], (VD, QD), jnp.float32) * s, 'bv': jnp.zeros((QD,), jnp.float32)}
    _L1_xattn_all = _L1_xattn_setup()
    _L1_xattn_in = {k: v for k, v in _L1_xattn_all.items() if k in ('Wq', 'bq', 'Wk', 'bk', 'Wv', 'bv')}
    del _L1_xattn_all

    def _L1_ffn_setup():
        import jax, jax.numpy as jnp
        import numpy as np
        B, L, H, E, I = (4, 512, 256, 8, 1024)
        S = B * L
        CAP_FACTOR_EVAL = 2.0
        MIN_CAP = 4
        _cap = int(np.floor(CAP_FACTOR_EVAL * S / E))
        _cap += _cap % 2
        CAPACITY = max(_cap, MIN_CAP)

        def _layer_norm(x, g, b, eps=1e-05):
            mu = x.mean(-1, keepdims=True)
            var = ((x - mu) ** 2).mean(-1, keepdims=True)
            return (x - mu) * jax.lax.rsqrt(var + eps) * g + b
        key = jax.random.key(seed)
        ks = jax.random.split(key, 8)
        gate_std = float(np.sqrt(0.1 / H))
        return {'inputs': jax.random.normal(ks[0], (B, L, H), jnp.float32), 'gate_weight': jax.random.normal(ks[1], (E, H), jnp.float32) * gate_std, 'ln_gamma': jnp.ones((H,), jnp.float32), 'ln_beta': jnp.zeros((H,), jnp.float32), 'wi': jax.random.normal(ks[2], (E, H, I), jnp.float32) * float(1.0 / np.sqrt(H)), 'wo': jax.random.normal(ks[3], (E, I, H), jnp.float32) * float(1.0 / np.sqrt(I)), 'conf_w1': jax.random.normal(ks[4], (H // 2, H), jnp.float32) * float(np.sqrt(2.0 / (H + H // 2))), 'conf_b1': -jnp.ones((H // 2,), jnp.float32), 'conf_w2': jax.random.normal(ks[5], (1, H // 2), jnp.float32) * float(np.sqrt(2.0 / (1 + H // 2))), 'conf_b2': -jnp.ones((1,), jnp.float32), 'comp_w': jax.random.normal(ks[6], (1, H), jnp.float32) * float(1.0 / np.sqrt(H)), 'comp_b': jnp.zeros((1,), jnp.float32)}
    _L1_ffn_all = _L1_ffn_setup()
    _L1_ffn_in = {k: v for k, v in _L1_ffn_all.items() if k in ('gate_weight', 'ln_gamma', 'ln_beta', 'wi', 'wo', 'conf_w1', 'conf_b1', 'conf_w2', 'conf_b2', 'comp_w', 'comp_b')}
    del _L1_ffn_all
    return {'x': x, 'ctx_512': ctx_512, 'L0_attn_W_theta': _L0_attn_in['W_theta'], 'L0_attn_W_phi': _L0_attn_in['W_phi'], 'L0_attn_W_g': _L0_attn_in['W_g'], 'L0_xattn_Wq': _L0_xattn_in['Wq'], 'L0_xattn_Wk': _L0_xattn_in['Wk'], 'L0_xattn_Wv': _L0_xattn_in['Wv'], 'L0_xattn_Wo': _L0_xattn_in['Wo'], 'L0_xattn_bo': _L0_xattn_in['bo'], 'L0_ffn_router_indices': _L0_ffn_in['router_indices'], 'L0_ffn_routing_weights': _L0_ffn_in['routing_weights'], 'L0_ffn_gate_up_proj': _L0_ffn_in['gate_up_proj'], 'L0_ffn_gate_up_proj_bias': _L0_ffn_in['gate_up_proj_bias'], 'L0_ffn_down_proj': _L0_ffn_in['down_proj'], 'L0_ffn_down_proj_bias': _L0_ffn_in['down_proj_bias'], 'L1_attn_Wq': _L1_attn_in['Wq'], 'L1_attn_Wk': _L1_attn_in['Wk'], 'L1_attn_Wv': _L1_attn_in['Wv'], 'L1_attn_Wg': _L1_attn_in['Wg'], 'L1_attn_Wgt': _L1_attn_in['Wgt'], 'L1_attn_Wo': _L1_attn_in['Wo'], 'L1_xattn_Wq': _L1_xattn_in['Wq'], 'L1_xattn_bq': _L1_xattn_in['bq'], 'L1_xattn_Wk': _L1_xattn_in['Wk'], 'L1_xattn_bk': _L1_xattn_in['bk'], 'L1_xattn_Wv': _L1_xattn_in['Wv'], 'L1_xattn_bv': _L1_xattn_in['bv'], 'L1_ffn_gate_weight': _L1_ffn_in['gate_weight'], 'L1_ffn_ln_gamma': _L1_ffn_in['ln_gamma'], 'L1_ffn_ln_beta': _L1_ffn_in['ln_beta'], 'L1_ffn_wi': _L1_ffn_in['wi'], 'L1_ffn_wo': _L1_ffn_in['wo'], 'L1_ffn_conf_w1': _L1_ffn_in['conf_w1'], 'L1_ffn_conf_b1': _L1_ffn_in['conf_b1'], 'L1_ffn_conf_w2': _L1_ffn_in['conf_w2'], 'L1_ffn_conf_b2': _L1_ffn_in['conf_b2'], 'L1_ffn_comp_w': _L1_ffn_in['comp_w'], 'L1_ffn_comp_b': _L1_ffn_in['comp_b']}

def reference(x, ctx_512, L0_attn_W_theta, L0_attn_W_phi, L0_attn_W_g, L0_xattn_Wq, L0_xattn_Wk, L0_xattn_Wv, L0_xattn_Wo, L0_xattn_bo, L0_ffn_router_indices, L0_ffn_routing_weights, L0_ffn_gate_up_proj, L0_ffn_gate_up_proj_bias, L0_ffn_down_proj, L0_ffn_down_proj_bias, L1_attn_Wq, L1_attn_Wk, L1_attn_Wv, L1_attn_Wg, L1_attn_Wgt, L1_attn_Wo, L1_xattn_Wq, L1_xattn_bq, L1_xattn_Wk, L1_xattn_bk, L1_xattn_Wv, L1_xattn_bv, L1_ffn_gate_weight, L1_ffn_ln_gamma, L1_ffn_ln_beta, L1_ffn_wi, L1_ffn_wo, L1_ffn_conf_w1, L1_ffn_conf_b1, L1_ffn_conf_w2, L1_ffn_conf_b2, L1_ffn_comp_w, L1_ffn_comp_b):
    import jax
    import jax.numpy as jnp

    def _L0_attn_ref(x, W_theta, W_phi, W_g):
        import jax, jax.numpy as jnp
        import numpy as np
        import math
        IN_DIM = 256
        LATENT_DIM = 64
        OUT_DIM = 256

        def _kaiming(key, fan_out, fan_in):
            std = math.sqrt(2.0 / fan_in)
            return jax.random.normal(key, (fan_out, fan_in), dtype=jnp.float32) * std
        theta_x = jnp.einsum('bnf,lf->bnl', x, W_theta)
        phi_x = jnp.einsum('bnf,lf->bnl', x, W_phi)
        fun_g_x = jnp.einsum('bnf,of->bno', x, W_g)
        scale = 1.0 / math.sqrt(IN_DIM)
        att = jnp.einsum('bnl,bml->bnm', theta_x, phi_x) * scale
        return jnp.einsum('bnm,bmo->bno', att, fun_g_x)

    def _L0_xattn_ref(q, kv, Wq, Wk, Wv, Wo, bo):
        import jax, jax.numpy as jnp
        import numpy as np
        NUM_HEADS = 16
        HEAD_DIM = 64
        Q_DIM = 256
        KV_DIM = 128
        INNER = NUM_HEADS * HEAD_DIM
        B, N, _ = q.shape
        M = kv.shape[1]
        scale = HEAD_DIM ** (-0.5)
        qh = (q @ Wq).reshape(B, N, NUM_HEADS, HEAD_DIM).transpose(0, 2, 1, 3)
        kh = (kv @ Wk).reshape(B, M, NUM_HEADS, HEAD_DIM).transpose(0, 2, 1, 3)
        vh = (kv @ Wv).reshape(B, M, NUM_HEADS, HEAD_DIM).transpose(0, 2, 1, 3)
        scores = jnp.einsum('bhnd,bhmd->bhnm', qh, kh) * scale
        attn = jax.nn.softmax(scores, axis=-1)
        out = jnp.einsum('bhnm,bhmd->bhnd', attn, vh)
        out = out.transpose(0, 2, 1, 3).reshape(B, N, INNER)
        return out @ Wo + bo

    def _L0_ffn_ref(hidden_states, router_indices, routing_weights, gate_up_proj, gate_up_proj_bias, down_proj, down_proj_bias):
        import jax, jax.numpy as jnp
        import numpy as np
        NUM_EXPERTS = 8
        HIDDEN = 256
        INTER = 256
        BATCH = 2
        SEQ = 256
        TOP_K = 2
        SWIGLU_ALPHA = 1.702
        LIMIT = 7.0

        def _grouped_mm(x, w, expert_ids):
            onehot = jax.nn.one_hot(expert_ids, w.shape[0], dtype=x.dtype)
            y_all = jnp.einsum('tk,ekn->etn', x, w)
            return jnp.einsum('te,etn->tn', onehot, y_all)

        def _gpt_oss_swiglu(x):
            gate = jnp.minimum(x[..., ::2], LIMIT)
            up = jnp.clip(x[..., 1::2], -LIMIT, LIMIT)
            glu = gate * jax.nn.sigmoid(gate * SWIGLU_ALPHA)
            return (up + 1.0) * glu
        B = hidden_states.shape[0]
        H = hidden_states.shape[-1]
        x = hidden_states.reshape(-1, H)
        M = x.shape[0]
        top_k = router_indices.shape[1]
        num_experts = gate_up_proj.shape[0]
        topk_weights = jnp.take_along_axis(routing_weights, router_indices, axis=1)
        flat_experts = router_indices.reshape(-1)
        sort_idx = jnp.argsort(flat_experts)
        sorted_pos = sort_idx // top_k
        expert_sorted = flat_experts[sort_idx]
        grouped = x[sorted_pos]
        gate_up = _grouped_mm(grouped, gate_up_proj, expert_sorted)
        gate_up = gate_up + gate_up_proj_bias[expert_sorted]
        inter = _gpt_oss_swiglu(gate_up)
        down = _grouped_mm(inter, down_proj, expert_sorted)
        down = down + down_proj_bias[expert_sorted]
        down = down * topk_weights.reshape(-1)[sort_idx][:, None]
        out = jnp.zeros((M, H), x.dtype).at[sorted_pos].add(down)
        return out.reshape(B, -1, H)

    def _L1_attn_ref(x, Wq, Wk, Wv, Wg, Wgt, Wo):
        import jax, jax.numpy as jnp
        import numpy as np
        EPS = 1e-06
        CHUNK = 64
        N_HEADS = 16
        GATE_NORM = 16.0

        def rmsnorm(x, eps=EPS):
            return x * jax.lax.rsqrt(jnp.mean(x * x, axis=-1, keepdims=True) + eps)

        def chunk_gate_retention(q, k, v, gt, chunk_size):
            b, h, t, d = q.shape
            c = chunk_size
            n = t // c
            scale = d ** (-0.5)
            q = q.reshape(b, h, n, c, d) * scale
            k = k.reshape(b, h, n, c, d)
            v = v.reshape(b, h, n, c, d)
            g = gt.reshape(b, h, n, c)
            bc = jnp.cumsum(g, axis=-1)
            B = bc[..., -1:]
            decay = jnp.exp(bc[..., :, None] - bc[..., None, :])
            mask = jnp.tril(jnp.ones((c, c), dtype=bool))
            A = jnp.einsum('bhnid,bhnjd->bhnij', q, k) * jnp.where(mask, decay, 0.0)
            o_intra = jnp.einsum('bhnij,bhnjd->bhnid', A, v)
            kd = k * jnp.exp(B - bc)[..., None]
            kv = jnp.einsum('bhncd,bhnce->bhnde', kd, v)
            qd = q * jnp.exp(bc)[..., None]

            def step(S, inp):
                qd_n, kv_n, B_n = inp
                o_cross = jnp.einsum('bhcd,bhde->bhce', qd_n, S)
                S_new = jnp.exp(B_n)[..., None] * S + kv_n
                return (S_new, o_cross)
            S0 = jnp.zeros((b, h, d, d), dtype=q.dtype)
            inps = (jnp.moveaxis(qd, 2, 0), jnp.moveaxis(kv, 2, 0), jnp.moveaxis(B, 2, 0))
            S_last, o_cross = jax.lax.scan(step, S0, inps)
            o_cross = jnp.moveaxis(o_cross, 0, 2)
            o = (o_intra + o_cross).reshape(b, h, t, d)
            return (o, S_last)
        b, t, dim = x.shape
        h = N_HEADS
        d = dim // h
        q = rmsnorm(x @ Wq)
        k = rmsnorm(x @ Wk)
        v = rmsnorm(x @ Wv)
        g = x @ Wg
        gt = jax.nn.log_sigmoid(x @ Wgt) / GATE_NORM
        qr = q.reshape(b, t, h, d).transpose(0, 2, 1, 3)
        kr = k.reshape(b, t, h, d).transpose(0, 2, 1, 3)
        vr = v.reshape(b, t, h, d).transpose(0, 2, 1, 3)
        gtr = gt.transpose(0, 2, 1)
        o, _ = chunk_gate_retention(qr, kr, vr, gtr, CHUNK)
        o = rmsnorm(o)
        o = o.transpose(0, 2, 1, 3).reshape(b, t, dim)
        o = jax.nn.silu(g) * o
        return o @ Wo

    def _L1_xattn_ref(query, key, value, Wq, bq, Wk, bk, Wv, bv):
        import jax, jax.numpy as jnp
        import numpy as np
        B, LQ, LK = (8, 512, 512)
        QD, KD, VD = (256, 128, 128)
        q = jnp.einsum('bld,de->ble', query, Wq) + bq
        k = jnp.einsum('bld,de->ble', key, Wk) + bk
        v = jnp.einsum('bld,de->ble', value, Wv) + bv
        scores = jnp.einsum('bqe,bke->bqk', q, k)
        attn = jax.nn.softmax(scores, axis=-1)
        out = jnp.einsum('bqk,bke->bqe', attn, v)
        return out

    def _L1_ffn_ref(inputs, gate_weight, ln_gamma, ln_beta, wi, wo, conf_w1, conf_b1, conf_w2, conf_b2, comp_w, comp_b):
        import jax, jax.numpy as jnp
        import numpy as np
        B, L, H, E, I = (4, 512, 256, 8, 1024)
        S = B * L
        CAP_FACTOR_EVAL = 2.0
        MIN_CAP = 4
        _cap = int(np.floor(CAP_FACTOR_EVAL * S / E))
        _cap += _cap % 2
        CAPACITY = max(_cap, MIN_CAP)

        def _layer_norm(x, g, b, eps=1e-05):
            mu = x.mean(-1, keepdims=True)
            var = ((x - mu) ** 2).mean(-1, keepdims=True)
            return (x - mu) * jax.lax.rsqrt(var + eps) * g + b
        tokens = inputs.reshape(-1, H)
        residual = tokens
        tokens = _layer_norm(tokens, ln_gamma, ln_beta)
        complexity_score = jax.nn.sigmoid(tokens @ comp_w.T + comp_b).mean()
        hdn = jax.nn.relu(tokens @ conf_w1.T + conf_b1)
        confidence_score = jax.nn.sigmoid(hdn @ conf_w2.T + conf_b2).mean()
        logits = tokens.astype(jnp.float32) @ gate_weight.astype(jnp.float32).T
        probs = jax.nn.softmax(logits, axis=-1)
        top1 = jnp.argmax(logits, axis=-1)
        onehot = jax.nn.one_hot(top1, E, dtype=jnp.int32)
        rank_e = jnp.cumsum(onehot, axis=0) - onehot
        rank = jnp.sum(rank_e * onehot, axis=-1)
        keep = rank < CAPACITY
        weight = jnp.take_along_axis(probs, top1[:, None], axis=-1)[:, 0]
        weight = (weight * keep).astype(tokens.dtype)
        slot = jnp.where(keep, rank, 0)
        dispatch = jnp.zeros((E, CAPACITY, H), tokens.dtype)
        dispatch = dispatch.at[top1, slot].add(tokens * keep[:, None])
        h = jax.nn.gelu(jnp.einsum('ech,ehi->eci', dispatch, wi), approximate=False)
        expert_out = jnp.einsum('eci,eih->ech', h, wo)
        combined = weight[:, None] * expert_out[top1, slot]
        out = (residual + combined).reshape(inputs.shape)
        return out
    x = _layernorm(x + _L0_attn_ref(x, L0_attn_W_theta, L0_attn_W_phi, L0_attn_W_g), axis=-1)
    x = _layernorm(x + _L0_xattn_ref(x, ctx_512, L0_xattn_Wq, L0_xattn_Wk, L0_xattn_Wv, L0_xattn_Wo, L0_xattn_bo), axis=-1)
    x = _layernorm(x + _L0_ffn_ref(x, L0_ffn_router_indices, L0_ffn_routing_weights, L0_ffn_gate_up_proj, L0_ffn_gate_up_proj_bias, L0_ffn_down_proj, L0_ffn_down_proj_bias), axis=-1)
    x = _layernorm(x + _L1_attn_ref(x, L1_attn_Wq, L1_attn_Wk, L1_attn_Wv, L1_attn_Wg, L1_attn_Wgt, L1_attn_Wo), axis=-1)
    x = _layernorm(x + _L1_xattn_ref(x, ctx_512, ctx_512, L1_xattn_Wq, L1_xattn_bq, L1_xattn_Wk, L1_xattn_bk, L1_xattn_Wv, L1_xattn_bv), axis=-1)
    x = _layernorm(x + _L1_ffn_ref(x, L1_ffn_gate_weight, L1_ffn_ln_gamma, L1_ffn_ln_beta, L1_ffn_wi, L1_ffn_wo, L1_ffn_conf_w1, L1_ffn_conf_b1, L1_ffn_conf_w2, L1_ffn_conf_b2, L1_ffn_comp_w, L1_ffn_comp_b), axis=-1)
    return x

_drawn_inputs = setup_inputs


def setup_inputs(seed=0):
    import zlib

    import numpy as np

    out = dict(_drawn_inputs(seed))
    spreads = {'L1_xattn_bq': (0.0, 0.366),
     'L1_xattn_bk': (0.0, 2.0),
     'L1_xattn_bv': (0.0, 0.1),
     'L1_ffn_ln_gamma': (1.0, 0.2),
     'L1_ffn_ln_beta': (0.0, 0.528),
     'L1_ffn_conf_b1': (-1.0, 0.2)}
    factors = {'L0_xattn_bo': 4.77,
     'L0_ffn_routing_weights': 8.0,
     'L0_ffn_gate_up_proj': 8.0,
     'L0_ffn_gate_up_proj_bias': 8.0,
     'L0_ffn_down_proj': 8.0,
     'L0_ffn_down_proj_bias': 64.0,
     'L1_attn_Wgt': 7.158}
    for name, (base, spread) in spreads.items():
        noise = np.random.default_rng([zlib.crc32(name.encode()), seed]).standard_normal(out[name].shape)
        drawn = base * np.exp(spread * noise) if base else spread * noise
        out[name] = jnp.asarray(drawn.astype(out[name].dtype))
    for name, factor in factors.items():
        out[name] = (out[name] * factor).astype(out[name].dtype)
    return out
```

```python
from contextlib import ExitStack
import concourse.bass as bass
from concourse import mybir

ALU = mybir.AluOpType
ACT = mybir.ActivationFunctionType
AX = mybir.AxisListType
F32 = mybir.dt.float32
BF16 = mybir.dt.bfloat16
I32 = mybir.dt.int32

P = 128
B, T, D = 32, 256, 256
NT = T // P
KD = D // P
LATENT = 64


def linear_attention(nc, res, ident, x_in, wthT, wphT, wgT):
    with ExitStack() as ctx:
        def sb(name, shape, dt=F32):
            return ctx.enter_context(nc.sbuf_tensor("A_" + name, shape, dt))

        def psum(name, shape):
            return ctx.enter_context(nc.psum_tensor("A_" + name, shape, F32))

        def sem(name):
            return ctx.enter_context(nc.semaphore("A_" + name))

        xn = sb("xn", [P, NT, D])
        xT = sb("xT", [P, KD, T])
        theta_w = sb("theta_w", [P, KD, LATENT])
        phi_w = sb("phi_w", [P, KD, LATENT])
        g_w = sb("g_w", [P, KD, D])
        gram = sb("gram", [P, KD, D])
        u = sb("u", [P, KD, LATENT])
        v = sb("v", [LATENT, D])
        thetaT = sb("thetaT", [LATENT, T])
        ps_xT = psum("ps_xT", [P, KD, T])
        ps_gram = psum("ps_gram", [P, KD, D])
        ps_u = psum("ps_u", [P, KD, LATENT])
        ps_v = psum("ps_v", [LATENT, D])
        ps_theta = psum("ps_theta", [LATENT, T])
        ps_out = psum("ps_out", [P, NT, D])
        names = "weights x_loaded xn xT_done xT gram_done gram u_done u v_done v theta_done theta out_done out".split()
        s = {n: sem(n) for n in names}

        block = ctx.enter_context(nc.Block())

        @block.sync
        def _(sp):
            sp.dma_start(theta_w[:], wthT.rearrange("(k p) l -> p k l", p=P)).then_inc(s["weights"], 16)
            sp.dma_start(phi_w[:], wphT.rearrange("(k p) l -> p k l", p=P)).then_inc(s["weights"], 16)
            sp.dma_start(g_w[:], wgT.rearrange("(k p) l -> p k l", p=P)).then_inc(s["weights"], 16)
            for c in range(B // 2):
                if c:
                    sp.wait_ge(s["x_loaded"], 16 * c)
                sp.dma_start(res[:, 2 * c:2 * c + 2], x_in[2 * c:2 * c + 2].rearrange("b (t p) d -> p b t d", p=P)).then_inc(s["x_loaded"], 16)

        @block.gpsimd
        def _(pool):
            def copy_x(b):
                pool.wait_ge(s["gram_done"], b)
                nc.gpsimd.tensor_copy(xn[:], res[:, b]).then_inc(s["xn"], 1)
            with pool.Fori(0, B // 2) as j:
                pool.wait_ge(s["x_loaded"], j * 16 + 16)
                copy_x(j * 2)
                copy_x(j * 2 + 1)

        @block.tensor
        def _(pe):
            pe.wait_ge(s["weights"], 48)

            def transpose_x(b):
                pe.wait_ge(s["xn"], b + 1)
                for k in range(KD):
                    for t in range(NT):
                        last = nc.tensor.transpose(ps_xT[:, k, t * P:(t + 1) * P], xn[:, t, k * P:(k + 1) * P], ident[:])
                last.then_inc(s["xT_done"], 1)

            def gram_mm(b):
                for k in range(KD):
                    for t in range(NT):
                        last = nc.tensor.matmul(ps_gram[:, k], xn[:, t, k * P:(k + 1) * P], xn[:, t], start=t == 0, stop=t == NT - 1)
                last.then_inc(s["gram_done"], 1)

            def theta_mm(b):
                pe.wait_ge(s["xT"], b + 1)
                pe.wait_ge(s["theta"], b)
                for k in range(KD):
                    last = nc.tensor.matmul(ps_theta[:], theta_w[:, k], xT[:, k], start=k == 0, stop=k == KD - 1)
                last.then_inc(s["theta_done"], 1)

            def u_mm(b):
                pe.wait_ge(s["gram"], b + 1)
                for m in range(KD):
                    for k in range(KD):
                        last = nc.tensor.matmul(ps_u[:, m], gram[:, k, m * P:(m + 1) * P], phi_w[:, k], start=k == 0, stop=k == KD - 1)
                last.then_inc(s["u_done"], 1)

            def v_mm(b):
                pe.wait_ge(s["u"], b + 1)
                for k in range(KD):
                    last = nc.tensor.matmul(ps_v[:], u[:, k], g_w[:, k], start=k == 0, stop=k == KD - 1)
                last.then_inc(s["v_done"], 1)

            def out_mm(b):
                pe.wait_ge(s["v"], b + 1)
                pe.wait_ge(s["theta"], b + 1)
                pe.wait_ge(s["out"], b)
                for t in range(NT):
                    last = nc.tensor.matmul(ps_out[:, t], thetaT[:, t * P:(t + 1) * P], v[:], start=True, stop=True)
                last.then_inc(s["out_done"], 1)

            transpose_x(0)
            gram_mm(0)
            theta_mm(0)
            with pe.Fori(0, B - 1) as b:
                transpose_x(b + 1)
                u_mm(b)
                gram_mm(b + 1)
                v_mm(b)
                out_mm(b)
                theta_mm(b + 1)
            u_mm(B - 1)
            v_mm(B - 1)
            out_mm(B - 1)

        @block.scalar
        def _(act):
            with act.Fori(0, B) as b:
                act.wait_ge(s["xT_done"], b + 1)
                nc.scalar.activation(xT[:], ps_xT[:], ACT.Copy).then_inc(s["xT"], 1)
                act.wait_ge(s["u_done"], b + 1)
                nc.scalar.activation(u[:], ps_u[:], ACT.Copy).then_inc(s["u"], 1)
                act.wait_ge(s["v_done"], b + 1)
                nc.scalar.activation(v[:], ps_v[:], ACT.Copy, scale=1.0 / 16).then_inc(s["v"], 1)
                act.wait_ge(s["theta_done"], b + 1)
                nc.scalar.activation(thetaT[:], ps_theta[:], ACT.Copy).then_inc(s["theta"], 1)

        @block.vector
        def _(dve):
            with dve.Fori(0, B) as b:
                dve.wait_ge(s["gram_done"], b + 1)
                nc.vector.tensor_copy(gram[:], ps_gram[:]).then_inc(s["gram"], 1)
                dve.wait_ge(s["out_done"], b + 1)
                nc.vector.tensor_tensor(res[:, b], res[:, b], ps_out[:], ALU.add).then_inc(s["out"], 1)




def cross_attention(nc, res, ident, half, eps, ctxT, wq_d, wk_d, wv_d, wo_d, bo_d):
    H, HD, S = 16, 64, ctxT.shape[2]
    INNER = H * HD
    MT = INNER // P
    HU = 8
    HB = 4
    UNITS = [(g, t) for g in range(H // HU) for t in range(NT)]
    U = len(UNITS)
    with ExitStack() as ctx:
        def sb(name, shape, dt=F32):
            return ctx.enter_context(nc.sbuf_tensor("B_" + name, shape, dt))

        def psum(name, shape):
            return ctx.enter_context(nc.psum_tensor("B_" + name, shape, F32))

        wq = sb("wq", [P, KD, INNER])
        wk = sb("wk", [P, INNER])
        wv = sb("wv", [P, INNER])
        wo = sb("wo", [P, MT, D])
        bo = sb("bo", [P, D])
        st = sb("st", [P, NT, 6])
        mv = sb("mv", [P, NT, 2])
        veps = sb("veps", [P, NT])
        rstd = sb("rstd", [P, NT])
        xn = sb("xn", [P, NT, D])
        xT = sb("xT", [P, KD, T])
        ctx_cur = sb("ctx_cur", [P, S])
        qT = sb("qT", [P, MT, T])
        kT = sb("kT", [P, MT, S])
        v = sb("v", [S, INNER])
        mx = sb("mx", [P, 2, HU])
        prob = sb("prob", [P, 2, HU * S])
        rsum = sb("rsum", [P, U, HU])
        rinv = sb("rinv", [P, U, HU])
        pT = sb("pT", [S, 2, HU, P])
        o = sb("o", [P, 2, HU * HD])
        oT = sb("oT", [P, MT, T])
        ps_s = [psum(f"ps_s{i}", [P, 2, 512]) for i in range(2)]
        ps_p = [psum(f"ps_p{i}", [P, 512]) for i in range(2)]
        ps_m = [psum(f"ps_m{i}", [P, 512]) for i in range(2)]

        def sem(name):
            return ctx.enter_context(nc.semaphore("B_" + name))

        w_loaded, stats, stats_seen, aggr, var_eps, rstd_ready, xn_ready, resid_ready, ctx_ready = map(
            sem, "w_loaded stats stats_seen aggr var_eps rstd_ready xn_ready resid_ready ctx_ready".split())
        s_done, pT_done, av_done, oT_done, q_done, k_done, v_done, xT_done, w_done = map(
            sem, "s_done pT_done av_done oT_done q_done k_done v_done xT_done w_done".split())
        exp_ready, pT_ready, oT_ready, q_ready, k_ready, v_ready, xT_ready = map(
            sem, "exp_ready pT_ready oT_ready q_ready k_ready v_ready xT_ready".split())
        max_ready, sub_ready, sum_ready, inv_ready, o_ready, res_ready = map(
            sem, "max_ready sub_ready sum_ready inv_ready o_ready res_ready".split())

        block = ctx.enter_context(nc.Block())

        @block.sync
        def _(sp):
            sp.dma_start(wq[:], wq_d.rearrange("(k p) n -> p k n", p=P)).then_inc(w_loaded, 16)
            sp.dma_start(wk[:], wk_d).then_inc(w_loaded, 16)
            sp.dma_start(wv[:], wv_d).then_inc(w_loaded, 16)
            sp.dma_start(wo[:], wo_d.rearrange("(k p) n -> p k n", p=P)).then_inc(w_loaded, 16)
            sp.dma_start(bo[:], bo_d.rearrange("(a n) -> a n", a=1).partition_broadcast(P)).then_inc(w_loaded, 16)

        @block.gpsimd
        def _(pool):
            def norm_scale(b):
                pool.wait_ge(aggr, b + 1)
                nc.gpsimd.tensor_tensor(veps[:], mv[:, :, 1], eps[:], ALU.add).then_inc(var_eps, 1)
                pool.wait_ge(var_eps, b + 1)
                nc.gpsimd.tensor_tensor(rstd[:], veps[:], half[:], ALU.pow).then_inc(rstd_ready, 1)

            def keep_residual(b):
                pool.wait_ge(xn_ready, b + 1)
                for t in range(NT):
                    last = nc.gpsimd.tensor_tensor(res[:, b, t], xn[:, t], bo[:], ALU.add)
                last.then_inc(resid_ready, 1)

            def stage_context(b):
                pool.wait_ge(v_done, b * 2)
                nc.gpsimd.tensor_copy(ctx_cur[:], ctxT[:, b]).then_inc(ctx_ready, 1)

            pool.wait_ge(w_loaded, 80)
            with pool.Fori(0, B) as b:
                norm_scale(b)
                stage_context(b)
                keep_residual(b)

        @block.tensor
        def _(pe):
            def scores(b, n):
                g, t = UNITS[n]
                for h in range(HU):
                    r = h % 2 * HD
                    m = g * HU // 2 + h // 2
                    last = nc.tensor.matmul(ps_s[n % 2][:, h % 2, h // 2 * S:(h // 2 + 1) * S],
                                            qT[r:r + HD, m, t * P:(t + 1) * P], kT[r:r + HD, m],
                                            start=True, stop=True)
                last.then_inc(s_done, 1)

            def transpose_probs(b, n):
                pe.wait_ge(exp_ready, b * U + n + 1)
                for h in range(HU):
                    if h % HB == 0 and n % 2:
                        pe.wait_ge(pT_ready, b * 2 * U + 2 * n + h // HB - 1)
                    last = nc.tensor.transpose(ps_p[h // HB][0:S, h % HB * P:(h % HB + 1) * P],
                                               prob[:, n % 2, h * S:(h + 1) * S], ident[:])
                    if h % HB == HB - 1:
                        last.then_inc(pT_done, 1)

            def values(b, n, bank):
                pe.wait_ge(pT_ready, b * 2 * U + 2 * n + 2)
                for h in range(HU):
                    head = UNITS[n][0] * HU + h
                    last = nc.tensor.matmul(ps_m[bank][:, h * HD:(h + 1) * HD], pT[:, n % 2, h % 2 * HB + h // 2],
                                            v[:, head * HD:(head + 1) * HD],
                                            start=True, stop=True)
                last.then_inc(av_done, 1)

            def transpose_out(b, n, bank):
                pe.wait_ge(o_ready, b * U + n + 1)
                for c in range(HU * HD // P):
                    last = nc.tensor.transpose(ps_m[bank][:, c * P:(c + 1) * P], o[:, n % 2, c * P:(c + 1) * P], ident[:])
                last.then_inc(oT_done, 1)

            def transpose_x(b, bank):
                pe.wait_ge(xn_ready, b + 1)
                for k in range(KD):
                    for t in range(NT):
                        last = nc.tensor.transpose(ps_m[bank][:, k * T + t * P:k * T + (t + 1) * P],
                                                   xn[:, t, k * P:(k + 1) * P], ident[:])
                last.then_inc(xT_done, 1)

            def project_q(b, c, bank):
                for m in range(2):
                    for k in range(KD):
                        last = nc.tensor.matmul(ps_m[bank][:, m * T:(m + 1) * T], wq[:, k, (2 * c + m) * P:(2 * c + m + 1) * P],
                                                xT[:, k], start=k == 0, stop=k == KD - 1)
                last.then_inc(q_done, 1)

            def project_k(b, c, bank):
                for m in range(HB):
                    last = nc.tensor.matmul(ps_m[bank][:, m * S:(m + 1) * S], wk[:, (HB * c + m) * P:(HB * c + m + 1) * P],
                                            ctx_cur[:], start=True, stop=True)
                last.then_inc(k_done, 1)

            def project_v(b, c, bank):
                nc.tensor.matmul(ps_m[bank][0:S], ctx_cur[:], wv[:, c * 512:(c + 1) * 512],
                                 start=True, stop=True).then_inc(v_done, 1)

            def project_out(b, t, bank):
                for m in range(MT):
                    last = nc.tensor.matmul(ps_m[bank][:, 0:D], oT[:, m, t * P:(t + 1) * P], wo[:, m],
                                            start=m == 0, stop=m == MT - 1)
                last.then_inc(w_done, 1)

            def body(b, more):
                nb = b + 1
                transpose_probs(b, 0)
                pe.wait_ge(sub_ready, b * U + 1)
                scores(b, 2)
                transpose_probs(b, 1)
                pe.wait_ge(sub_ready, b * U + 2)
                scores(b, 3)
                pe.wait_ge(res_ready, b * 2)
                if more:
                    pe.wait_ge(ctx_ready, nb + 1)
                    project_k(nb, 0, 0)
                    project_k(nb, 1, 1)
                    pe.wait_ge(k_ready, b * 2 + 3)
                values(b, 0, 0)
                if more:
                    pe.wait_ge(k_ready, b * 2 + 4)
                    transpose_x(nb, 1)
                pe.wait_ge(o_ready, b * U + 1)
                values(b, 1, 0)
                transpose_probs(b, 2)
                if more:
                    pe.wait_ge(xT_ready, b + 2)
                transpose_out(b, 0, 1)
                pe.wait_ge(o_ready, b * U + 2)
                if more:
                    project_q(nb, 0, 0)
                transpose_probs(b, 3)
                pe.wait_ge(oT_ready, b * U + 1)
                transpose_out(b, 1, 1)
                if more:
                    pe.wait_ge(q_ready, b * U + 5)
                    project_q(nb, 1, 0)
                pe.wait_ge(oT_ready, b * U + 2)
                values(b, 2, 1)
                if more:
                    pe.wait_ge(q_ready, b * U + 6)
                    project_q(nb, 2, 0)
                pe.wait_ge(o_ready, b * U + 3)
                values(b, 3, 1)
                if more:
                    pe.wait_ge(q_ready, b * U + 7)
                    project_q(nb, 3, 0)
                pe.wait_ge(o_ready, b * U + 4)
                transpose_out(b, 2, 1)
                if more:
                    pe.wait_ge(q_ready, b * U + 8)
                    project_v(nb, 0, 0)
                    pe.wait_ge(oT_ready, b * U + 3)
                    project_v(nb, 1, 1)
                    pe.wait_ge(sub_ready, b * U + 3)
                    scores(nb, 0)
                    pe.wait_ge(v_ready, b * 2 + 3)
                transpose_out(b, 3, 0)
                if more:
                    pe.wait_ge(v_ready, b * 2 + 4)
                pe.wait_ge(oT_ready, b * U + 3)
                project_out(b, 0, 1)
                if more:
                    pe.wait_ge(sub_ready, b * U + 4)
                    scores(nb, 1)
                pe.wait_ge(oT_ready, b * U + 4)
                project_out(b, 1, 0)

            pe.wait_ge(w_loaded, 80)
            pe.wait_ge(ctx_ready, 1)
            project_k(0, 0, 0)
            project_k(0, 1, 1)
            pe.wait_ge(k_ready, 2)
            transpose_x(0, 1)
            pe.wait_ge(xT_ready, 1)
            project_q(0, 0, 0)
            project_q(0, 1, 1)
            pe.wait_ge(q_ready, 2)
            project_q(0, 2, 0)
            project_q(0, 3, 1)
            pe.wait_ge(q_ready, 4)
            project_v(0, 0, 0)
            project_v(0, 1, 1)
            scores(0, 0)
            scores(0, 1)
            pe.wait_ge(v_ready, 2)
            with pe.Fori(0, B - 1) as b:
                body(b, True)
            body(B - 1, False)

        @block.scalar
        def _(act):
            def copy_pT(b, n):
                for i in range(2):
                    act.wait_ge(pT_done, b * 2 * U + 2 * n + i + 1)
                    nc.scalar.activation(pT[:, n % 2, i * HB:(i + 1) * HB], ps_p[i][0:S], ACT.Copy).then_inc(pT_ready, 1)

            def exponential(b, n):
                act.wait_ge(sub_ready, b * U + n + 1)
                nc.scalar.activation(prob[:, n % 2], prob[:, n % 2], ACT.Exp, scale=HD ** -0.5).then_inc(exp_ready, 1)

            def copy_k(b, c, bank):
                act.wait_ge(k_done, b * 2 + c + 1)
                nc.scalar.activation(kT[:, c * HB:(c + 1) * HB], ps_m[bank][:, 0:HB * S], ACT.Copy).then_inc(k_ready, 1)

            def copy_x(b, bank):
                act.wait_ge(xT_done, b + 1)
                nc.scalar.activation(xT[:], ps_m[bank][:], ACT.Copy).then_inc(xT_ready, 1)

            def copy_q(b, c, bank):
                act.wait_ge(q_done, b * 4 + c + 1)
                nc.scalar.activation(qT[:, 2 * c:2 * c + 2], ps_m[bank][:], ACT.Copy).then_inc(q_ready, 1)

            def copy_v(b, c, bank):
                act.wait_ge(v_done, b * 2 + c + 1)
                nc.scalar.activation(v[:, c * 512:(c + 1) * 512], ps_m[bank][0:S], ACT.Copy).then_inc(v_ready, 1)

            def copy_oT(b, n, bank):
                g, t = UNITS[n]
                act.wait_ge(oT_done, b * U + n + 1)
                nc.scalar.activation(oT[:, g * 4:(g + 1) * 4, t * P:(t + 1) * P],
                                     ps_m[bank][:].rearrange("p (c i) -> p c i", c=4), ACT.Copy).then_inc(oT_ready, 1)

            def body(b, more):
                nb = b + 1
                copy_pT(b, 0)
                copy_pT(b, 1)
                if more:
                    copy_k(nb, 0, 0)
                    copy_k(nb, 1, 1)
                exponential(b, 2)
                if more:
                    copy_x(nb, 1)
                exponential(b, 3)
                copy_pT(b, 2)
                copy_oT(b, 0, 1)
                if more:
                    copy_q(nb, 0, 0)
                copy_pT(b, 3)
                copy_oT(b, 1, 1)
                if more:
                    copy_q(nb, 1, 0)
                    copy_q(nb, 2, 0)
                    copy_q(nb, 3, 0)
                copy_oT(b, 2, 1)
                if more:
                    copy_v(nb, 0, 0)
                    copy_v(nb, 1, 1)
                    exponential(nb, 0)
                copy_oT(b, 3, 0)
                if more:
                    exponential(nb, 1)

            copy_k(0, 0, 0)
            copy_k(0, 1, 1)
            copy_x(0, 1)
            for c in range(4):
                copy_q(0, c, c % 2)
            copy_v(0, 0, 0)
            copy_v(0, 1, 1)
            exponential(0, 0)
            exponential(0, 1)
            with act.Fori(0, B - 1) as b:
                body(b, True)
            body(B - 1, False)

        @block.vector
        def _(dve):
            def norm_stats(b):
                for t in range(NT):
                    last = nc.vector.bn_stats(st[:, t], res[:, b, t])
                last.then_inc(stats, 1)
                dve.wait_ge(stats, b + 1)
                dve.sem_inc(stats_seen)
                for t in range(NT):
                    last = nc.vector.bn_aggr(mv[:, t], st[:, t])
                last.then_inc(aggr, 1)

            def norm_apply(b):
                dve.wait_ge(rstd_ready, b + 1)
                dve.wait_ge(xT_done, b)
                dve.wait_ge(resid_ready, b)
                for t in range(NT):
                    last = nc.vector.tensor_scalar(xn[:, t], res[:, b, t], mv[:, t, 0:1], rstd[:, t:t + 1],
                                                   ALU.subtract, ALU.mult)
                last.then_inc(xn_ready, 1)

            def shift(b, n):
                sc = ps_s[n % 2][:, :, 0:HB * S].rearrange("p a (h k) -> p a h k", k=S)
                m = mx[:, n % 2]
                dve.wait_ge(s_done, b * U + n + 1)
                nc.vector.tensor_reduce(m.rearrange("p (a h) -> p a h", a=2), sc, AX.X, ALU.max).then_inc(max_ready, 1)
                dve.wait_ge(max_ready, b * U + n + 1)
                nc.vector.tensor_tensor(prob[:, n % 2].rearrange("p (a h k) -> p a h k", a=2, k=S), sc,
                                        m.rearrange("p (a h) -> p a h", a=2).unsqueeze(3).to_broadcast([P, 2, HB, S]),
                                        ALU.subtract).then_inc(sub_ready, 1)

            def row_sums(b, n):
                dve.wait_ge(exp_ready, b * U + n + 1)
                nc.vector.tensor_reduce(rsum[:, n], prob[:, n % 2].rearrange("p (h k) -> p h k", k=S),
                                        AX.X, ALU.add).then_inc(sum_ready, 1)
                dve.wait_ge(sum_ready, b * U + n + 1)
                nc.vector.reciprocal(rinv[:, n], rsum[:, n]).then_inc(inv_ready, 1)

            def normalise(b, n, bank):
                dve.wait_ge(av_done, b * U + n + 1)
                dve.wait_ge(inv_ready, b * U + n + 1)
                nc.vector.tensor_tensor(o[:, n % 2].rearrange("p (j a d) -> p j a d", a=2, d=HD),
                                        ps_m[bank][:].rearrange("p (j a d) -> p j a d", a=2, d=HD),
                                        rinv[:, n].rearrange("p (a j) -> p j a", a=2).unsqueeze(3).to_broadcast([P, HB, 2, HD]),
                                        ALU.mult).then_inc(o_ready, 1)

            def add_out(b, t, bank):
                dve.wait_ge(w_done, b * 2 + t + 1)
                nc.vector.tensor_tensor(res[:, b, t], res[:, b, t], ps_m[bank][:, 0:D], ALU.add).then_inc(res_ready, 1)

            def body(b, more):
                nb = b + 1
                dve.wait_ge(pT_done, b * 2 * U + 2)
                shift(b, 2)
                if more:
                    norm_stats(nb)
                dve.wait_ge(pT_done, b * 2 * U + 4)
                shift(b, 3)
                if more:
                    norm_apply(nb)
                normalise(b, 0, 0)
                normalise(b, 1, 0)
                row_sums(b, 2)
                row_sums(b, 3)
                normalise(b, 2, 1)
                normalise(b, 3, 1)
                if more:
                    dve.wait_ge(pT_done, b * 2 * U + 6)
                    shift(nb, 0)
                dve.wait_ge(resid_ready, b + 1)
                add_out(b, 0, 1)
                if more:
                    dve.wait_ge(pT_done, b * 2 * U + 8)
                    shift(nb, 1)
                    row_sums(nb, 0)
                add_out(b, 1, 0)
                if more:
                    row_sums(nb, 1)

            norm_stats(0)
            norm_apply(0)
            shift(0, 0)
            shift(0, 1)
            row_sums(0, 0)
            row_sums(0, 1)
            with dve.Fori(0, B - 1) as b:
                body(b, True)
            body(B - 1, False)


def expert_ffn(nc, res, ident, half, eps, idx_d, rw_d, wgu_d, bgu_d, wdn_d, bdn_d):
    E, NTOK = wgu_d.shape[0], idx_d.shape[0]
    TI = NTOK // P
    NB = NTOK // T
    with ExitStack() as ctx:
        def sb(name, shape, dt=F32):
            return ctx.enter_context(nc.sbuf_tensor("C_" + name, shape, dt))

        def psum(name, shape):
            return ctx.enter_context(nc.psum_tensor("C_" + name, shape, F32))

        idx = sb("idx", [P, TI, 2], I32)
        idxf = sb("idxf", [P, TI, 2])
        rw = sb("rw", [P, TI, E])
        expert_no = sb("expert_no", [P, E])
        hit = sb("hit", [P, 2, TI, E])
        hits = sb("hits", [P, TI, E])
        coef = sb("coef", [P, TI, E])
        coefT = sb("coefT", [E, TI, P])
        bdn = sb("bdn", [E, D])
        bgu = sb("bgu", [P, E, 2 * KD])
        wgu = sb("wgu", [P, 2, KD, 2 * D])
        wdn = sb("wdn", [P, 2, KD, D])
        st = sb("st", [P, TI, 6])
        mv = sb("mv", [P, TI, 2])
        veps = sb("veps", [P, TI])
        rstd = sb("rstd", [P, TI])
        xn = sb("xn", [P, TI, D])
        xT = sb("xT", [P, KD, NTOK])
        gate = sb("gate", [P, KD, NTOK])
        up = sb("up", [P, KD, NTOK])
        eg = sb("eg", [P, KD, NTOK])
        inter = sb("inter", [P, KD, NTOK])
        ps_h = [psum(f"ps_h{i}", [P, NTOK]) for i in range(2 * KD)]
        ps_d = [psum(f"ps_d{i}", [P, 2, D]) for i in range(TI // 2)]

        def sem(name):
            return ctx.enter_context(nc.semaphore("C_" + name))

        in_loaded, w_loaded0, w_loaded1, step, stats, aggr, var_eps, rstd_ready, xn_ready = map(
            sem, "in_loaded w_loaded0 w_loaded1 step stats aggr var_eps rstd_ready xn_ready".split())
        xT_done, xT_ready, coef_ready, cT_done, cT_ready, bias_done, acc_init = map(
            sem, "xT_done xT_ready coef_ready cT_done cT_ready bias_done acc_init".split())
        h_done, h_read, eg_ready, inter_step, inter_ready, d_done, d_read = map(
            sem, "h_done h_read eg_ready inter_step inter_ready d_done d_read".split())
        w_loaded = [w_loaded0, w_loaded1]

        block = ctx.enter_context(nc.Block())

        @block.sync
        def _(sp):
            sp.dma_start(idx[:], idx_d.rearrange("(t p) k -> p t k", p=P)).then_inc(in_loaded, 16)
            sp.dma_start(rw[:], rw_d.rearrange("(t p) e -> p t e", p=P)).then_inc(in_loaded, 16)
            sp.dma_start(bdn[:], bdn_d).then_inc(in_loaded, 16)
            sp.dma_start(bgu[:], bgu_d).then_inc(in_loaded, 16)

            def load(e, u):
                sp.dma_start(wgu[:, u], wgu_d[e].rearrange("(k p) n -> p k n", p=P)).then_inc(w_loaded[u], 16)
                sp.dma_start(wdn[:, u], wdn_d[e].rearrange("(k p) n -> p k n", p=P)).then_inc(w_loaded[u], 16)
            load(0, 0)
            load(1, 1)
            with sp.Fori(0, E // 2 - 1) as j:
                for u in range(2):
                    sp.wait_ge(d_done, j * 2 * TI + (u + 1) * TI)
                    load(j * 2 + (2 + u), u)

        @block.gpsimd
        def _(pool):
            nc.gpsimd.iota(hits[:, 0].bitcast(I32), [[1, E]], base=0, channel_multiplier=0).then_inc(step, 1)
            pool.wait_ge(step, 1)
            nc.gpsimd.tensor_copy(expert_no[:], hits[:, 0].bitcast(I32)).then_inc(step, 1)
            pool.wait_ge(aggr, 1)
            nc.gpsimd.tensor_scalar(veps[:], mv[:, :, 1], 1e-5, None, ALU.add).then_inc(var_eps, 1)
            pool.wait_ge(var_eps, 1)
            for i in range(TI // NT):
                last = nc.gpsimd.tensor_tensor(rstd[:, i * NT:(i + 1) * NT], veps[:, i * NT:(i + 1) * NT], half[:], ALU.pow)
            last.then_inc(rstd_ready, 1)

        @block.tensor
        def _(pe):
            pe.wait_ge(xn_ready, 1)
            for k in range(KD):
                for t in range(TI):
                    last = nc.tensor.transpose(ps_h[k][:, t * P:(t + 1) * P], xn[:, t, k * P:(k + 1) * P], ident[:])
            last.then_inc(xT_done, 1)
            pe.wait_ge(coef_ready, 1)
            for t in range(TI):
                last = nc.tensor.transpose(ps_h[2][0:E, t * P:(t + 1) * P], coef[:, t], ident[:])
            last.then_inc(cT_done, 1)
            pe.wait_ge(cT_ready, 1)
            for t in range(TI):
                last = nc.tensor.matmul(ps_d[t // 2][:, t % 2], coefT[:, t], bdn[:], start=True, stop=True)
            last.then_inc(bias_done, 1)
            pe.wait_ge(xT_ready, 1)

            def hidden(e, u, first=False):
                for m in range(2 * KD):
                    if not first:
                        pe.wait_ge(h_read, e * 2 * KD + (m + 1 - 2 * KD))
                    for k in range(KD):
                        last = nc.tensor.matmul(ps_h[m][:], wgu[:, u, k, m * P:(m + 1) * P], xT[:, k], start=k == 0, stop=k == KD - 1)
                    last.then_inc(h_done, 1)

            def down(e, u, first=False):
                pe.wait_ge(inter_ready, e + 1)
                for t in range(TI):
                    if t % 2 == 0 and not first:
                        pe.wait_ge(d_read, e * TI + (t + 2 - TI))
                    for k in range(KD):
                        last = nc.tensor.matmul(ps_d[t // 2][:, t % 2], inter[:, k, t * P:(t + 1) * P], wdn[:, u, k],
                                                start=k == 0, stop=k == KD - 1)
                    last.then_inc(d_done, 1)

            pe.wait_ge(w_loaded[0], 32)
            hidden(0, 0, first=True)
            pe.wait_ge(acc_init, 1)
            pe.wait_ge(w_loaded[1], 32)
            hidden(1, 1)
            down(0, 0, first=True)
            with pe.Fori(0, E // 2 - 1) as j:
                pe.wait_ge(w_loaded[0], j * 32 + 64)
                hidden(j * 2 + 2, 0)
                down(j * 2 + 1, 1)
                pe.wait_ge(w_loaded[1], j * 32 + 64)
                hidden(j * 2 + 3, 1)
                down(j * 2 + 2, 0)
            down(E - 1, 1)

        @block.scalar
        def _(act):
            act.wait_ge(xT_done, 1)
            for k in range(KD):
                last = nc.scalar.activation(xT[:, k], ps_h[k][:], ACT.Copy)
            last.then_inc(xT_ready, 1)
            act.wait_ge(cT_done, 1)
            nc.scalar.activation(coefT[:], ps_h[2][0:E].rearrange("e (t p) -> e t p", p=P), ACT.Copy).then_inc(cT_ready, 1)
            with act.Fori(0, E) as e:
                act.wait_ge(h_read, e * 2 * KD + KD)
                nc.scalar.activation(eg[:], gate[:], ACT.Exp, scale=-1.702).then_inc(eg_ready, 1)

        @block.vector
        def _(dve):
            for t in range(TI):
                last = nc.vector.bn_stats(st[:, t], res[:, t // NT, t % NT])
            last.then_inc(stats, 1)
            dve.wait_ge(stats, 1)
            for t in range(TI):
                last = nc.vector.bn_aggr(mv[:, t], st[:, t])
            last.then_inc(aggr, 1)
            dve.wait_ge(rstd_ready, 1)
            for t in range(TI):
                last = nc.vector.tensor_scalar(xn[:, t], res[:, t // NT, t % NT], mv[:, t, 0:1], rstd[:, t:t + 1],
                                               ALU.subtract, ALU.mult)
            last.then_inc(xn_ready, 1)
            dve.wait_ge(in_loaded, 64)
            nc.vector.tensor_copy(idxf[:], idx[:]).then_inc(step, 1)
            dve.wait_ge(step, 3)
            for k in range(2):
                last = nc.vector.tensor_tensor(hit[:, k], idxf[:, :, k].unsqueeze(2).to_broadcast([P, TI, E]),
                                               expert_no[:].unsqueeze(1).to_broadcast([P, TI, E]), ALU.is_equal)
            last.then_inc(step, 1)
            dve.wait_ge(step, 4)
            nc.vector.tensor_tensor(hits[:], hit[:, 0], hit[:, 1], ALU.add).then_inc(step, 1)
            dve.wait_ge(step, 5)
            nc.vector.tensor_tensor(coef[:], hits[:], rw[:], ALU.mult).then_inc(coef_ready, 1)
            dve.wait_ge(bias_done, 1)
            dve.wait_ge(xn_ready, 1)
            for i in range(NB):
                last = nc.vector.tensor_tensor(res[:, i], xn[:, i * NT:(i + 1) * NT], ps_d[i][:], ALU.add)
            last.then_inc(acc_init, 1)
            dve.wait_ge(acc_init, 1)

            def swiglu(e):
                for m in range(2 * KD):
                    dve.wait_ge(h_done, e * 2 * KD + m + 1)
                    nc.vector.tensor_scalar((gate if m < KD else up)[:, m % KD], ps_h[m][:], bgu[:, e, m:m + 1], 7.0,
                                            ALU.add, ALU.min).then_inc(h_read, 1)
                dve.wait_ge(h_read, e * 2 * KD + 2 * KD)
                nc.vector.tensor_scalar(up[:], up[:], -7.0, 1.0, ALU.max, ALU.add).then_inc(inter_step, 1)
                dve.wait_ge(inter_step, e * 4 + 1)
                nc.vector.tensor_tensor(up[:], up[:], gate[:], ALU.mult).then_inc(inter_step, 1)
                dve.wait_ge(eg_ready, e + 1)
                nc.vector.tensor_scalar(eg[:], eg[:], 1.0, None, ALU.add).then_inc(inter_step, 1)
                dve.wait_ge(inter_step, e * 4 + 3)
                nc.vector.reciprocal(eg[:], eg[:]).then_inc(inter_step, 1)
                dve.wait_ge(inter_step, e * 4 + 4)
                dve.wait_ge(d_done, e * TI)
                nc.vector.tensor_tensor(inter[:], up[:], eg[:], ALU.mult).then_inc(inter_ready, 1)

            def accumulate(e):
                for t in range(TI):
                    r = res[:, t // NT, t % NT]
                    if t == 0:
                        dve.wait_ge(d_read, e * TI)
                    dve.wait_ge(d_done, e * TI + 2 * (t // 2) + 2)
                    nc.vector.scalar_tensor_tensor(r, ps_d[t // 2][:, t % 2], coef[:, t, bass.ds(e, 1)], r,
                                                   ALU.mult, ALU.add).then_inc(d_read, 1)

            swiglu(0)
            with dve.Fori(0, E - 1) as e:
                accumulate(e)
                swiglu(e + 1)
            accumulate(E - 1)


RET_H, RET_D = 16, 16
RET_U = 4


def retention_head(p):
    r, rg, half, e = p // 8, p // 4 % 2, p // 2 % 2, p % 2
    return half * 8 + (2 * r + rg) * 2 + e


def gated_retention(nc, res, ident, half, x_w, const):
    H, HD, U = RET_H, RET_D, RET_U
    HT = H // 2
    with ExitStack() as ctx:
        def sb(name, shape, dt=F32):
            return ctx.enter_context(nc.sbuf_tensor("D_" + name, shape, dt))

        def psum(name, shape):
            return ctx.enter_context(nc.psum_tensor("D_" + name, shape, F32))

        wqk = sb("wqk", [P, KD, 2 * D])
        wvg = sb("wvg", [P, KD, 2 * D])
        wgt = sb("wgt", [P, KD, H])
        wo = sb("wo", [P, KD, D])
        upto = sb("upto", [P, P])
        after = sb("after", [P, P])
        head_mask = sb("head_mask", [P, 2])
        block_mask = sb("block_mask", [P, P])
        sel = sb("sel", [P, H, P], BF16)
        nsel = sb("nsel", [P, H, P], BF16)
        st = sb("st", [P, NT, 6])
        mv = sb("mv", [P, NT, 2])
        veps = sb("veps", [P, NT])
        rstd = sb("rstd", [P, NT])
        xn = sb("xn", [P, NT, D])
        xT = sb("xT", [P, KD, T])
        qk = sb("qk", [P, NT, 2, D])
        v_raw = sb("v_raw", [P, NT, D])
        g_raw = sb("g_raw", [P, NT, D])
        v = sb("v", [P, NT, D])
        sq = sb("sq", [P, 3, NT, D])
        ssq = sb("ssq", [P, 3, NT])
        msq = sb("msq", [P, 3, NT])
        half6 = sb("half6", [P, 3, NT])
        half32 = sb("half32", [P, NT, H])
        rms = sb("rms", [P, 3, NT])
        za = sb("za", [P, NT, H])
        zm = sb("zm", [P, NT, H])
        ze = sb("ze", [P, NT, H])
        zl = sb("zl", [P, NT, H])
        ld = sb("ld", [P, NT, 4, 32])
        dec = sb("dec", [P, 2, H])
        F = sb("F", [P, NT, P], BF16)
        Fr = sb("Fr", [P, NT, P])
        q2T = sb("q2T", [P, NT, 2, 2, P])
        kT = sb("kT", [P, NT, 2, P])
        qd = sb("qd", [P, D])
        kd = sb("kd", [P, D])
        qdT = sb("qdT", [P, 2, P])
        state = sb("state", [P, 2, P])
        dexp = sb("dexp", [P, 2, HT * P])
        att = sb("att", [P, 2, HT, P])
        osq = sb("osq", [P, NT, H, HD])
        oss = sb("oss", [P, NT, H])
        oms = sb("oms", [P, NT, H])
        orms = sb("orms", [P, NT, H])
        eg = sb("eg", [P, NT, D])
        sg = sb("sg", [P, NT, D])
        y = sb("y", [P, NT, D])
        yT = sb("yT", [P, KD, T])
        ps_e = psum("ps_e", [P, 2, 512])
        ps_s = psum("ps_s", [P, 2, 512])
        ps_f = [psum(f"ps_f{i}", [P, 512]) for i in range(2)]
        ps_c = psum("ps_c", [P, 512])
        ps_o = psum("ps_o", [P, NT, D])
        c_bc, c_bcT, c_z = ps_c[:, 0:2 * H], ps_c[:, 64:64 + T], ps_c[:, 384:384 + NT * H]

        def sem(name):
            return ctx.enter_context(nc.semaphore("D_" + name))

        w_loaded, set_ready, stats, seen, aggr, var_eps, rstd_ready, xn_ready, resid_ready = map(
            sem, "w_loaded set_ready stats seen aggr var_eps rstd_ready xn_ready resid_ready".split())
        xT_done, qk_done, vg_done, z_done, bc_done, bcT_done, qkT_done, qdT_done = map(
            sem, "xT_done qk_done vg_done z_done bc_done bcT_done qkT_done qdT_done".split())
        e_done, s_done, st_done, av_done, yT_done, w_done = map(
            sem, "e_done s_done st_done av_done yT_done w_done".split())
        xT_ready, qk_raw, vg_raw, ssq_ready, ze_ready, zl_ready, dec_ready, qkT_ready, qdT_ready = map(
            sem, "xT_ready qk_raw vg_raw ssq_ready ze_ready zl_ready dec_ready qkT_ready qdT_ready".split())
        exp_ready, osq_ready, eg_ready, yT_ready = map(sem, "exp_ready osq_ready eg_ready yT_ready".split())
        z_step, z_ready, ld_ready, f_step, f_ready, qk_ready, v_ready, att_raw, state_ready, oss_ready = map(
            sem, "z_step z_ready ld_ready f_step f_ready qk_ready v_ready att_raw state_ready oss_ready".split())
        y_step, y_ready, sg_step, sg_ready, res_ready = map(sem, "y_step y_ready sg_step sg_ready res_ready".split())
        msq_ready, rms_ready, kqd_ready, att_ready, oms_ready, orms_ready = map(
            sem, "msq_ready rms_ready kqd_ready att_ready oms_ready orms_ready".split())

        block = ctx.enter_context(nc.Block())

        @block.sync
        def _(sp):
            for dst, name in ((wqk, "wqk"), (wvg, "wvg"), (wgt, "wgt"), (wo, "wo")):
                sp.dma_start(dst[:], x_w[name].rearrange("(k p) n -> p k n", p=P)).then_inc(w_loaded, 16)
            for dst, name in ((upto, "upto"), (after, "after"), (head_mask, "head_mask"), (block_mask, "block_mask"),
                              (sel, "sel"), (nsel, "nsel")):
                sp.dma_start(dst[:], const[name]).then_inc(w_loaded, 16)
        LOADED = 160

        @block.gpsimd
        def _(pool):
            def norm_scale(n):
                pool.wait_ge(aggr, n + 1)
                pool.sem_inc(seen)
                nc.gpsimd.tensor_scalar(veps[:], mv[:, :, 1], 1e-5, None, ALU.add).then_inc(var_eps, 1)
                pool.wait_ge(var_eps, n + 1)
                nc.gpsimd.tensor_tensor(rstd[:], veps[:], half[:], ALU.pow).then_inc(rstd_ready, 1)

            def keep_residual(b, n):
                pool.wait_ge(xn_ready, n + 1)
                nc.gpsimd.tensor_copy(res[:, b], xn[:]).then_inc(resid_ready, 1)

            def qkv_scale(b):
                pool.wait_ge(ssq_ready, b * 6 + 6)
                pool.sem_inc(seen)
                nc.gpsimd.tensor_scalar(msq[:], ssq[:], 1.0 / D, 1e-6, ALU.mult, ALU.add).then_inc(msq_ready, 1)
                pool.wait_ge(msq_ready, b + 1)
                nc.gpsimd.tensor_tensor(rms[:], msq[:], half6[:], ALU.pow).then_inc(rms_ready, 1)

            def decayed(b):
                pool.wait_ge(qk_ready, b + 1)
                pool.wait_ge(dec_ready, b + 1)
                for dst, c, w, n in ((qd, 1, 0, 0), (kd, 0, 1, 1)):
                    last = nc.gpsimd.tensor_tensor(dst[:].rearrange("p (h d) -> p h d", d=HD),
                                                   qk[:, c, w].rearrange("p (h d) -> p h d", d=HD),
                                                   dec[:, n].unsqueeze(2).to_broadcast([P, H, HD]), ALU.mult)
                last.then_inc(kqd_ready, 1)

            def causal(b, n):
                pool.wait_ge(att_raw, b * U + n + 1)
                pool.sem_inc(seen)
                nc.gpsimd.affine_select(out=att[:, n % 2], in_=att[:, n % 2], compare_op=ALU.is_ge, fill=0.0, base=0,
                                        pattern=[[0, HT], [1, P]], channel_multiplier=-1).then_inc(att_ready, 1)

            def out_scale(b):
                pool.wait_ge(oss_ready, b + 1)
                pool.sem_inc(seen)
                nc.gpsimd.tensor_scalar(oms[:], oss[:], 1.0 / HD, 1e-6, ALU.mult, ALU.add).then_inc(oms_ready, 1)
                pool.wait_ge(oms_ready, b + 1)
                nc.gpsimd.tensor_tensor(orms[:], oms[:], half32[:], ALU.pow).then_inc(orms_ready, 1)

            def body(b, first, more):
                nb = b + 1
                if not first:
                    out_scale(b - 1)
                if more:
                    if first:
                        norm_scale(1)
                        keep_residual(nb, 1)
                    else:
                        norm_scale(b * 2)
                        norm_scale(b * 2 + 1)
                causal(b, 0)
                if more and not first:
                    keep_residual(nb, b * 2 + 1)
                causal(b, 1)
                causal(b, 2)
                if more:
                    qkv_scale(nb)
                causal(b, 3)
                if more:
                    pool.wait_ge(st_done, b + 1)
                    decayed(nb)

            for i in range(3):
                nc.gpsimd.memset(half6[:, i], -0.5)
            nc.gpsimd.memset(half32[:], -0.5)
            nc.gpsimd.memset(ld[:], 0.0).then_inc(set_ready, 1)
            norm_scale(0)
            keep_residual(0, 0)
            qkv_scale(0)
            decayed(0)
            body(0, True, True)
            with pool.Fori(1, B - 1) as b:
                body(b, False, True)
            body(B - 1, False, False)
            out_scale(B - 1)

        @block.tensor
        def _(pe):
            def transpose_x(b, n):
                pe.wait_ge(xn_ready, n + 1)
                for k in range(KD):
                    for t in range(NT):
                        last = nc.tensor.transpose(ps_f[0][:, k * T + t * P:k * T + (t + 1) * P],
                                                   xn[:, t, k * P:(k + 1) * P], ident[:])
                last.then_inc(xT_done, 1)

            def project(b, t, w, bank, done):
                for k in range(KD):
                    last = nc.tensor.matmul(ps_f[bank][:], xT[:, k, t * P:(t + 1) * P], w[:, k], start=k == 0, stop=k == KD - 1)
                last.then_inc(done, 1)

            def gates(b):
                for t in range(NT):
                    for k in range(KD):
                        last = nc.tensor.matmul(c_z[:, t * H:(t + 1) * H], xT[:, k, t * P:(t + 1) * P], wgt[:, k],
                                                start=k == 0, stop=k == KD - 1)
                last.then_inc(z_done, 1)

            def running_sums(b):
                pe.wait_ge(ld_ready, b + 1)
                nc.tensor.matmul(c_bc[:, 0:H], upto[:], ld[:, 1, 0, 0:H], start=True, stop=True)
                nc.tensor.matmul(c_bc[:, H:2 * H], after[:], ld[:, 0, 0, 0:H], start=True, stop=True).then_inc(bc_done, 1)
                for c in range(NT):
                    last = nc.tensor.matmul(c_bcT[:, c * P:(c + 1) * P], ld[:, c].rearrange("p s h -> p (s h)"), upto[:],
                                            start=True, stop=True)
                last.then_inc(bcT_done, 1)

            def transpose_qk(b, c, bank):
                pe.wait_ge(qk_ready, b + 1)
                for w in range(2):
                    for hf in range(2):
                        last = nc.tensor.transpose(ps_f[bank][:, (w * 2 + hf) * P:(w * 2 + hf + 1) * P],
                                                   qk[:, c, w, hf * P:(hf + 1) * P], ident[:])
                last.then_inc(qkT_done, 1)

            def transpose_qd(b):
                pe.wait_ge(kqd_ready, b + 1)
                for hf in range(2):
                    last = nc.tensor.transpose(ps_f[1][:, hf * P:(hf + 1) * P], qd[:, hf * P:(hf + 1) * P], ident[:])
                last.then_inc(qdT_done, 1)

            def exponents(b, n):
                c, r = n // 2, n % 2
                for bank in range(2):
                    pl = r * HT + bank * 4
                    nc.tensor.matmul(ps_e[:, bank], F[:, c], nsel[:, pl:pl + 4], start=True, stop=False)
                    for i in range(4):
                        last = nc.tensor.matmul(ps_e[:, bank, i * P:(i + 1) * P], sel[:, pl + i], F[:, c], start=False, stop=i == 3)
                last.then_inc(e_done, 1)

            def products(b, n):
                c, r = n // 2, n % 2
                for bank in range(2):
                    rows = slice(32 * (2 * r + bank), 32 * (2 * r + bank) + 32)
                    for hf in range(2):
                        last = nc.tensor.matmul(ps_s[:, bank, hf * T:(hf + 1) * T], kT[rows, c, hf],
                                                q2T[rows, c, hf].rearrange("p e i -> p (e i)"), start=True, stop=True)
                last.then_inc(s_done, 1)

            def values(b, n):
                c, r = n // 2, n % 2
                pe.wait_ge(att_ready, b * U + n + 1)
                for i in range(HT):
                    h = retention_head(r * HT + i)
                    last = nc.tensor.matmul(ps_o[:, c, h * HD:(h + 1) * HD], att[:, n % 2, i], v[:, c, h * HD:(h + 1) * HD],
                                            start=n == 0 and i == 0, stop=n == U - 1 and i == HT - 1, skip_group_check=True)
                last.then_inc(av_done, 1)

            def state_update(b):
                for hf in range(2):
                    last = nc.tensor.matmul(ps_f[0][:, hf * P:(hf + 1) * P], kd[:, hf * P:(hf + 1) * P], v[:, 0, hf * P:(hf + 1) * P],
                                            start=True, stop=True)
                last.then_inc(st_done, 1)

            def cross(b):
                pe.wait_ge(state_ready, b + 1)
                for hf in range(2):
                    nc.tensor.matmul(ps_o[:, 1, hf * P:(hf + 1) * P], qdT[:, hf], state[:, hf], start=False, stop=False,
                                     skip_group_check=True)

            def transpose_y(b):
                pe.wait_ge(y_ready, b + 1)
                for k in range(KD):
                    for t in range(NT):
                        last = nc.tensor.transpose(ps_f[1][:, k * T + t * P:k * T + (t + 1) * P],
                                                   y[:, t, k * P:(k + 1) * P], ident[:])
                last.then_inc(yT_done, 1)

            def project_out(b):
                pe.wait_ge(yT_ready, b + 1)
                for t in range(NT):
                    for k in range(KD):
                        last = nc.tensor.matmul(ps_f[1][:, t * D:(t + 1) * D], yT[:, k, t * P:(t + 1) * P], wo[:, k],
                                                start=k == 0, stop=k == KD - 1)
                last.then_inc(w_done, 1)

            def body(b, first, more):
                nb = b + 1
                pe.wait_ge(f_ready, b + 1)
                exponents(b, 0)
                pe.wait_ge(qkT_ready, b * 2 + 2)
                products(b, 0)
                pe.wait_ge(exp_ready, b * U + 1)
                exponents(b, 1)
                pe.wait_ge(qdT_ready, b + 1)
                if not first:
                    transpose_y(b - 1)
                pe.wait_ge(att_raw, b * U + 1)
                products(b, 1)
                if more:
                    transpose_x(nb, 1 if first else b * 2 + 1)
                if not first:
                    project_out(b - 1)
                if more:
                    pe.wait_ge(xT_ready, nb + 1)
                    project(nb, 0, wqk, 0, qk_done)
                pe.wait_ge(v_ready, b + 1)
                values(b, 0)
                if not first:
                    pe.wait_ge(res_ready, b)
                if more:
                    project(nb, 1, wqk, 1, qk_done)
                pe.wait_ge(exp_ready, b * U + 2)
                exponents(b, 2)
                pe.wait_ge(att_raw, b * U + 2)
                products(b, 2)
                if more:
                    pe.wait_ge(qk_raw, b * 2 + 3)
                    project(nb, 0, wvg, 0, vg_done)
                values(b, 1)
                if more:
                    pe.wait_ge(qk_raw, b * 2 + 4)
                    project(nb, 1, wvg, 1, vg_done)
                    pe.wait_ge(dec_ready, b + 1)
                    gates(nb)
                pe.wait_ge(exp_ready, b * U + 3)
                exponents(b, 3)
                pe.wait_ge(att_raw, b * U + 3)
                products(b, 3)
                if more:
                    pe.wait_ge(vg_raw, b * 2 + 3)
                pe.wait_ge(kqd_ready, b + 1)
                state_update(b)
                values(b, 2)
                if more:
                    running_sums(nb)
                cross(b)
                if more:
                    pe.wait_ge(vg_raw, b * 2 + 4)
                    transpose_qk(nb, 0, 1)
                values(b, 3)
                if more:
                    transpose_qk(nb, 1, 0)
                    pe.wait_ge(qkT_ready, b * 2 + 3)
                    transpose_qd(nb)

            pe.wait_ge(w_loaded, LOADED)
            pe.wait_ge(set_ready, 1)
            transpose_x(0, 0)
            pe.wait_ge(xT_ready, 1)
            project(0, 0, wqk, 0, qk_done)
            project(0, 1, wqk, 1, qk_done)
            pe.wait_ge(qk_raw, 1)
            project(0, 0, wvg, 0, vg_done)
            pe.wait_ge(qk_raw, 2)
            project(0, 1, wvg, 1, vg_done)
            gates(0)
            running_sums(0)
            pe.wait_ge(vg_raw, 2)
            transpose_qk(0, 0, 1)
            transpose_qk(0, 1, 0)
            pe.wait_ge(qkT_ready, 1)
            transpose_qd(0)
            body(0, True, True)
            with pe.Fori(1, B - 1) as b:
                body(b, False, True)
            body(B - 1, False, False)
            transpose_y(B - 1)
            project_out(B - 1)

        @block.scalar
        def _(act):
            def exponential(b, n):
                act.wait_ge(e_done, b * U + n + 1)
                nc.scalar.activation(dexp[:, n % 2], ps_e[:].rearrange("p a n -> p (a n)"), ACT.Exp).then_inc(exp_ready, 1)

            def copy_x(b):
                act.wait_ge(xT_done, b + 1)
                nc.scalar.activation(xT[:].rearrange("p k t -> p (k t)"), ps_f[0][:], ACT.Copy).then_inc(xT_ready, 1)

            def copy_qk(b, t):
                act.wait_ge(qk_done, b * 2 + t + 1)
                nc.scalar.activation(qk[:, t].rearrange("p w d -> p (w d)"), ps_f[t][:], ACT.Copy).then_inc(qk_raw, 1)

            def squares_qk(b, t):
                act.wait_ge(qk_raw, b * 2 + t + 1)
                for w in range(2):
                    nc.scalar.activation(sq[:, w, t], qk[:, t, w], ACT.Square, accum_out=ssq[:, w, t:t + 1]).then_inc(ssq_ready, 1)

            def copy_vg(b, t):
                act.wait_ge(vg_done, b * 2 + t + 1)
                nc.scalar.activation(v_raw[:, t], ps_f[t][:, 0:D], ACT.Copy)
                nc.scalar.activation(g_raw[:, t], ps_f[t][:, D:2 * D], ACT.Copy).then_inc(vg_raw, 1)

            def squares_v(b, t):
                act.wait_ge(vg_raw, b * 2 + t + 1)
                nc.scalar.activation(sq[:, 2, t], v_raw[:, t], ACT.Square, accum_out=ssq[:, 2, t:t + 1]).then_inc(ssq_ready, 1)

            def softplus(b):
                act.wait_ge(z_ready, b + 1)
                nc.scalar.activation(ze[:], za[:], ACT.Exp, scale=-1.0).then_inc(ze_ready, 1)
                act.wait_ge(ze_ready, b + 1)
                nc.scalar.activation(zl[:], ze[:], ACT.Ln, bias=1.0).then_inc(zl_ready, 1)

            def border_decay(b):
                act.wait_ge(bcT_done, b + 1)
                nc.scalar.activation(dec[:].rearrange("p n h -> p (n h)"), c_bc, ACT.Exp).then_inc(dec_ready, 1)

            def copy_qkT(b, c, bank):
                act.wait_ge(qkT_done, b * 2 + c + 1)
                ps = ps_f[bank][:].rearrange("p (w f i) -> p w f i", w=2, f=2)
                for e in range(2):
                    nc.scalar.activation(q2T[:, c, :, e], ps[:, 0], ACT.Copy, scale=head_mask[:, e:e + 1])
                nc.scalar.activation(kT[:, c], ps[:, 1], ACT.Copy).then_inc(qkT_ready, 1)

            def copy_qdT(b):
                act.wait_ge(qdT_done, b + 1)
                nc.scalar.activation(qdT[:].rearrange("p f i -> p (f i)"), ps_f[1][:, 0:2 * P], ACT.Copy).then_inc(qdT_ready, 1)

            def out_squares(b):
                act.wait_ge(av_done, b * U + U)
                nc.scalar.activation(osq[:].rearrange("p t h d -> p (t h d)"), ps_o[:].rearrange("p t d -> p (t d)"),
                                     ACT.Square).then_inc(osq_ready, 1)

            def gate_exp(b):
                nc.scalar.activation(eg[:], g_raw[:], ACT.Exp, scale=-1.0).then_inc(eg_ready, 1)

            def copy_y(b):
                act.wait_ge(yT_done, b + 1)
                nc.scalar.activation(yT[:].rearrange("p k t -> p (k t)"), ps_f[1][:], ACT.Copy).then_inc(yT_ready, 1)

            def body(b, first, more):
                nb = b + 1
                if not first:
                    out_squares(b - 1)
                act.wait_ge(vg_raw, b * 2 + 2)
                gate_exp(b)
                exponential(b, 0)
                exponential(b, 1)
                if not first:
                    copy_y(b - 1)
                if more:
                    copy_x(nb)
                    act.wait_ge(kqd_ready, b + 1)
                    copy_qk(nb, 0)
                    squares_qk(nb, 0)
                    copy_qk(nb, 1)
                act.wait_ge(att_raw, b * U + 1)
                exponential(b, 2)
                if more:
                    squares_qk(nb, 1)
                    act.wait_ge(sg_ready, b + 1)
                    copy_vg(nb, 0)
                    squares_v(nb, 0)
                    copy_vg(nb, 1)
                act.wait_ge(att_raw, b * U + 2)
                exponential(b, 3)
                if more:
                    squares_v(nb, 1)
                    softplus(nb)
                    border_decay(nb)
                    copy_qkT(nb, 0, 1)
                    copy_qkT(nb, 1, 0)
                    copy_qdT(nb)

            act.wait_ge(w_loaded, LOADED)
            copy_x(0)
            for t in range(NT):
                copy_qk(0, t)
                squares_qk(0, t)
            for t in range(NT):
                copy_vg(0, t)
                squares_v(0, t)
            softplus(0)
            border_decay(0)
            copy_qkT(0, 0, 1)
            copy_qkT(0, 1, 0)
            copy_qdT(0)
            body(0, True, True)
            with act.Fori(1, B - 1) as b:
                body(b, False, True)
            body(B - 1, False, False)
            out_squares(B - 1)
            copy_y(B - 1)

        @block.vector
        def _(dve):
            def norm_stats(src, n):
                for t in range(NT):
                    last = nc.vector.bn_stats(st[:, t], src[t])
                last.then_inc(stats, 1)
                dve.wait_ge(stats, n + 1)
                dve.sem_inc(seen)
                for t in range(NT):
                    last = nc.vector.bn_aggr(mv[:, t], st[:, t])
                last.then_inc(aggr, 1)

            def norm_apply(src, n):
                dve.wait_ge(rstd_ready, n + 1)
                for t in range(NT):
                    last = nc.vector.tensor_scalar(xn[:, t], src[t], mv[:, t, 0:1], rstd[:, t:t + 1], ALU.subtract, ALU.mult)
                last.then_inc(xn_ready, 1)

            def scale_qk(b):
                dve.wait_ge(rms_ready, b + 1)
                for t in range(NT):
                    for w in range(2):
                        last = nc.vector.tensor_scalar(qk[:, t, w], qk[:, t, w], rms[:, w, t:t + 1], None, ALU.mult)
                last.then_inc(qk_ready, 1)

            def scale_v(b):
                for t in range(NT):
                    last = nc.vector.tensor_scalar(v[:, t], v_raw[:, t], rms[:, 2, t:t + 1], None, ALU.mult)
                last.then_inc(v_ready, 1)

            def gate_parts(b):
                dve.wait_ge(z_done, b + 1)
                nc.vector.tensor_scalar(zm[:].rearrange("p t h -> p (t h)"), c_z, 0.0, None, ALU.min).then_inc(z_step, 1)
                dve.wait_ge(z_step, b + 1)
                nc.vector.scalar_tensor_tensor(za[:].rearrange("p t h -> p (t h)"), c_z, 0.0, zm[:].rearrange("p t h -> p (t h)"),
                                               ALU.max, ALU.subtract).then_inc(z_ready, 1)

            def log_decay(b):
                dve.wait_ge(zl_ready, b + 1)
                dve.wait_ge(z_ready, b + 1)
                for s in (0, 2, 3):
                    last = nc.vector.tensor_tensor(ld[:, :, s, 0:H], zm[:], zl[:], ALU.subtract)
                last.then_inc(ld_ready, 1)

            def split_sums(b):
                f, fr = F[:].rearrange("p c i -> p (c i)"), Fr[:].rearrange("p c i -> p (c i)")
                dve.wait_ge(dec_ready, b + 1)
                dve.wait_ge(bcT_done, b + 1)
                nc.vector.tensor_copy(f, c_bcT).then_inc(f_step, 1)
                dve.wait_ge(f_step, b * 3 + 1)
                nc.vector.tensor_tensor(fr[64:P], c_bcT[64:P], f[64:P], ALU.subtract).then_inc(f_step, 1)
                dve.wait_ge(f_step, b * 3 + 2)
                nc.vector.tensor_copy(f[64:P], fr[64:P]).then_inc(f_step, 1)
                dve.wait_ge(f_step, b * 3 + 3)
                nc.vector.tensor_tensor(f[96:P], fr[96:P], f[96:P], ALU.subtract).then_inc(f_ready, 1)

            def attend(b, n):
                dve.wait_ge(exp_ready, b * U + n + 1)
                dve.wait_ge(s_done, b * U + n + 1)
                nc.vector.tensor_tensor(att[:, n % 2].rearrange("p h i -> p (h i)"), ps_s[:].rearrange("p a n -> p (a n)"),
                                        dexp[:, n % 2], ALU.mult).then_inc(att_raw, 1)

            def copy_state(b):
                dve.wait_ge(st_done, b + 1)
                nc.vector.tensor_tensor(state[:], ps_f[0][:, 0:2 * P].rearrange("p (f n) -> p f n", f=2),
                                        block_mask[:].unsqueeze(1).to_broadcast([P, 2, P]), ALU.mult).then_inc(state_ready, 1)

            def out_sums(b):
                dve.wait_ge(osq_ready, b + 1)
                nc.vector.tensor_reduce(oss[:], osq[:], AX.X, ALU.add).then_inc(oss_ready, 1)

            def gated_out(b):
                dve.wait_ge(orms_ready, b + 1)
                nc.vector.tensor_tensor(y[:].rearrange("p t (h d) -> p (t h) d", d=HD),
                                        ps_o[:].rearrange("p t (h d) -> p (t h) d", d=HD),
                                        orms[:].rearrange("p t h -> p (t h)").unsqueeze(2).to_broadcast([P, NT * H, HD]),
                                        ALU.mult).then_inc(y_step, 1)
                dve.wait_ge(y_step, b + 1)
                nc.vector.tensor_tensor(y[:], y[:], sg[:], ALU.mult).then_inc(y_ready, 1)

            def silu(b):
                dve.wait_ge(eg_ready, b + 1)
                nc.vector.tensor_scalar(eg[:], eg[:], 1.0, None, ALU.add).then_inc(sg_step, 1)
                dve.wait_ge(sg_step, b * 2 + 1)
                nc.vector.reciprocal(eg[:], eg[:]).then_inc(sg_step, 1)
                dve.wait_ge(sg_step, b * 2 + 2)
                nc.vector.tensor_tensor(sg[:], g_raw[:], eg[:], ALU.mult).then_inc(sg_ready, 1)

            def add_out(b):
                dve.wait_ge(resid_ready, b + 1)
                dve.wait_ge(w_done, b + 1)
                nc.vector.tensor_tensor(res[:, b], res[:, b], ps_f[1][:].rearrange("p (t d) -> p t d", t=NT), ALU.add)\
                    .then_inc(res_ready, 1)

            def body(b, first, more):
                nb = b + 1
                if not first:
                    out_sums(b - 1)
                if more:
                    src = [res[:, nb, t] for t in range(NT)]
                    kept = [xn[:, t] for t in range(NT)]
                    n = 1 if first else b * 2
                    norm_stats(src, n)
                    dve.wait_ge(xT_done, b + 1)
                    dve.wait_ge(resid_ready, b + 1)
                    norm_apply(src, n)
                    if not first:
                        dve.wait_ge(xn_ready, b * 2 + 1)
                        norm_stats(kept, b * 2 + 1)
                        norm_apply(kept, b * 2 + 1)
                if not first:
                    gated_out(b - 1)
                attend(b, 0)
                silu(b)
                attend(b, 1)
                if not first:
                    add_out(b - 1)
                dve.wait_ge(av_done, b * U + 1)
                attend(b, 2)
                if more:
                    gate_parts(nb)
                dve.wait_ge(av_done, b * U + 2)
                attend(b, 3)
                copy_state(b)
                if more:
                    scale_qk(nb)
                    log_decay(nb)
                    split_sums(nb)
                    dve.wait_ge(av_done, b * U + 4)
                    scale_v(nb)

            first_src = [res[:, 0, t] for t in range(NT)]
            norm_stats(first_src, 0)
            norm_apply(first_src, 0)
            scale_qk(0)
            scale_v(0)
            dve.wait_ge(set_ready, 1)
            gate_parts(0)
            log_decay(0)
            split_sums(0)
            dve.wait_ge(w_loaded, LOADED)
            body(0, True, True)
            with dve.Fori(1, B - 1) as b:
                body(b, False, True)
            body(B - 1, False, False)
            out_sums(B - 1)
            gated_out(B - 1)
            add_out(B - 1)


def cross_attention_single(nc, res, ident, half, ctxT, wqT_d, bq_d, wk_d, bk_d, wv_d, bv_d):
    S = ctxT.shape[2]
    with ExitStack() as ctx:
        def sb(name, shape, dt=F32):
            return ctx.enter_context(nc.sbuf_tensor("E_" + name, shape, dt))

        def psum(name, shape):
            return ctx.enter_context(nc.psum_tensor("E_" + name, shape, F32))

        def sem(name):
            return ctx.enter_context(nc.semaphore("E_" + name))

        wqT = sb("wqT", [P, KD, D])
        wk = sb("wk", [P, D])
        wv = sb("wv", [P, D])
        bq = sb("bq", [P, KD])
        bk = sb("bk", [P, KD])
        bv = sb("bv", [S, D])
        bq_rows = sb("bq_rows", [P, KD, P])
        st = sb("st", [P, NT, 6])
        mv = sb("mv", [P, NT, 2])
        veps = sb("veps", [P, NT])
        rstd = sb("rstd", [P, NT])
        xn = sb("xn", [P, NT, D])
        xT = sb("xT", [P, KD, T])
        ctx_cur = sb("ctx_cur", [P, S])
        kT = sb("kT", [P, KD, S])
        kq = sb("kq", [P, KD, S])
        v = sb("v", [S, D])
        nmx = sb("nmx", [P, NT])
        prob = sb("prob", [P, NT, S])
        rsum = sb("rsum", [P, NT])
        rinv = sb("rinv", [P, NT])
        pT = sb("pT", [S, NT, P])
        ps_x = psum("ps_x", [P, KD, T])
        ps_k = psum("ps_k", [P, 512])
        ps_kq = psum("ps_kq", [P, 512])
        ps_v = psum("ps_v", [P, 512])
        ps_s = psum("ps_s", [P, 512])
        ps_p = psum("ps_p", [P, 512])
        ps_o = psum("ps_o", [P, NT, D])
        k_out, kq_out, s_out = (x[:, 0:2 * S].rearrange("p (k s) -> p k s", k=2) for x in (ps_k, ps_kq, ps_s))

        w_loaded, bias_ready, stats, seen, aggr, var_eps, rstd_ready, xn_ready, resid_ready, ctx_ready = map(
            sem, "w_loaded bias_ready stats seen aggr var_eps rstd_ready xn_ready resid_ready ctx_ready".split())
        xT_done, k_done, kq_done, v_done, s_done, pT_done, o_done = map(
            sem, "xT_done k_done kq_done v_done s_done pT_done o_done".split())
        xT_ready, k_ready, kq_ready, v_ready, max_ready, exp_ready, pT_ready, inv_ready, res_ready = map(
            sem, "xT_ready k_ready kq_ready v_ready max_ready exp_ready pT_ready inv_ready res_ready".split())

        block = ctx.enter_context(nc.Block())

        @block.sync
        def _(sp):
            with nc.allow_non_contiguous_dma("biases, one element a partition"):
                sp.dma_start(bq[:], bq_d.rearrange("(k p) -> p k", p=P)).then_inc(w_loaded, 16)
                sp.dma_start(bk[:], bk_d.rearrange("(k p) -> p k", p=P)).then_inc(w_loaded, 16)
            sp.dma_start(wqT[:], wqT_d.rearrange("(k p) n -> p k n", p=P)).then_inc(w_loaded, 16)
            sp.dma_start(wk[:], wk_d).then_inc(w_loaded, 16)
            sp.dma_start(wv[:], wv_d).then_inc(w_loaded, 16)
            sp.dma_start(bv[:], bv_d.rearrange("(a n) -> a n", a=1).partition_broadcast(S)).then_inc(w_loaded, 16)
        LOADED = 96

        @block.gpsimd
        def _(pool):
            with pool.Fori(0, B) as b:
                pool.wait_ge(aggr, b + 1)
                pool.sem_inc(seen)
                nc.gpsimd.tensor_scalar(veps[:], mv[:, :, 1], 1e-5, None, ALU.add).then_inc(var_eps, 1)
                pool.wait_ge(var_eps, b + 1)
                nc.gpsimd.tensor_tensor(rstd[:], veps[:], half[:], ALU.pow).then_inc(rstd_ready, 1)
                pool.wait_ge(v_done, b)
                nc.gpsimd.tensor_copy(ctx_cur[:], ctxT[:, b]).then_inc(ctx_ready, 1)
                pool.wait_ge(xn_ready, b + 1)
                nc.gpsimd.tensor_copy(res[:, b], xn[:]).then_inc(resid_ready, 1)

        @block.tensor
        def _(pe):
            def transpose_x(b):
                pe.wait_ge(xn_ready, b + 1)
                for k in range(KD):
                    for t in range(NT):
                        last = nc.tensor.transpose(ps_x[:, k, t * P:(t + 1) * P], xn[:, t, k * P:(k + 1) * P], ident[:])
                last.then_inc(xT_done, 1)

            def project_k(b):
                pe.wait_ge(ctx_ready, b + 1)
                for m in range(KD):
                    last = nc.tensor.matmul(k_out[:, m], wk[:, m * P:(m + 1) * P], ctx_cur[:], start=True, stop=True)
                last.then_inc(k_done, 1)

            def fold_q(b):
                pe.wait_ge(k_ready, b + 1)
                for m in range(KD):
                    for k in range(KD):
                        last = nc.tensor.matmul(kq_out[:, m], wqT[:, k, m * P:(m + 1) * P], kT[:, k], start=k == 0, stop=k == KD - 1)
                last.then_inc(kq_done, 1)

            def project_v(b):
                nc.tensor.matmul(ps_v[0:S, 0:D], ctx_cur[:], wv[:], start=True, stop=True).then_inc(v_done, 1)

            def scores(b):
                pe.wait_ge(xT_ready, b + 1)
                pe.wait_ge(kq_ready, b + 1)
                for t in range(NT):
                    for k in range(KD):
                        nc.tensor.matmul(s_out[:, t], xT[:, k, t * P:(t + 1) * P], kq[:, k], start=k == 0, stop=False)
                    for k in range(KD):
                        last = nc.tensor.matmul(s_out[:, t], bq_rows[:, k], kT[:, k], start=False, stop=k == KD - 1)
                last.then_inc(s_done, 1)

            def transpose_probs(b):
                pe.wait_ge(exp_ready, b * NT + NT)
                for t in range(NT):
                    last = nc.tensor.transpose(ps_p[0:S, t * P:(t + 1) * P], prob[:, t], ident[:])
                last.then_inc(pT_done, 1)

            def values(b):
                pe.wait_ge(pT_ready, b + 1)
                pe.wait_ge(v_ready, b + 1)
                pe.wait_ge(res_ready, b * NT)
                for t in range(NT):
                    last = nc.tensor.matmul(ps_o[:, t], pT[:, t], v[:], start=True, stop=True)
                last.then_inc(o_done, 1)

            pe.wait_ge(w_loaded, LOADED)
            pe.wait_ge(bias_ready, 1)
            transpose_x(0)
            project_k(0)
            fold_q(0)
            project_v(0)
            with pe.Fori(0, B - 1) as b:
                scores(b)
                transpose_x(b + 1)
                project_k(b + 1)
                transpose_probs(b)
                fold_q(b + 1)
                values(b)
                project_v(b + 1)
            scores(B - 1)
            transpose_probs(B - 1)
            values(B - 1)

        @block.scalar
        def _(act):
            def copy_x(b):
                act.wait_ge(xT_done, b + 1)
                nc.scalar.activation(xT[:], ps_x[:], ACT.Copy).then_inc(xT_ready, 1)

            def copy_k(b):
                act.wait_ge(k_done, b + 1)
                for m in range(KD):
                    last = nc.scalar.activation(kT[:, m], k_out[:, m], ACT.Identity, bias=bk[:, m:m + 1])
                last.then_inc(k_ready, 1)

            def copy_kq(b):
                act.wait_ge(kq_done, b + 1)
                nc.scalar.activation(kq[:], kq_out, ACT.Copy).then_inc(kq_ready, 1)

            def exponential(b):
                act.wait_ge(max_ready, b + 1)
                for t in range(NT):
                    nc.scalar.activation(prob[:, t], s_out[:, t], ACT.Exp, bias=nmx[:, t:t + 1],
                                         accum_out=rsum[:, t:t + 1]).then_inc(exp_ready, 1)

            def copy_pT(b):
                act.wait_ge(pT_done, b + 1)
                nc.scalar.activation(pT[:].rearrange("s t i -> s (t i)"), ps_p[0:S, 0:NT * P], ACT.Copy).then_inc(pT_ready, 1)

            act.wait_ge(w_loaded, LOADED)
            copy_x(0)
            copy_k(0)
            copy_kq(0)
            with act.Fori(0, B - 1) as b:
                exponential(b)
                copy_x(b + 1)
                copy_k(b + 1)
                copy_pT(b)
                copy_kq(b + 1)
            exponential(B - 1)
            copy_pT(B - 1)

        @block.vector
        def _(dve):
            def norm_stats(b):
                for t in range(NT):
                    last = nc.vector.bn_stats(st[:, t], res[:, b, t])
                last.then_inc(stats, 1)
                dve.wait_ge(stats, b + 1)
                dve.sem_inc(seen)
                for t in range(NT):
                    last = nc.vector.bn_aggr(mv[:, t], st[:, t])
                last.then_inc(aggr, 1)

            def norm_apply(b):
                dve.wait_ge(rstd_ready, b + 1)
                dve.wait_ge(xT_done, b)
                dve.wait_ge(resid_ready, b)
                for t in range(NT):
                    last = nc.vector.tensor_scalar(xn[:, t], res[:, b, t], mv[:, t, 0:1], rstd[:, t:t + 1],
                                                   ALU.subtract, ALU.mult)
                last.then_inc(xn_ready, 1)

            def maxima(b):
                dve.wait_ge(s_done, b + 1)
                nc.vector.tensor_reduce(nmx[:], s_out, AX.X, ALU.max, negate=True).then_inc(max_ready, 1)

            def copy_v(b):
                dve.wait_ge(v_done, b + 1)
                nc.vector.tensor_tensor(v[:], ps_v[0:S, 0:D], bv[:], ALU.add).then_inc(v_ready, 1)

            def add_out(b):
                dve.wait_ge(exp_ready, b * NT + NT)
                nc.vector.reciprocal(rinv[:], rsum[:]).then_inc(inv_ready, 1)
                dve.wait_ge(inv_ready, b + 1)
                dve.wait_ge(resid_ready, b + 1)
                dve.wait_ge(o_done, b + 1)
                for t in range(NT):
                    nc.vector.scalar_tensor_tensor(res[:, b, t], ps_o[:, t], rinv[:, t:t + 1], res[:, b, t],
                                                   ALU.mult, ALU.add).then_inc(res_ready, 1)

            dve.wait_ge(w_loaded, LOADED)
            nc.vector.tensor_copy(bq_rows[:], bq[:].unsqueeze(2).to_broadcast([P, KD, P])).then_inc(bias_ready, 1)
            norm_stats(0)
            norm_apply(0)
            copy_v(0)
            with dve.Fori(0, B - 1) as b:
                norm_stats(b + 1)
                maxima(b)
                norm_apply(b + 1)
                add_out(b)
                copy_v(b + 1)
            maxima(B - 1)
            add_out(B - 1)


def tokens_and_logits(nc, res, ident, half, logits, gammaT, betaT, gateT, x5_d, out):
    E = logits.shape[2]
    with ExitStack() as ctx:
        def sb(name, shape, dt=F32):
            return ctx.enter_context(nc.sbuf_tensor("F_" + name, shape, dt))

        def sem(name):
            return ctx.enter_context(nc.semaphore("F_" + name))

        st = sb("st", [P, NT, 6])
        mv = sb("mv", [P, NT, 2])
        veps = sb("veps", [P, 2, NT])
        rstd = sb("rstd", [P, 2, NT])
        x5 = sb("x5", [P, 2, NT, D])
        n5 = sb("n5", [P, NT, D])
        fin = sb("fin", [P, 2, NT, D])
        tokT = sb("tokT", [P, KD, T])
        ps_x = ctx.enter_context(nc.psum_tensor("F_ps_x", [P, KD, T], F32))
        ps_l = ctx.enter_context(nc.psum_tensor("F_ps_l", [P, NT, E], F32))
        stats, seen, aggr, var_eps, rstd_ready, x5_ready, n5_ready, xT_done, tok_ready, l_done, l_ready, x5_out0, x5_out1, fin_ready, fin_out0, fin_out1 = map(
            sem, "stats seen aggr var_eps rstd_ready x5_ready n5_ready xT_done tok_ready l_done l_ready x5_out0 x5_out1 fin_ready fin_out0 fin_out1".split())
        x5_out, fin_out = (x5_out0, x5_out1), (fin_out0, fin_out1)
        x5_rows = x5_d.rearrange("(b t p) d -> b p t d", p=P, t=NT)
        out_rows = out.rearrange("b (t p) d -> b p t d", p=P)

        block = ctx.enter_context(nc.Block())

        @block.sync
        def _(sp):
            with sp.Fori(0, B // 2) as j:
                for u in range(2):
                    b = j * 2 + u
                    sp.wait_ge(x5_ready, b + 1)
                    sp.dma_start(x5_rows[b], x5[:, u]).then_inc(x5_out[u], 16)
                    sp.wait_ge(fin_ready, b + 1)
                    sp.dma_start(out_rows[b], fin[:, u]).then_inc(fin_out[u], 16)
            for s in (*x5_out, *fin_out):
                sp.wait_ge(s, B // 2 * 16)

        @block.gpsimd
        def _(pool):
            with pool.Fori(0, B * 2) as n:
                pool.wait_ge(aggr, n + 1)
                pool.sem_inc(seen)
                nc.gpsimd.tensor_scalar(veps[:, 0], mv[:, :, 1], 1e-5, None, ALU.add)
                nc.gpsimd.tensor_scalar(veps[:, 1], mv[:, :, 1], 0.25e-5, None, ALU.add).then_inc(var_eps, 1)
                pool.wait_ge(var_eps, n + 1)
                for i in range(2):
                    last = nc.gpsimd.tensor_tensor(rstd[:, i], veps[:, i], half[:], ALU.pow)
                last.then_inc(rstd_ready, 1)

        @block.tensor
        def _(pe):
            with pe.Fori(0, B // 2) as j:
                for u in range(2):
                    b = j * 2 + u
                    pe.wait_ge(n5_ready, b + 1)
                    pe.wait_ge(tok_ready, b)
                    for k in range(KD):
                        for t in range(NT):
                            last = nc.tensor.transpose(ps_x[:, k, t * P:(t + 1) * P], n5[:, t, k * P:(k + 1) * P], ident[:])
                    last.then_inc(xT_done, 1)
                    pe.wait_ge(tok_ready, b + 1)
                    pe.wait_ge(l_ready, b)
                    for t in range(NT):
                        for k in range(KD):
                            last = nc.tensor.matmul(ps_l[:, t], tokT[:, k, t * P:(t + 1) * P], gateT[:, k], start=k == 0, stop=k == KD - 1)
                    last.then_inc(l_done, 1)

        @block.scalar
        def _(act):
            with act.Fori(0, B) as b:
                act.wait_ge(xT_done, b + 1)
                for k in range(KD):
                    last = nc.scalar.activation(tokT[:, k], ps_x[:, k], ACT.Identity, scale=gammaT[:, k:k + 1], bias=betaT[:, k:k + 1])
                last.then_inc(tok_ready, 1)

        @block.vector
        def _(dve):
            def norm(src, dst, n, ready, twice=None):
                for t in range(NT):
                    last = nc.vector.bn_stats(st[:, t], src[t])
                last.then_inc(stats, 1)
                dve.wait_ge(stats, n + 1)
                dve.sem_inc(seen)
                for t in range(NT):
                    last = nc.vector.bn_aggr(mv[:, t], st[:, t])
                last.then_inc(aggr, 1)
                dve.wait_ge(rstd_ready, n + 1)
                for t in range(NT):
                    last = nc.vector.tensor_scalar(dst[t], src[t], mv[:, t, 0:1], rstd[:, 0, t:t + 1], ALU.subtract, ALU.mult)
                last.then_inc(ready, 1)
                if twice is not None:
                    for t in range(NT):
                        last = nc.vector.tensor_scalar(twice[t], src[t], mv[:, t, 0:1], rstd[:, 1, t:t + 1], ALU.subtract, ALU.mult)
                    last.then_inc(fin_ready, 1)

            with dve.Fori(0, B // 2) as j:
                for u in range(2):
                    b = j * 2 + u
                    kept = [x5[:, u, t] for t in range(NT)]
                    dve.wait_ge(x5_out[u], j * 16)
                    norm([res[:, b, t] for t in range(NT)], kept, b * 2, x5_ready)
                    dve.wait_ge(x5_ready, b + 1)
                    dve.wait_ge(fin_out[u], j * 16)
                    dve.wait_ge(xT_done, b)
                    norm(kept, [n5[:, t] for t in range(NT)], b * 2 + 1, n5_ready, [fin[:, u, t] for t in range(NT)])
                    dve.wait_ge(l_done, b + 1)
                    nc.vector.tensor_copy(logits[:, bass.ds(j * 4 + 2 * u, NT)], ps_l[:]).then_inc(l_ready, 1)


def route(nc, ones, logits, before, table_d, capacity):
    NTILE, E = logits.shape[1], logits.shape[2]
    NONE = 1 << 20
    with ExitStack() as ctx:
        def sb(name, shape, dt=F32):
            return ctx.enter_context(nc.sbuf_tensor("G_" + name, shape, dt))

        def sem(name):
            return ctx.enter_context(nc.semaphore("G_" + name))

        none = sb("none", [P, E * capacity // P, 2], I32)
        no_i = sb("no_i", [P, E], I32)
        no = sb("no", [P, E])
        no8 = sb("no8", [P, E])
        top = sb("top", [P, NTILE])
        is_top = sb("is_top", [P, NTILE, E])
        cand = sb("cand", [P, NTILE, E])
        first = sb("first", [P, NTILE])
        onehot = sb("onehot", [P, NTILE, E])
        shifted = sb("shifted", [P, NTILE, E])
        expo = sb("expo", [P, NTILE, E])
        esum = sb("esum", [P, NTILE])
        prob = sb("prob", [P, NTILE])
        run = [sb(f"run{i}", [P, NTILE, E]) for i in range(2)]
        tot = sb("tot", [P, NTILE, E])
        offset = sb("offset", [P, NTILE, E])
        ahead = sb("ahead", [P, NTILE, E])
        rank = sb("rank", [P, NTILE])
        over = sb("over", [P, NTILE])
        slot = sb("slot", [P, NTILE])
        slot_i = sb("slot_i", [P, NTILE], I32)
        entry = sb("entry", [P, NTILE, 2], I32)
        ps_in = ctx.enter_context(nc.psum_tensor("G_ps_in", [P, NTILE, E], F32))
        ps_tot = ctx.enter_context(nc.psum_tensor("G_ps_tot", [P, NTILE, E], F32))
        consts, none_out, chain, shifted_ready, expo_ready, onehot_ready, counted, entry_ready, scattered = map(
            sem, "consts none_out chain shifted_ready expo_ready onehot_ready counted entry_ready scattered".split())
        block = ctx.enter_context(nc.Block())

        @block.gpsimd
        def _(pool):
            nc.gpsimd.iota(none[:], [[0, E * capacity // P], [0, 2]], base=NONE, channel_multiplier=0).then_inc(consts, 1)
            nc.gpsimd.iota(no_i[:], [[1, E]], base=0, channel_multiplier=0).then_inc(consts, 1)
            nc.gpsimd.iota(entry[:, :, 0], [[P, NTILE]], base=0, channel_multiplier=1).then_inc(consts, 1)
            pool.wait_ge(none_out, 16)
            pool.wait_ge(entry_ready, 1)
            for i in range(NTILE):
                nc.gpsimd.indirect_dma_start(out=table_d, out_offset=bass.IndirectOffsetOnAxis(ap=slot_i[:, i:i + 1], axis=0),
                                             in_=entry[:, i], in_offset=None, bounds_check=E * capacity - 1,
                                             oob_is_err=False).then_inc(scattered, 16)
            pool.wait_ge(scattered, 16 * NTILE)

        @block.sync
        def _(sp):
            sp.wait_ge(consts, 3)
            sp.dma_start(table_d.rearrange("(s p) k -> p s k", p=P), none[:]).then_inc(none_out, 16)
            sp.wait_ge(none_out, 16)

        @block.tensor
        def _(pe):
            pe.wait_ge(onehot_ready, 1)
            nc.tensor.matmul(ps_in[:], before[:], onehot[:], start=True, stop=True)
            nc.tensor.matmul(ps_tot[:], ones[:], onehot[:], start=True, stop=True).then_inc(counted, 1)

        @block.scalar
        def _(act):
            act.wait_ge(shifted_ready, 1)
            nc.scalar.activation(expo[:], shifted[:], ACT.Exp).then_inc(expo_ready, 1)

        @block.vector
        def _(dve):
            count = [0]

            def then(ins):
                count[0] += 1
                ins.then_inc(chain, 1)
                dve.wait_ge(chain, count[0])

            def per_tile(x):
                return x[:].unsqueeze(2).to_broadcast([P, NTILE, E])

            def per_expert(x):
                return x[:].unsqueeze(1).to_broadcast([P, NTILE, E])

            dve.wait_ge(consts, 3)
            then(nc.vector.tensor_copy(no[:], no_i[:]))
            nc.vector.tensor_scalar(no8[:], no[:], float(E), None, ALU.add)
            then(nc.vector.tensor_reduce(top[:], logits[:], AX.X, ALU.max))
            nc.vector.tensor_tensor(shifted[:], logits[:], per_tile(top), ALU.subtract).then_inc(shifted_ready, 1)
            then(nc.vector.tensor_tensor(is_top[:], logits[:], per_tile(top), ALU.is_ge))
            then(nc.vector.scalar_tensor_tensor(cand[:], is_top[:], -float(E), per_expert(no8), ALU.mult, ALU.add))
            then(nc.vector.tensor_reduce(first[:], cand[:], AX.X, ALU.min))
            nc.vector.tensor_tensor(onehot[:], per_expert(no), per_tile(first), ALU.is_equal).then_inc(onehot_ready, 1)
            dve.wait_ge(expo_ready, 1)
            then(nc.vector.tensor_reduce(esum[:], expo[:], AX.X, ALU.add))
            then(nc.vector.reciprocal(prob[:], esum[:]))
            nc.vector.tensor_scalar(entry[:, :, 1].bitcast(F32), prob[:], 0.5, None, ALU.mult)
            dve.wait_ge(counted, 1)
            then(nc.vector.tensor_copy(tot[:], ps_tot[:]))
            then(nc.vector.tensor_copy(run[0][:], tot[:]))
            k, i = 1, 0
            while k < NTILE:
                nc.vector.tensor_copy(run[1 - i][:, 0:k], run[i][:, 0:k])
                then(nc.vector.tensor_tensor(run[1 - i][:, k:], run[i][:, k:], run[i][:, 0:NTILE - k], ALU.add))
                k, i = 2 * k, 1 - i
            then(nc.vector.tensor_tensor(offset[:], run[i][:], tot[:], ALU.subtract))
            then(nc.vector.tensor_tensor(ahead[:], ps_in[:], offset[:], ALU.add))
            then(nc.vector.tensor_tensor(ahead[:], ahead[:], onehot[:], ALU.mult))
            then(nc.vector.tensor_reduce(rank[:], ahead[:], AX.X, ALU.add))
            then(nc.vector.tensor_scalar(over[:], rank[:], float(capacity), float(NONE), ALU.is_ge, ALU.mult))
            then(nc.vector.scalar_tensor_tensor(slot[:], first[:], float(capacity), rank[:], ALU.mult, ALU.add))
            nc.vector.tensor_tensor(slot_i[:], slot[:], over[:], ALU.add).then_inc(entry_ready, 1)


def moe_ffn(nc, ident, half, gammaT, betaT, table_d, x5_d, wi_d, wo_d, out, capacity):
    E, _, I = wi_d.shape
    NTOK = x5_d.shape[0]
    TI, MI = capacity // P, I // P
    EPS = 1e-5
    rows = out.rearrange("b t d -> (b t) d")
    with ExitStack() as ctx:
        def sb(name, shape, dt=F32):
            return ctx.enter_context(nc.sbuf_tensor("H_" + name, shape, dt))

        def psum(name, shape):
            return ctx.enter_context(nc.psum_tensor("H_" + name, shape, F32))

        def sem(name):
            return ctx.enter_context(nc.semaphore("H_" + name))

        table = sb("table", [P, E * TI, 2], I32)
        slots = sb("slots", [P, 2, TI, 2], I32)
        wi = sb("wi", [P, 2, KD, I])
        wo = sb("wo", [P, 2, MI, D])
        xg = sb("xg", [P, 2, TI, D])
        ng = sb("ng", [P, TI, D])
        tokT = sb("tokT", [P, KD, capacity])
        hT = sb("hT", [P, MI, capacity])
        fin = sb("fin", [P, TI, D])
        st = sb("st", [P, TI, 6])
        mv = sb("mv", [P, TI, 2])
        veps = sb("veps", [P, TI])
        rstd = sb("rstd", [P, TI])
        ps_x = [psum(f"ps_x{i}", [P, capacity]) for i in range(KD)]
        ps_h = [psum(f"ps_h{i}", [P, capacity]) for i in range(2)]
        ps_d = [psum(f"ps_d{i}", [P, 2, D]) for i in range(TI // 2)]
        table_in, w_in0, w_in1, gathered0, gathered1, clear, staged, scattered = map(
            sem, "table_in w_in0 w_in1 gathered0 gathered1 clear staged scattered".split())
        stats, seen, aggr, var_eps, rstd_ready, ng_ready, xT_done, tok_ready, h_done, h_ready, d_done, sum_ready, fin_ready = map(
            sem, "stats seen aggr var_eps rstd_ready ng_ready xT_done tok_ready h_done h_ready d_done sum_ready fin_ready".split())
        w_in, gathered = (w_in0, w_in1), (gathered0, gathered1)

        block = ctx.enter_context(nc.Block())

        @block.sync
        def _(sp):
            sp.dma_start(table[:], table_d.rearrange("(s p) k -> p s k", p=P)).then_inc(table_in, 16)

            def load(e, u):
                sp.dma_start(wi[:, u], wi_d[e].rearrange("(k p) n -> p k n", p=P)).then_inc(w_in[u], 16)
                sp.dma_start(wo[:, u], wo_d[e].rearrange("(k p) n -> p k n", p=P)).then_inc(w_in[u], 16)
            load(0, 0)
            load(1, 1)
            with sp.Fori(0, E // 2 - 1) as j:
                for u in range(2):
                    sp.wait_ge(d_done, j * 2 * TI + (u + 1) * TI)
                    load(j * 2 + (2 + u), u)

        @block.gpsimd
        def _(pool):
            def norm_scale(n, eps):
                pool.wait_ge(aggr, n + 1)
                pool.sem_inc(seen)
                nc.gpsimd.tensor_scalar(veps[:], mv[:, :, 1], eps, None, ALU.add).then_inc(var_eps, 1)
                pool.wait_ge(var_eps, n + 1)
                for i in range(TI // NT):
                    last = nc.gpsimd.tensor_tensor(rstd[:, i * NT:(i + 1) * NT], veps[:, i * NT:(i + 1) * NT], half[:], ALU.pow)
                last.then_inc(rstd_ready, 1)

            def gather(e, u, n):
                nc.gpsimd.tensor_copy(slots[:, u], table[:, bass.ds(e * TI, TI)] if n is None else table[:, n * TI:(n + 1) * TI])\
                    .then_inc(staged, 1)
                pool.wait_ge(staged, e + 1)
                pool.sem_inc(seen)
                for i in range(TI):
                    nc.gpsimd.indirect_dma_start(out=xg[:, u, i], out_offset=None, in_=x5_d,
                                                 in_offset=bass.IndirectOffsetOnAxis(ap=slots[:, u, i, 0:1], axis=0),
                                                 bounds_check=NTOK - 1, oob_is_err=False).then_inc(gathered[u], 16)

            def scatter(e, u):
                pool.wait_ge(fin_ready, e + 1)
                pool.sem_inc(seen)
                for i in range(TI):
                    nc.gpsimd.indirect_dma_start(out=rows, out_offset=bass.IndirectOffsetOnAxis(ap=slots[:, u, i, 0:1], axis=0),
                                                 in_=fin[:, i], in_offset=None, bounds_check=NTOK - 1,
                                                 oob_is_err=False).then_inc(scattered, 16)

            def body(e, u, more, more2):
                if more:
                    norm_scale(e * 2 + 1, EPS)
                norm_scale(e * 2 + 2 if more else E * 2 - 1, EPS / 4)
                scatter(e, u)
                if more2:
                    pool.wait_ge(scattered, e * TI * 16 + TI * 16)
                    gather(e + 2, u, None)

            nc.gpsimd.memset(xg[:], 0.0).then_inc(clear, 1)
            pool.wait_ge(clear, 1)
            pool.wait_ge(table_in, 16)
            gather(0, 0, 0)
            gather(1, 1, 1)
            norm_scale(0, EPS)
            with pool.Fori(0, E // 2 - 1) as j:
                body(j * 2, 0, True, True)
                body(j * 2 + 1, 1, True, True)
            body(E - 2, 0, True, False)
            body(E - 1, 1, False, False)
            pool.wait_ge(scattered, 16 * TI * E)

        @block.tensor
        def _(pe):
            def transpose(e):
                pe.wait_ge(ng_ready, e + 1)
                for k in range(KD):
                    for t in range(TI):
                        last = nc.tensor.transpose(ps_x[k][:, t * P:(t + 1) * P], ng[:, t, k * P:(k + 1) * P], ident[:])
                last.then_inc(xT_done, 1)

            def hidden(e, u, m, first):
                if not (first and m < 2):
                    pe.wait_ge(h_ready, e * MI + (m - 1))
                for k in range(KD):
                    last = nc.tensor.matmul(ps_h[m % 2][:], wi[:, u, k, m * P:(m + 1) * P], tokT[:, k], start=k == 0, stop=k == KD - 1)
                last.then_inc(h_done, 1)

            def down(e, u, first):
                for t in range(TI):
                    if t % 2 == 0 and not first:
                        pe.wait_ge(sum_ready, e * TI + (t + 2 - TI))
                    for m in range(MI):
                        if t == 0 and m >= MI - 2:
                            pe.wait_ge(h_ready, e * MI + m + 1)
                        elif t == 0 and m == 0:
                            pe.wait_ge(h_ready, e * MI + MI - 2)
                        last = nc.tensor.matmul(ps_d[t // 2][:, t % 2], hT[:, m, t * P:(t + 1) * P], wo[:, u, m],
                                                start=m == 0, stop=m == MI - 1)
                    last.then_inc(d_done, 1)

            def body(e, u, j, first=False, more=True):
                pe.wait_ge(w_in[u], j * 32 + 32)
                pe.wait_ge(tok_ready, e + 1)
                for m in range(MI):
                    hidden(e, u, m, first)
                if more:
                    transpose(e + 1)
                down(e, u, first)

            transpose(0)
            body(0, 0, 0, first=True)
            body(1, 1, 0)
            with pe.Fori(1, E // 2 - 1) as j:
                body(j * 2, 0, j)
                body(j * 2 + 1, 1, j)
            body(E - 2, 0, E // 2 - 1)
            body(E - 1, 1, E // 2 - 1, more=False)

        @block.scalar
        def _(act):
            def tokens(e):
                act.wait_ge(xT_done, e + 1)
                for k in range(KD):
                    last = nc.scalar.activation(tokT[:, k], ps_x[k][:], ACT.Identity, scale=gammaT[:, k:k + 1], bias=betaT[:, k:k + 1])
                last.then_inc(tok_ready, 1)

            def body(e, more):
                for m in range(MI):
                    act.wait_ge(h_done, e * MI + m + 1)
                    nc.scalar.activation(hT[:, m], ps_h[m % 2][:], ACT.Gelu).then_inc(h_ready, 1)
                if more:
                    tokens(e + 1)

            tokens(0)
            with act.Fori(0, E - 1) as e:
                body(e, True)
            body(E - 1, False)

        @block.vector
        def _(dve):
            def norm(src, dst, n, ready):
                for t in range(TI):
                    last = nc.vector.bn_stats(st[:, t], src[:, t])
                last.then_inc(stats, 1)
                dve.wait_ge(stats, n + 1)
                dve.sem_inc(seen)
                for t in range(TI):
                    last = nc.vector.bn_aggr(mv[:, t], st[:, t])
                last.then_inc(aggr, 1)
                dve.wait_ge(rstd_ready, n + 1)
                for t in range(TI):
                    last = nc.vector.tensor_scalar(dst[:, t], src[:, t], mv[:, t, 0:1], rstd[:, t:t + 1], ALU.subtract, ALU.mult)
                last.then_inc(ready, 1)

            def before(e, u, j, n):
                dve.wait_ge(gathered[u], j * TI * 16 + TI * 16)
                dve.wait_ge(xT_done, e)
                norm(xg[:, u], ng[:], n, ng_ready)

            def after(e, u, n, first):
                for t in range(TI):
                    dve.wait_ge(d_done, e * TI + 2 * (t // 2) + 2)
                    nc.vector.scalar_tensor_tensor(xg[:, u, t], ps_d[t // 2][:, t % 2], slots[:, u, t, 1:2].bitcast(F32), xg[:, u, t],
                                                   ALU.mult, ALU.add).then_inc(sum_ready, 1)
                dve.wait_ge(sum_ready, e * TI + TI)
                if not first:
                    dve.wait_ge(scattered, e * TI * 16)
                norm(xg[:, u], fin[:], n, fin_ready)

            before(0, 0, 0, 0)
            before(1, 1, 0, 1)
            after(0, 0, 2, True)
            with dve.Fori(1, E // 2) as j:
                before(j * 2, 0, j, j * 4 - 1)
                after(j * 2 - 1, 1, j * 4, False)
                before(j * 2 + 1, 1, j, j * 4 + 1)
                after(j * 2, 0, j * 4 + 2, False)
            after(E - 1, 1, E * 2 - 1, False)


def clear_used_semaphores(nc):
    used = sorted(nc.released_uncleared_semaphores)
    with nc.Block() as block:
        @block.gpsimd
        def _(pool):
            start = 0
            for n in range(1, len(used) + 1):
                if n == len(used) or used[n] != used[n - 1] + 1:
                    pool.sem_clear(range(used[start], used[n - 1] + 1))
                    start = n


def program(nc, i, out, stop):
    with ExitStack() as ctx:
        res = ctx.enter_context(nc.sbuf_tensor("res", [P, B, NT, D], F32))
        ident = ctx.enter_context(nc.sbuf_tensor("ident", [P, P], F32))
        ones = ctx.enter_context(nc.sbuf_tensor("ones", [P, P], F32))
        half = ctx.enter_context(nc.sbuf_tensor("half", [P, NT], F32))
        eps = ctx.enter_context(nc.sbuf_tensor("eps", [P, NT], F32))
        ctxT = ctx.enter_context(nc.sbuf_tensor("ctxT", [P, B, i["ctxT"].shape[2]], F32))
        set_ready = ctx.enter_context(nc.semaphore("set_ready"))
        ctx_loaded = ctx.enter_context(nc.semaphore("ctx_loaded"))
        with nc.Block() as block:
            @block.sync
            def _(sp):
                sp.dma_start(ctxT[:], i["ctxT"].rearrange("b p s -> p b s")).then_inc(ctx_loaded, 16)
                sp.wait_ge(ctx_loaded, 16)

            @block.gpsimd
            def _(pool):
                nc.gpsimd.memset(half[:], -0.5)
                nc.gpsimd.memset(eps[:], 1e-5)
                nc.gpsimd.memset(ones[:], 1.0).then_inc(set_ready, 1)
                pool.wait_ge(set_ready, 1)
                nc.gpsimd.affine_select(out=ident[:], in_=ones[:], compare_op=ALU.is_equal, fill=0.0, base=0,
                                        pattern=[[-1, P]], channel_multiplier=1)
        linear_attention(nc, res, ident, i["x"], i["L0_attn_W_thetaT"], i["L0_attn_W_phiT"], i["L0_attn_W_gT"])
        if stop > 0:
            cross_attention(nc, res, ident, half, eps, ctxT, i["L0_xattn_Wq"], i["L0_xattn_Wk"], i["L0_xattn_Wv"], i["L0_xattn_Wo"],
                            i["L0_xattn_bo"])
        if stop > 1:
            expert_ffn(nc, res, ident, half, eps, i["L0_ffn_router_indices"], i["L0_ffn_routing_weights"], i["L0_ffn_gate_up"],
                       i["L0_ffn_gate_up_bias"], i["L0_ffn_down_proj"], i["L0_ffn_down_proj_bias"])
        if stop > 2:
            gated_retention(nc, res, ident, half, {k: i["L1_attn_" + k] for k in ("wqk", "wvg", "wgt", "wo")}, i)
        if stop > 3:
            cross_attention_single(nc, res, ident, half, ctxT, i["L1_xattn_WqT"], i["L1_xattn_bq"], i["L1_xattn_Wk"],
                                   i["L1_xattn_bk"], i["L1_xattn_Wv"], i["L1_xattn_bv"])
        if stop > 4:
            NTOK, E = B * T, i["L1_ffn_wi"].shape[0]
            x5_d = nc.dram_tensor("x5_d", (NTOK, D), F32, kind="Internal").ap()
            table_d = nc.dram_tensor("table_d", (E * CAPACITY, 2), I32, kind="Internal").ap()
            logits = ctx.enter_context(nc.sbuf_tensor("logits", [P, NTOK // P, E], F32))
            before = ctx.enter_context(nc.sbuf_tensor("before", [P, P], F32))
            gateT = ctx.enter_context(nc.sbuf_tensor("gateT", [P, KD, E], F32))
            gammaT = ctx.enter_context(nc.sbuf_tensor("gammaT", [P, KD], F32))
            betaT = ctx.enter_context(nc.sbuf_tensor("betaT", [P, KD], F32))
            gate_loaded = ctx.enter_context(nc.semaphore("gate_loaded"))
            with nc.Block() as block:
                @block.sync
                def _(sp):
                    sp.dma_start(before[:], i["before"]).then_inc(gate_loaded, 16)
                    with nc.allow_non_contiguous_dma("small: the router's weights, one element a partition"):
                        sp.dma_start(gateT[:], i["L1_ffn_gateT"].rearrange("(k p) e -> p k e", p=P)).then_inc(gate_loaded, 16)
                        sp.dma_start(gammaT[:], i["L1_ffn_ln_gamma"].rearrange("(k p) -> p k", p=P)).then_inc(gate_loaded, 16)
                        sp.dma_start(betaT[:], i["L1_ffn_ln_beta"].rearrange("(k p) -> p k", p=P)).then_inc(gate_loaded, 16)
                    sp.wait_ge(gate_loaded, 64)
            clear_used_semaphores(nc)
            tokens_and_logits(nc, res, ident, half, logits, gammaT, betaT, gateT, x5_d, out)
            route(nc, ones, logits, before, table_d, CAPACITY)
            moe_ffn(nc, ident, half, gammaT, betaT, table_d, x5_d, i["L1_ffn_wi"], i["L1_ffn_wo"], out, CAPACITY)
            return
        s_out = ctx.enter_context(nc.semaphore("s_out"))
        with nc.Block() as block:
            @block.sync
            def _(sp):
                sp.dma_start(out.rearrange("b (t p) d -> p b t d", p=P), res[:]).then_inc(s_out, 16)
                sp.wait_ge(s_out, 16)


CAPACITY = 512
STOP = 6


def kernel(**inputs):
    import ml_dtypes
    import numpy as np
    import concourse.bacc as bacc
    from concourse.bass_utils import run_bass_kernel_spmd

    nc = bacc.Bacc("TRN2", target_bir_lowering=False, num_devices=1)
    given = {k: np.asarray(v) for k, v in inputs.items()}
    arrays = {k: given[k] for k in ("x", "L0_xattn_Wq", "L0_xattn_Wk", "L0_xattn_Wv", "L0_xattn_Wo", "L0_xattn_bo")}
    arrays["ctxT"] = given["ctx_512"].transpose(0, 2, 1)
    for k in ("L0_attn_W_theta", "L0_attn_W_phi", "L0_attn_W_g"):
        arrays[k + "T"] = given[k].T
    for k in ("L0_ffn_router_indices", "L0_ffn_routing_weights", "L0_ffn_down_proj", "L0_ffn_down_proj_bias"):
        arrays[k] = given[k]
    w, bias = given["L0_ffn_gate_up_proj"], given["L0_ffn_gate_up_proj_bias"]
    arrays["L0_ffn_gate_up"] = np.concatenate([w[..., ::2], w[..., 1::2]], -1)
    arrays["L0_ffn_gate_up_bias"] = np.concatenate([bias[:, ::2], bias[:, 1::2]], -1).reshape(len(bias), -1, P).transpose(2, 0, 1)
    for k in ("L1_xattn_bq", "L1_xattn_Wk", "L1_xattn_bk", "L1_xattn_Wv", "L1_xattn_bv", "L1_ffn_ln_gamma", "L1_ffn_ln_beta",
              "L1_ffn_wi", "L1_ffn_wo"):
        arrays[k] = given[k]
    arrays["L1_xattn_WqT"], arrays["L1_ffn_gateT"] = given["L1_xattn_Wq"].T, given["L1_ffn_gate_weight"].T
    arrays["L1_attn_wqk"] = np.concatenate([given["L1_attn_Wq"], given["L1_attn_Wk"]], 1)
    arrays["L1_attn_wvg"] = np.concatenate([given["L1_attn_Wv"], given["L1_attn_Wg"]], 1)
    arrays["L1_attn_wgt"], arrays["L1_attn_wo"] = given["L1_attn_Wgt"], given["L1_attn_Wo"]
    row, col = np.arange(P)[:, None], np.arange(P)[None, :]
    arrays["before"] = (row < col).astype(np.float32)
    arrays["upto"] = ((row <= col) / 16).astype(np.float32)
    arrays["after"] = ((row > col) / 16).astype(np.float32)
    arrays["head_mask"] = ((row // RET_D % 2 == np.arange(2)) / 4).astype(np.float32)
    arrays["block_mask"] = ((row // RET_D == col // RET_D) / 4).astype(np.float32)
    heads = np.array([retention_head(p) for p in range(RET_H)])
    of_head = (row % 32 == heads) & (row // 32 != 1)
    arrays["sel"] = np.repeat(of_head[:, :, None], P, 2).astype(ml_dtypes.bfloat16)
    arrays["nsel"] = -arrays["sel"]
    arrays = {k: np.ascontiguousarray(a) for k, a in arrays.items()}
    ins = {k: nc.dram_tensor("in_" + k, a.shape, mybir.dt.from_np(a.dtype), kind="ExternalInput").ap() for k, a in arrays.items()}
    out = nc.dram_tensor("out", (B, T, D), F32, kind="ExternalOutput").ap()
    program(nc, ins, out, STOP)
    r = run_bass_kernel_spmd(nc, [{"in_" + k: a for k, a in arrays.items()}], core_ids=[0])
    return r.results[0]["out"]
```

```python
from contextlib import ExitStack
import concourse.bass as bass
from concourse import mybir

ALU = mybir.AluOpType
ACT = mybir.ActivationFunctionType
AX = mybir.AxisListType
F32 = mybir.dt.float32
BF16 = mybir.dt.bfloat16
I32 = mybir.dt.int32

P = 128
B, T, D = 32, 256, 256
NT = T // P
KD = D // P
LATENT = 64


def linear_attention(nc, res, ident, x_in, wthT, wphT, wgT):
    with ExitStack() as ctx:
        def sb(name, shape, dt=F32):
            return ctx.enter_context(nc.sbuf_tensor("A_" + name, shape, dt))

        def psum(name, shape):
            return ctx.enter_context(nc.psum_tensor("A_" + name, shape, F32))

        def sem(name):
            return ctx.enter_context(nc.semaphore("A_" + name))

        xn = sb("xn", [P, NT, D])
        xT = sb("xT", [P, KD, T])
        theta_w = sb("theta_w", [P, KD, LATENT])
        phi_w = sb("phi_w", [P, KD, LATENT])
        g_w = sb("g_w", [P, KD, D])
        gram = sb("gram", [P, KD, D])
        u = sb("u", [P, KD, LATENT])
        v = sb("v", [LATENT, D])
        thetaT = sb("thetaT", [LATENT, T])
        ps_xT = psum("ps_xT", [P, KD, T])
        ps_gram = psum("ps_gram", [P, KD, D])
        ps_u = psum("ps_u", [P, KD, LATENT])
        ps_v = psum("ps_v", [LATENT, D])
        ps_theta = psum("ps_theta", [LATENT, T])
        ps_out = psum("ps_out", [P, NT, D])
        names = "weights x_loaded xn xT_done xT gram_done gram u_done u v_done v theta_done theta out_done out".split()
        s = {n: sem(n) for n in names}

        block = ctx.enter_context(nc.Block())

        @block.sync
        def _(sp):
            sp.dma_start(theta_w[:], wthT.rearrange("(k p) l -> p k l", p=P)).then_inc(s["weights"], 16)
            sp.dma_start(phi_w[:], wphT.rearrange("(k p) l -> p k l", p=P)).then_inc(s["weights"], 16)
            sp.dma_start(g_w[:], wgT.rearrange("(k p) l -> p k l", p=P)).then_inc(s["weights"], 16)
            for c in range(B // 2):
                if c:
                    sp.wait_ge(s["x_loaded"], 16 * c)
                sp.dma_start(res[:, 2 * c:2 * c + 2], x_in[2 * c:2 * c + 2].rearrange("b (t p) d -> p b t d", p=P)).then_inc(s["x_loaded"], 16)

        @block.gpsimd
        def _(pool):
            def copy_x(b):
                pool.wait_ge(s["gram_done"], b)
                nc.gpsimd.tensor_copy(xn[:], res[:, b]).then_inc(s["xn"], 1)
            with pool.Fori(0, B // 2) as j:
                pool.wait_ge(s["x_loaded"], j * 16 + 16)
                copy_x(j * 2)
                copy_x(j * 2 + 1)

        @block.tensor
        def _(pe):
            pe.wait_ge(s["weights"], 48)

            def transpose_x(b):
                pe.wait_ge(s["xn"], b + 1)
                for k in range(KD):
                    for t in range(NT):
                        last = nc.tensor.transpose(ps_xT[:, k, t * P:(t + 1) * P], xn[:, t, k * P:(k + 1) * P], ident[:])
                last.then_inc(s["xT_done"], 1)

            def gram_mm(b):
                for k in range(KD):
                    for t in range(NT):
                        last = nc.tensor.matmul(ps_gram[:, k], xn[:, t, k * P:(k + 1) * P], xn[:, t], start=t == 0, stop=t == NT - 1)
                last.then_inc(s["gram_done"], 1)

            def theta_mm(b):
                pe.wait_ge(s["xT"], b + 1)
                pe.wait_ge(s["theta"], b)
                for k in range(KD):
                    last = nc.tensor.matmul(ps_theta[:], theta_w[:, k], xT[:, k], start=k == 0, stop=k == KD - 1)
                last.then_inc(s["theta_done"], 1)

            def u_mm(b):
                pe.wait_ge(s["gram"], b + 1)
                for m in range(KD):
                    for k in range(KD):
                        last = nc.tensor.matmul(ps_u[:, m], gram[:, k, m * P:(m + 1) * P], phi_w[:, k], start=k == 0, stop=k == KD - 1)
                last.then_inc(s["u_done"], 1)

            def v_mm(b):
                pe.wait_ge(s["u"], b + 1)
                for k in range(KD):
                    last = nc.tensor.matmul(ps_v[:], u[:, k], g_w[:, k], start=k == 0, stop=k == KD - 1)
                last.then_inc(s["v_done"], 1)

            def out_mm(b):
                pe.wait_ge(s["v"], b + 1)
                pe.wait_ge(s["theta"], b + 1)
                pe.wait_ge(s["out"], b)
                for t in range(NT):
                    last = nc.tensor.matmul(ps_out[:, t], thetaT[:, t * P:(t + 1) * P], v[:], start=True, stop=True)
                last.then_inc(s["out_done"], 1)

            transpose_x(0)
            gram_mm(0)
            theta_mm(0)
            with pe.Fori(0, B - 1) as b:
                transpose_x(b + 1)
                u_mm(b)
                gram_mm(b + 1)
                v_mm(b)
                theta_mm(b + 1)
                out_mm(b)
            u_mm(B - 1)
            v_mm(B - 1)
            out_mm(B - 1)

        @block.scalar
        def _(act):
            def copy_x(b):
                act.wait_ge(s["xT_done"], b + 1)
                nc.scalar.activation(xT[:], ps_xT[:], ACT.Copy).then_inc(s["xT"], 1)

            def copy_theta(b):
                act.wait_ge(s["theta_done"], b + 1)
                act.wait_ge(s["out_done"], b)
                nc.scalar.activation(thetaT[:], ps_theta[:], ACT.Copy).then_inc(s["theta"], 1)

            def copy_u(b):
                act.wait_ge(s["u_done"], b + 1)
                nc.scalar.activation(u[:], ps_u[:], ACT.Copy).then_inc(s["u"], 1)

            def copy_v(b):
                act.wait_ge(s["v_done"], b + 1)
                nc.scalar.activation(v[:], ps_v[:], ACT.Copy, scale=1.0 / 16).then_inc(s["v"], 1)

            copy_x(0)
            copy_theta(0)
            with act.Fori(0, B - 1) as b:
                copy_x(b + 1)
                copy_u(b)
                copy_v(b)
                copy_theta(b + 1)
            copy_u(B - 1)
            copy_v(B - 1)

        @block.vector
        def _(dve):
            def copy_gram(b):
                dve.wait_ge(s["gram_done"], b + 1)
                nc.vector.tensor_copy(gram[:], ps_gram[:]).then_inc(s["gram"], 1)

            def add_out(b):
                dve.wait_ge(s["out_done"], b + 1)
                nc.vector.tensor_tensor(res[:, b], res[:, b], ps_out[:], ALU.add).then_inc(s["out"], 1)

            copy_gram(0)
            with dve.Fori(0, B - 1) as b:
                copy_gram(b + 1)
                add_out(b)
            add_out(B - 1)




def cross_attention(nc, res, ident, half, eps, ctxT, ctx_loaded, wq_d, wk_d, wv_d, wo_d, bo_d):
    H, HD, S = 16, 64, ctxT.shape[2]
    INNER = H * HD
    MT = INNER // P
    HU = 8
    HB = 4
    UNITS = [(g, t) for g in range(H // HU) for t in range(NT)]
    U = len(UNITS)
    with ExitStack() as ctx:
        def sb(name, shape, dt=F32):
            return ctx.enter_context(nc.sbuf_tensor("B_" + name, shape, dt))

        def psum(name, shape):
            return ctx.enter_context(nc.psum_tensor("B_" + name, shape, F32))

        wq = sb("wq", [P, KD, INNER])
        wk = sb("wk", [P, INNER])
        wv = sb("wv", [P, INNER])
        wo = sb("wo", [P, MT, D])
        bo = sb("bo", [P, D])
        st = sb("st", [P, NT, 6])
        mv = sb("mv", [P, NT, 2])
        veps = sb("veps", [P, NT])
        rstd = sb("rstd", [P, NT])
        xn = sb("xn", [P, NT, D])
        xT = sb("xT", [P, KD, T])
        ctx_cur = sb("ctx_cur", [P, S])
        qT = sb("qT", [P, MT, T])
        kT = sb("kT", [P, MT, S])
        v = sb("v", [S, INNER])
        mx = sb("mx", [P, 2, HU])
        prob = sb("prob", [P, 2, HU * S])
        rsum = sb("rsum", [P, U, HU])
        rinv = sb("rinv", [P, U, HU])
        pT = sb("pT", [S, 2, HU, P])
        oT = sb("oT", [P, MT, T])
        ps_s = [psum(f"ps_s{i}", [P, 2, 512]) for i in range(2)]
        ps_p = [psum(f"ps_p{i}", [P, 512]) for i in range(2)]
        ps_m = [psum(f"ps_m{i}", [P, 512]) for i in range(2)]

        def sem(name):
            return ctx.enter_context(nc.semaphore("B_" + name))

        w_loaded, stats, stats_seen, aggr, var_eps, rstd_ready, xn_ready, resid_ready, ctx_ready = map(
            sem, "w_loaded stats stats_seen aggr var_eps rstd_ready xn_ready resid_ready ctx_ready".split())
        s_done, pT_done, av_done, q_done, k_done, v_done, xT_done, w_done = map(
            sem, "s_done pT_done av_done q_done k_done v_done xT_done w_done".split())
        exp_ready, pT_ready, oT_ready, q_ready, k_ready, v_ready, xT_ready = map(
            sem, "exp_ready pT_ready oT_ready q_ready k_ready v_ready xT_ready".split())
        max_ready, sub_ready, sum_ready, inv_ready, prob_ready, res_ready = map(
            sem, "max_ready sub_ready sum_ready inv_ready prob_ready res_ready".split())

        block = ctx.enter_context(nc.Block())

        @block.sync
        def _(sp):
            sp.dma_start(wq[:], wq_d.rearrange("(k p) n -> p k n", p=P)).then_inc(w_loaded, 16)
            sp.dma_start(wk[:], wk_d).then_inc(w_loaded, 16)
            sp.dma_start(wv[:], wv_d).then_inc(w_loaded, 16)
            sp.dma_start(wo[:], wo_d.rearrange("(k p) n -> p k n", p=P)).then_inc(w_loaded, 16)
            sp.dma_start(bo[:], bo_d.rearrange("(a n) -> a n", a=1).partition_broadcast(P)).then_inc(w_loaded, 16)

        @block.gpsimd
        def _(pool):
            def norm_scale(b):
                pool.wait_ge(aggr, b + 1)
                nc.gpsimd.tensor_tensor(veps[:], mv[:, :, 1], eps[:], ALU.add).then_inc(var_eps, 1)
                pool.wait_ge(var_eps, b + 1)
                nc.gpsimd.tensor_tensor(rstd[:], veps[:], half[:], ALU.pow).then_inc(rstd_ready, 1)

            def keep_residual(b):
                pool.wait_ge(xn_ready, b + 1)
                for t in range(NT):
                    last = nc.gpsimd.tensor_tensor(res[:, b, t], xn[:, t], bo[:], ALU.add)
                last.then_inc(resid_ready, 1)

            def stage_context(b):
                pool.wait_ge(v_done, b * 2)
                nc.gpsimd.tensor_copy(ctx_cur[:], ctxT[:, b]).then_inc(ctx_ready, 1)

            pool.wait_ge(w_loaded, 80)
            pool.wait_ge(ctx_loaded, 16)
            with pool.Fori(0, B) as b:
                stage_context(b)
                norm_scale(b)
                keep_residual(b)

        @block.tensor
        def _(pe):
            def scores(b, n):
                g, t = UNITS[n]
                for h in range(HU):
                    r = h % 2 * HD
                    m = g * HU // 2 + h // 2
                    last = nc.tensor.matmul(ps_s[n % 2][:, h % 2, h // 2 * S:(h // 2 + 1) * S],
                                            qT[r:r + HD, m, t * P:(t + 1) * P], kT[r:r + HD, m],
                                            start=True, stop=True)
                last.then_inc(s_done, 1)

            def transpose_probs(b, n):
                pe.wait_ge(prob_ready, b * U + n + 1)
                for h in range(HU):
                    if h % HB == 0 and n % 2:
                        pe.wait_ge(pT_ready, b * 2 * U + 2 * n + h // HB - 1)
                    last = nc.tensor.transpose(ps_p[h // HB][0:S, h % HB * P:(h % HB + 1) * P],
                                               prob[:, n % 2, h * S:(h + 1) * S], ident[:])
                    if h % HB == HB - 1:
                        last.then_inc(pT_done, 1)

            def values(b, n, bank):
                pe.wait_ge(pT_ready, b * 2 * U + 2 * n + 2)
                for h in range(HU):
                    head = UNITS[n][0] * HU + h
                    r = h % 2 * HD
                    last = nc.tensor.matmul(ps_m[bank][r:r + HD, h // 2 * P:(h // 2 + 1) * P], v[:, head * HD:(head + 1) * HD],
                                            pT[:, n % 2, h % 2 * HB + h // 2], start=True, stop=True)
                last.then_inc(av_done, 1)

            def transpose_x(b, bank):
                pe.wait_ge(xn_ready, b + 1)
                for k in range(KD):
                    for t in range(NT):
                        last = nc.tensor.transpose(ps_m[bank][:, k * T + t * P:k * T + (t + 1) * P],
                                                   xn[:, t, k * P:(k + 1) * P], ident[:])
                last.then_inc(xT_done, 1)

            def project_q(b, c, bank):
                for m in range(2):
                    for k in range(KD):
                        last = nc.tensor.matmul(ps_m[bank][:, m * T:(m + 1) * T], wq[:, k, (2 * c + m) * P:(2 * c + m + 1) * P],
                                                xT[:, k], start=k == 0, stop=k == KD - 1)
                last.then_inc(q_done, 1)

            def project_k(b, c, bank):
                for m in range(HB):
                    last = nc.tensor.matmul(ps_m[bank][:, m * S:(m + 1) * S], wk[:, (HB * c + m) * P:(HB * c + m + 1) * P],
                                            ctx_cur[:], start=True, stop=True)
                last.then_inc(k_done, 1)

            def project_v(b, c, bank):
                nc.tensor.matmul(ps_m[bank][0:S], ctx_cur[:], wv[:, c * 512:(c + 1) * 512],
                                 start=True, stop=True).then_inc(v_done, 1)

            def project_out(b, t, bank):
                for m in range(MT):
                    last = nc.tensor.matmul(ps_m[bank][:, 0:D], oT[:, m, t * P:(t + 1) * P], wo[:, m],
                                            start=m == 0, stop=m == MT - 1)
                last.then_inc(w_done, 1)

            def body(b, more):
                nb = b + 1
                transpose_probs(b, 0)
                pe.wait_ge(sub_ready, b * U + 1)
                scores(b, 2)
                transpose_probs(b, 1)
                pe.wait_ge(sub_ready, b * U + 2)
                scores(b, 3)
                pe.wait_ge(res_ready, b * 2)
                if more:
                    pe.wait_ge(ctx_ready, nb + 1)
                    project_k(nb, 0, 0)
                    project_k(nb, 1, 1)
                    pe.wait_ge(k_ready, b * 2 + 3)
                values(b, 0, 0)
                if more:
                    pe.wait_ge(k_ready, b * 2 + 4)
                    transpose_x(nb, 1)
                pe.wait_ge(oT_ready, b * U + 1)
                values(b, 1, 0)
                transpose_probs(b, 2)
                if more:
                    pe.wait_ge(xT_ready, b + 2)
                    project_q(nb, 0, 1)
                transpose_probs(b, 3)
                pe.wait_ge(oT_ready, b * U + 2)
                if more:
                    project_q(nb, 1, 0)
                    pe.wait_ge(q_ready, b * U + 5)
                values(b, 2, 1)
                if more:
                    pe.wait_ge(q_ready, b * U + 6)
                    project_q(nb, 2, 0)
                pe.wait_ge(oT_ready, b * U + 3)
                values(b, 3, 1)
                if more:
                    pe.wait_ge(q_ready, b * U + 7)
                    project_q(nb, 3, 0)
                pe.wait_ge(oT_ready, b * U + 4)
                if more:
                    project_v(nb, 0, 1)
                    pe.wait_ge(q_ready, b * U + 8)
                    project_v(nb, 1, 0)
                    pe.wait_ge(sub_ready, b * U + 3)
                    scores(nb, 0)
                    pe.wait_ge(v_ready, b * 2 + 3)
                project_out(b, 0, 1)
                if more:
                    pe.wait_ge(sub_ready, b * U + 4)
                    scores(nb, 1)
                    pe.wait_ge(v_ready, b * 2 + 4)
                project_out(b, 1, 0)

            pe.wait_ge(w_loaded, 80)
            pe.wait_ge(ctx_ready, 1)
            project_k(0, 0, 0)
            project_k(0, 1, 1)
            pe.wait_ge(k_ready, 2)
            transpose_x(0, 1)
            pe.wait_ge(xT_ready, 1)
            project_q(0, 0, 0)
            project_q(0, 1, 1)
            pe.wait_ge(q_ready, 2)
            project_q(0, 2, 0)
            project_q(0, 3, 1)
            pe.wait_ge(q_ready, 4)
            project_v(0, 0, 0)
            project_v(0, 1, 1)
            scores(0, 0)
            scores(0, 1)
            pe.wait_ge(v_ready, 2)
            with pe.Fori(0, B - 1) as b:
                body(b, True)
            body(B - 1, False)

        @block.scalar
        def _(act):
            def copy_pT(b, n):
                for i in range(2):
                    act.wait_ge(pT_done, b * 2 * U + 2 * n + i + 1)
                    nc.scalar.activation(pT[:, n % 2, i * HB:(i + 1) * HB], ps_p[i][0:S], ACT.Copy).then_inc(pT_ready, 1)

            def exponential(b, n):
                act.wait_ge(sub_ready, b * U + n + 1)
                nc.scalar.activation(prob[:, n % 2], prob[:, n % 2], ACT.Exp, scale=HD ** -0.5).then_inc(exp_ready, 1)

            def copy_k(b, c, bank):
                act.wait_ge(k_done, b * 2 + c + 1)
                nc.scalar.activation(kT[:, c * HB:(c + 1) * HB], ps_m[bank][:, 0:HB * S], ACT.Copy).then_inc(k_ready, 1)

            def copy_x(b, bank):
                act.wait_ge(xT_done, b + 1)
                nc.scalar.activation(xT[:], ps_m[bank][:], ACT.Copy).then_inc(xT_ready, 1)

            def copy_q(b, c, bank):
                act.wait_ge(q_done, b * 4 + c + 1)
                nc.scalar.activation(qT[:, 2 * c:2 * c + 2], ps_m[bank][:], ACT.Copy).then_inc(q_ready, 1)

            def copy_v(b, c, bank):
                act.wait_ge(v_done, b * 2 + c + 1)
                nc.scalar.activation(v[:, c * 512:(c + 1) * 512], ps_m[bank][0:S], ACT.Copy).then_inc(v_ready, 1)

            def copy_oT(b, n, bank):
                g, t = UNITS[n]
                act.wait_ge(av_done, b * U + n + 1)
                nc.scalar.activation(oT[:, g * 4:(g + 1) * 4, t * P:(t + 1) * P],
                                     ps_m[bank][:].rearrange("p (c i) -> p c i", c=4), ACT.Copy).then_inc(oT_ready, 1)

            def body(b, more):
                nb = b + 1
                copy_pT(b, 0)
                copy_pT(b, 1)
                exponential(b, 2)
                if more:
                    copy_k(nb, 0, 0)
                    copy_k(nb, 1, 1)
                exponential(b, 3)
                copy_oT(b, 0, 0)
                if more:
                    copy_x(nb, 1)
                copy_oT(b, 1, 0)
                copy_pT(b, 2)
                if more:
                    copy_q(nb, 0, 1)
                copy_pT(b, 3)
                if more:
                    copy_q(nb, 1, 0)
                copy_oT(b, 2, 1)
                if more:
                    copy_q(nb, 2, 0)
                copy_oT(b, 3, 1)
                if more:
                    copy_q(nb, 3, 0)
                    copy_v(nb, 0, 1)
                    copy_v(nb, 1, 0)
                    exponential(nb, 0)
                    exponential(nb, 1)

            copy_k(0, 0, 0)
            copy_k(0, 1, 1)
            copy_x(0, 1)
            for c in range(4):
                copy_q(0, c, c % 2)
            copy_v(0, 0, 0)
            copy_v(0, 1, 1)
            exponential(0, 0)
            exponential(0, 1)
            with act.Fori(0, B - 1) as b:
                body(b, True)
            body(B - 1, False)

        @block.vector
        def _(dve):
            def norm_stats(b):
                for t in range(NT):
                    last = nc.vector.bn_stats(st[:, t], res[:, b, t])
                last.then_inc(stats, 1)
                dve.wait_ge(stats, b + 1)
                dve.sem_inc(stats_seen)
                for t in range(NT):
                    last = nc.vector.bn_aggr(mv[:, t], st[:, t])
                last.then_inc(aggr, 1)

            def norm_apply(b):
                dve.wait_ge(rstd_ready, b + 1)
                dve.wait_ge(xT_done, b)
                dve.wait_ge(resid_ready, b)
                for t in range(NT):
                    last = nc.vector.tensor_scalar(xn[:, t], res[:, b, t], mv[:, t, 0:1], rstd[:, t:t + 1],
                                                   ALU.subtract, ALU.mult)
                last.then_inc(xn_ready, 1)

            def shift(b, n):
                sc = ps_s[n % 2][:, :, 0:HB * S].rearrange("p a (h k) -> p a h k", k=S)
                m = mx[:, n % 2]
                dve.wait_ge(s_done, b * U + n + 1)
                nc.vector.tensor_reduce(m.rearrange("p (a h) -> p a h", a=2), sc, AX.X, ALU.max).then_inc(max_ready, 1)
                dve.wait_ge(max_ready, b * U + n + 1)
                nc.vector.tensor_tensor(prob[:, n % 2].rearrange("p (a h k) -> p a h k", a=2, k=S), sc,
                                        m.rearrange("p (a h) -> p a h", a=2).unsqueeze(3).to_broadcast([P, 2, HB, S]),
                                        ALU.subtract).then_inc(sub_ready, 1)

            def normalise(b, n):
                p = prob[:, n % 2].rearrange("p (h k) -> p h k", k=S)
                dve.wait_ge(exp_ready, b * U + n + 1)
                nc.vector.tensor_reduce(rsum[:, n], p, AX.X, ALU.add).then_inc(sum_ready, 1)
                dve.wait_ge(sum_ready, b * U + n + 1)
                nc.vector.reciprocal(rinv[:, n], rsum[:, n]).then_inc(inv_ready, 1)
                dve.wait_ge(inv_ready, b * U + n + 1)
                nc.vector.tensor_tensor(p, p, rinv[:, n].unsqueeze(2).to_broadcast([P, HU, S]), ALU.mult).then_inc(prob_ready, 1)

            def add_out(b, t, bank):
                dve.wait_ge(w_done, b * 2 + t + 1)
                nc.vector.tensor_tensor(res[:, b, t], res[:, b, t], ps_m[bank][:, 0:D], ALU.add).then_inc(res_ready, 1)

            def body(b, more):
                nb = b + 1
                dve.wait_ge(pT_done, b * 2 * U + 2)
                shift(b, 2)
                if more:
                    norm_stats(nb)
                dve.wait_ge(pT_done, b * 2 * U + 4)
                shift(b, 3)
                if more:
                    norm_apply(nb)
                normalise(b, 2)
                normalise(b, 3)
                if more:
                    dve.wait_ge(pT_done, b * 2 * U + 6)
                    shift(nb, 0)
                    normalise(nb, 0)
                dve.wait_ge(resid_ready, b + 1)
                add_out(b, 0, 1)
                if more:
                    dve.wait_ge(pT_done, b * 2 * U + 8)
                    shift(nb, 1)
                    normalise(nb, 1)
                add_out(b, 1, 0)

            norm_stats(0)
            norm_apply(0)
            shift(0, 0)
            shift(0, 1)
            normalise(0, 0)
            normalise(0, 1)
            with dve.Fori(0, B - 1) as b:
                body(b, True)
            body(B - 1, False)


def expert_ffn(nc, res, ident, half, eps, idx_d, rw_d, wgu_d, bgu_d, wdn_d, bdn_d):
    E, NTOK = wgu_d.shape[0], idx_d.shape[0]
    TI = NTOK // P
    NB = NTOK // T
    with ExitStack() as ctx:
        def sb(name, shape, dt=F32):
            return ctx.enter_context(nc.sbuf_tensor("C_" + name, shape, dt))

        def psum(name, shape):
            return ctx.enter_context(nc.psum_tensor("C_" + name, shape, F32))

        idx = sb("idx", [P, TI, 2], I32)
        idxf = sb("idxf", [P, TI, 2])
        rw = sb("rw", [P, TI, E])
        expert_no = sb("expert_no", [P, E])
        hit = sb("hit", [P, 2, TI, E])
        hits = sb("hits", [P, TI, E])
        coef = sb("coef", [P, TI, E])
        coefT = sb("coefT", [E, TI, P])
        bdn = sb("bdn", [E, D])
        bgu = sb("bgu", [P, E, 2 * KD])
        wgu = sb("wgu", [P, 2, KD, 2 * D])
        wdn = sb("wdn", [P, 2, KD, D])
        st = sb("st", [P, TI, 6])
        mv = sb("mv", [P, TI, 2])
        veps = sb("veps", [P, TI])
        rstd = sb("rstd", [P, TI])
        xn = sb("xn", [P, TI, D])
        xT = sb("xT", [P, KD, NTOK])
        gate = sb("gate", [P, KD, NTOK])
        up = sb("up", [P, KD, NTOK])
        sig = sb("sig", [P, KD, NTOK])
        inter = sb("inter", [P, KD, NTOK])
        ps_h = [psum(f"ps_h{i}", [P, NTOK]) for i in range(2 * KD)]
        ps_d = [psum(f"ps_d{i}", [P, 2, D]) for i in range(TI // 2)]

        def sem(name):
            return ctx.enter_context(nc.semaphore("C_" + name))

        in_loaded, w_loaded0, w_loaded1, step, stats, aggr, var_eps, rstd_ready, xn_ready = map(
            sem, "in_loaded w_loaded0 w_loaded1 step stats aggr var_eps rstd_ready xn_ready".split())
        xT_done, xT_ready, coef_ready, cT_done, cT_ready, bias_done, acc_init = map(
            sem, "xT_done xT_ready coef_ready cT_done cT_ready bias_done acc_init".split())
        h_done, h_read, sig_ready, inter_step, inter_ready, d_done, d_read = map(
            sem, "h_done h_read sig_ready inter_step inter_ready d_done d_read".split())
        w_loaded = [w_loaded0, w_loaded1]

        block = ctx.enter_context(nc.Block())

        @block.sync
        def _(sp):
            sp.dma_start(idx[:], idx_d.rearrange("(t p) k -> p t k", p=P)).then_inc(in_loaded, 16)
            sp.dma_start(rw[:], rw_d.rearrange("(t p) e -> p t e", p=P)).then_inc(in_loaded, 16)
            sp.dma_start(bdn[:], bdn_d).then_inc(in_loaded, 16)
            sp.dma_start(bgu[:], bgu_d).then_inc(in_loaded, 16)

            def load(e, u):
                sp.dma_start(wgu[:, u], wgu_d[e].rearrange("(k p) n -> p k n", p=P)).then_inc(w_loaded[u], 16)
                sp.dma_start(wdn[:, u], wdn_d[e].rearrange("(k p) n -> p k n", p=P)).then_inc(w_loaded[u], 16)
            load(0, 0)
            load(1, 1)
            with sp.Fori(0, E // 2 - 1) as j:
                for u in range(2):
                    sp.wait_ge(d_done, j * 2 * TI + (u + 1) * TI)
                    load(j * 2 + (2 + u), u)

        @block.gpsimd
        def _(pool):
            nc.gpsimd.iota(hits[:, 0].bitcast(I32), [[1, E]], base=0, channel_multiplier=0).then_inc(step, 1)
            pool.wait_ge(step, 1)
            nc.gpsimd.tensor_copy(expert_no[:], hits[:, 0].bitcast(I32)).then_inc(step, 1)
            pool.wait_ge(aggr, 1)
            nc.gpsimd.tensor_scalar(veps[:], mv[:, :, 1], 1e-5, None, ALU.add).then_inc(var_eps, 1)
            pool.wait_ge(var_eps, 1)
            for i in range(TI // NT):
                last = nc.gpsimd.tensor_tensor(rstd[:, i * NT:(i + 1) * NT], veps[:, i * NT:(i + 1) * NT], half[:], ALU.pow)
            last.then_inc(rstd_ready, 1)

        @block.tensor
        def _(pe):
            pe.wait_ge(xn_ready, 1)
            for k in range(KD):
                for t in range(TI):
                    last = nc.tensor.transpose(ps_h[k][:, t * P:(t + 1) * P], xn[:, t, k * P:(k + 1) * P], ident[:])
            last.then_inc(xT_done, 1)
            pe.wait_ge(coef_ready, 1)
            for t in range(TI):
                last = nc.tensor.transpose(ps_h[2][0:E, t * P:(t + 1) * P], coef[:, t], ident[:])
            last.then_inc(cT_done, 1)
            pe.wait_ge(cT_ready, 1)
            for t in range(TI):
                last = nc.tensor.matmul(ps_d[t // 2][:, t % 2], coefT[:, t], bdn[:], start=True, stop=True)
            last.then_inc(bias_done, 1)
            pe.wait_ge(xT_ready, 1)

            def hidden(e, u, first=False):
                for m in range(2 * KD):
                    if not first:
                        pe.wait_ge(h_read, e * 2 * KD + (m + 1 - 2 * KD))
                    for k in range(KD):
                        last = nc.tensor.matmul(ps_h[m][:], wgu[:, u, k, m * P:(m + 1) * P], xT[:, k], start=k == 0, stop=k == KD - 1)
                    last.then_inc(h_done, 1)

            def down(e, u, first=False):
                pe.wait_ge(inter_ready, e + 1)
                for t in range(TI):
                    if t % 2 == 0 and not first:
                        pe.wait_ge(d_read, e * TI + (t + 2 - TI))
                    for k in range(KD):
                        last = nc.tensor.matmul(ps_d[t // 2][:, t % 2], inter[:, k, t * P:(t + 1) * P], wdn[:, u, k],
                                                start=k == 0, stop=k == KD - 1)
                    last.then_inc(d_done, 1)

            pe.wait_ge(w_loaded[0], 32)
            hidden(0, 0, first=True)
            pe.wait_ge(acc_init, 1)
            pe.wait_ge(w_loaded[1], 32)
            hidden(1, 1)
            down(0, 0, first=True)
            with pe.Fori(0, E // 2 - 1) as j:
                pe.wait_ge(w_loaded[0], j * 32 + 64)
                hidden(j * 2 + 2, 0)
                down(j * 2 + 1, 1)
                pe.wait_ge(w_loaded[1], j * 32 + 64)
                hidden(j * 2 + 3, 1)
                down(j * 2 + 2, 0)
            down(E - 1, 1)

        @block.scalar
        def _(act):
            act.wait_ge(xT_done, 1)
            for k in range(KD):
                last = nc.scalar.activation(xT[:, k], ps_h[k][:], ACT.Copy)
            last.then_inc(xT_ready, 1)
            act.wait_ge(cT_done, 1)
            nc.scalar.activation(coefT[:], ps_h[2][0:E].rearrange("e (t p) -> e t p", p=P), ACT.Copy).then_inc(cT_ready, 1)
            with act.Fori(0, E) as e:
                act.wait_ge(h_read, e * 2 * KD + KD)
                nc.scalar.activation(sig[:], gate[:], ACT.Sigmoid, scale=1.702).then_inc(sig_ready, 1)

        @block.vector
        def _(dve):
            for t in range(TI):
                last = nc.vector.bn_stats(st[:, t], res[:, t // NT, t % NT])
            last.then_inc(stats, 1)
            dve.wait_ge(stats, 1)
            for t in range(TI):
                last = nc.vector.bn_aggr(mv[:, t], st[:, t])
            last.then_inc(aggr, 1)
            dve.wait_ge(rstd_ready, 1)
            for t in range(TI):
                last = nc.vector.tensor_scalar(xn[:, t], res[:, t // NT, t % NT], mv[:, t, 0:1], rstd[:, t:t + 1],
                                               ALU.subtract, ALU.mult)
            last.then_inc(xn_ready, 1)
            dve.wait_ge(in_loaded, 64)
            nc.vector.tensor_copy(idxf[:], idx[:]).then_inc(step, 1)
            dve.wait_ge(step, 3)
            for k in range(2):
                last = nc.vector.tensor_tensor(hit[:, k], idxf[:, :, k].unsqueeze(2).to_broadcast([P, TI, E]),
                                               expert_no[:].unsqueeze(1).to_broadcast([P, TI, E]), ALU.is_equal)
            last.then_inc(step, 1)
            dve.wait_ge(step, 4)
            nc.vector.tensor_tensor(hits[:], hit[:, 0], hit[:, 1], ALU.add).then_inc(step, 1)
            dve.wait_ge(step, 5)
            nc.vector.tensor_tensor(coef[:], hits[:], rw[:], ALU.mult).then_inc(coef_ready, 1)
            dve.wait_ge(bias_done, 1)
            dve.wait_ge(xn_ready, 1)
            for i in range(NB):
                last = nc.vector.tensor_tensor(res[:, i], xn[:, i * NT:(i + 1) * NT], ps_d[i][:], ALU.add)
            last.then_inc(acc_init, 1)
            dve.wait_ge(acc_init, 1)

            def swiglu(e):
                for m in range(2 * KD):
                    if m == KD:
                        dve.wait_ge(inter_ready, e)
                    dve.wait_ge(h_done, e * 2 * KD + m + 1)
                    nc.vector.tensor_scalar((gate if m < KD else up)[:, m % KD], ps_h[m][:], bgu[:, e, m:m + 1], 7.0,
                                            ALU.add, ALU.min).then_inc(h_read, 1)
                dve.wait_ge(h_read, e * 2 * KD + 2 * KD)
                nc.vector.tensor_scalar(up[:], up[:], -7.0, 1.0, ALU.max, ALU.add).then_inc(inter_step, 1)
                dve.wait_ge(inter_step, e * 2 + 1)
                nc.vector.tensor_tensor(up[:], up[:], gate[:], ALU.mult).then_inc(inter_step, 1)
                dve.wait_ge(inter_step, e * 2 + 2)
                dve.wait_ge(sig_ready, e + 1)
                dve.wait_ge(d_done, e * TI)
                nc.vector.tensor_tensor(inter[:], up[:], sig[:], ALU.mult).then_inc(inter_ready, 1)

            def accumulate(e):
                for t in range(TI):
                    r = res[:, t // NT, t % NT]
                    if t == 0:
                        dve.wait_ge(d_read, e * TI)
                    dve.wait_ge(d_done, e * TI + 2 * (t // 2) + 2)
                    nc.vector.scalar_tensor_tensor(r, ps_d[t // 2][:, t % 2], coef[:, t, bass.ds(e, 1)], r,
                                                   ALU.mult, ALU.add).then_inc(d_read, 1)

            swiglu(0)
            with dve.Fori(0, E - 1) as e:
                swiglu(e + 1)
                accumulate(e)
            accumulate(E - 1)


RET_H, RET_D = 16, 16
RET_U = 4


def retention_head(p):
    r, rg, half, e = p // 8, p // 4 % 2, p // 2 % 2, p % 2
    return half * 8 + (2 * r + rg) * 2 + e


def gated_retention(nc, res, ident, half, eps, x_w, const):
    H, HD, U = RET_H, RET_D, RET_U
    HT = H // 2
    with ExitStack() as ctx:
        def sb(name, shape, dt=F32):
            return ctx.enter_context(nc.sbuf_tensor("D_" + name, shape, dt))

        def psum(name, shape):
            return ctx.enter_context(nc.psum_tensor("D_" + name, shape, F32))

        wqk = sb("wqk", [P, KD, 2 * D])
        wvg = sb("wvg", [P, KD, 2 * D])
        wgt = sb("wgt", [P, KD, H])
        wo = sb("wo", [P, KD, D])
        upto = sb("upto", [P, P])
        after = sb("after", [P, P])
        head_mask = sb("head_mask", [P, 2])
        block_mask = sb("block_mask", [P, P])
        sel = sb("sel", [P, H, P], BF16)
        nsel = sb("nsel", [P, H, P], BF16)
        st = sb("st", [P, NT, 6])
        mv = sb("mv", [P, NT, 2])
        veps = sb("veps", [P, NT])
        r1 = sb("r1", [P, NT])
        r1sq = sb("r1sq", [P, NT])
        var1 = sb("var1", [P, NT])
        var1_eps = sb("var1_eps", [P, NT])
        r2 = sb("r2", [P, NT])
        rstd = sb("rstd", [P, NT])
        xn = sb("xn", [P, NT, D])
        xT = sb("xT", [P, KD, T])
        qk = sb("qk", [P, NT, 2, D])
        v_raw = sb("v_raw", [P, NT, D])
        g_raw = sb("g_raw", [P, NT, D])
        v = sb("v", [P, NT, D])
        sq = sb("sq", [P, 3, NT, D])
        ssq = sb("ssq", [P, 3, NT])
        msq = sb("msq", [P, 3, NT])
        half6 = sb("half6", [P, 3, NT])
        half32 = sb("half32", [P, NT, H])
        rms = sb("rms", [P, 3, NT])
        za = sb("za", [P, NT, H])
        zm = sb("zm", [P, NT, H])
        ze = sb("ze", [P, NT, H])
        zl = sb("zl", [P, NT, H])
        ld = sb("ld", [P, NT, 4, 32])
        dec = sb("dec", [P, 2, H])
        F = sb("F", [P, NT, P], BF16)
        Fr = sb("Fr", [P, NT, P])
        q2T = sb("q2T", [P, NT, 2, 2, P])
        kT = sb("kT", [P, NT, 2, P])
        qd = sb("qd", [P, D])
        kd = sb("kd", [P, D])
        qdT = sb("qdT", [P, 2, P])
        state = sb("state", [P, 2, P])
        dexp = sb("dexp", [P, 2, HT * P])
        att = sb("att", [P, 2, HT, P])
        o_raw = sb("o_raw", [P, NT, D])
        osq = sb("osq", [P, NT, H, HD])
        oss = sb("oss", [P, NT, H])
        oms = sb("oms", [P, NT, H])
        orms = sb("orms", [P, NT, H])
        eg = sb("eg", [P, NT, D])
        sg = sb("sg", [P, NT, D])
        y = sb("y", [P, NT, D])
        yT = sb("yT", [P, KD, T])
        ps_e = psum("ps_e", [P, 2, 512])
        ps_s = psum("ps_s", [P, 2, 512])
        ps_f = [psum(f"ps_f{i}", [P, 512]) for i in range(2)]
        ps_c = psum("ps_c", [P, 512])
        ps_o = psum("ps_o", [P, NT, D])
        c_bc, c_bcT, c_z = ps_c[:, 0:2 * H], ps_c[:, 64:64 + T], ps_c[:, 384:384 + NT * H]

        def sem(name):
            return ctx.enter_context(nc.semaphore("D_" + name))

        w_loaded, set_ready, stats, seen, aggr, var_eps, rstd_ready, xn_ready, resid_ready = map(
            sem, "w_loaded set_ready stats seen aggr var_eps rstd_ready xn_ready resid_ready".split())
        xT_done, qk_done, vg_done, z_done, bc_done, bcT_done, qkT_done, qdT_done = map(
            sem, "xT_done qk_done vg_done z_done bc_done bcT_done qkT_done qdT_done".split())
        e_done, s_done, st_done, av_done, yT_done, w_done = map(
            sem, "e_done s_done st_done av_done yT_done w_done".split())
        xT_ready, qk_raw, vg_raw, ssq_ready, ze_ready, zl_ready, dec_ready, qkT_ready, qdT_ready = map(
            sem, "xT_ready qk_raw vg_raw ssq_ready ze_ready zl_ready dec_ready qkT_ready qdT_ready".split())
        exp_ready, osq_ready, o_ready, eg_ready, yT_ready, norm_step = map(
            sem, "exp_ready osq_ready o_ready eg_ready yT_ready norm_step".split())
        z_step, z_ready, ld_ready, f_step, f_ready, qk_ready, v_ready, att_raw, state_ready, oss_ready = map(
            sem, "z_step z_ready ld_ready f_step f_ready qk_ready v_ready att_raw state_ready oss_ready".split())
        y_step, y_ready, sg_step, sg_ready, res_ready = map(sem, "y_step y_ready sg_step sg_ready res_ready".split())
        msq_ready, rms_ready, kqd_ready, att_ready, oms_ready, orms_ready = map(
            sem, "msq_ready rms_ready kqd_ready att_ready oms_ready orms_ready".split())

        block = ctx.enter_context(nc.Block())

        def steps(engine, body):
            body(0, prev=False, nxt=True, nxt2=True)
            with engine.Fori(1, B - 2) as b:
                body(b, prev=True, nxt=True, nxt2=True)
            body(B - 2, prev=True, nxt=True, nxt2=False)
            body(B - 1, prev=True, nxt=False, nxt2=False)

        @block.sync
        def _(sp):
            for dst, name in ((wqk, "wqk"), (wvg, "wvg"), (wgt, "wgt"), (wo, "wo")):
                sp.dma_start(dst[:], x_w[name].rearrange("(k p) n -> p k n", p=P)).then_inc(w_loaded, 16)
            for dst, name in ((upto, "upto"), (after, "after"), (head_mask, "head_mask"), (block_mask, "block_mask"),
                              (sel, "sel"), (nsel, "nsel")):
                sp.dma_start(dst[:], const[name]).then_inc(w_loaded, 16)
        LOADED = 160

        @block.gpsimd
        def _(pool):
            def norm_scale(b, double):
                pool.wait_ge(aggr, b + 1)
                nc.gpsimd.tensor_tensor(veps[:], mv[:, :, 1], eps[:], ALU.add).then_inc(var_eps, 1)
                pool.wait_ge(var_eps, b + 1)
                if not double:
                    nc.gpsimd.tensor_tensor(rstd[:], veps[:], half[:], ALU.pow).then_inc(rstd_ready, 1)
                    return
                n = (b - 2) * 5
                nc.gpsimd.tensor_tensor(r1[:], veps[:], half[:], ALU.pow).then_inc(norm_step, 1)
                pool.wait_ge(norm_step, n + 1)
                nc.gpsimd.tensor_tensor(r1sq[:], r1[:], r1[:], ALU.mult).then_inc(norm_step, 1)
                pool.wait_ge(norm_step, n + 2)
                nc.gpsimd.tensor_tensor(var1[:], r1sq[:], mv[:, :, 1], ALU.mult).then_inc(norm_step, 1)
                pool.wait_ge(norm_step, n + 3)
                nc.gpsimd.tensor_tensor(var1_eps[:], var1[:], eps[:], ALU.add).then_inc(norm_step, 1)
                pool.wait_ge(norm_step, n + 4)
                nc.gpsimd.tensor_tensor(r2[:], var1_eps[:], half[:], ALU.pow).then_inc(norm_step, 1)
                pool.wait_ge(norm_step, n + 5)
                nc.gpsimd.tensor_tensor(rstd[:], r1[:], r2[:], ALU.mult).then_inc(rstd_ready, 1)

            def keep_residual(b):
                pool.wait_ge(xn_ready, b + 1)
                nc.gpsimd.tensor_copy(res[:, b], xn[:]).then_inc(resid_ready, 1)

            def qkv_scale(b):
                pool.wait_ge(ssq_ready, b * 6 + 6)
                pool.sem_inc(seen)
                nc.gpsimd.tensor_scalar(msq[:], ssq[:], 1.0 / D, 1e-6, ALU.mult, ALU.add).then_inc(msq_ready, 1)
                pool.wait_ge(msq_ready, b + 1)
                nc.gpsimd.tensor_tensor(rms[:], msq[:], half6[:], ALU.pow).then_inc(rms_ready, 1)

            def decayed(b):
                pool.wait_ge(qk_ready, b + 1)
                pool.wait_ge(dec_ready, b + 1)
                for dst, c, w, n in ((qd, 1, 0, 0), (kd, 0, 1, 1)):
                    last = nc.gpsimd.tensor_tensor(dst[:].rearrange("p (h d) -> p h d", d=HD),
                                                   qk[:, c, w].rearrange("p (h d) -> p h d", d=HD),
                                                   dec[:, n].unsqueeze(2).to_broadcast([P, H, HD]), ALU.mult)
                last.then_inc(kqd_ready, 1)

            def causal(b, n):
                pool.wait_ge(att_raw, b * U + n + 1)
                pool.sem_inc(seen)
                nc.gpsimd.affine_select(out=att[:, n % 2], in_=att[:, n % 2], compare_op=ALU.is_ge, fill=0.0, base=0,
                                        pattern=[[0, HT], [1, P]], channel_multiplier=-1).then_inc(att_ready, 1)

            def out_scale(b):
                pool.wait_ge(oss_ready, b + 1)
                pool.sem_inc(seen)
                nc.gpsimd.tensor_scalar(oms[:], oss[:], 1.0 / HD, 1e-6, ALU.mult, ALU.add).then_inc(oms_ready, 1)
                pool.wait_ge(oms_ready, b + 1)
                nc.gpsimd.tensor_tensor(orms[:], oms[:], half32[:], ALU.pow).then_inc(orms_ready, 1)

            def body(b, prev, nxt, nxt2):
                if prev:
                    out_scale(b - 1)
                causal(b, 0)
                if nxt2:
                    norm_scale(b + 2, True)
                causal(b, 1)
                if nxt2:
                    keep_residual(b + 2)
                causal(b, 2)
                if nxt:
                    qkv_scale(b + 1)
                causal(b, 3)
                if nxt:
                    pool.wait_ge(st_done, b + 1)
                    decayed(b + 1)

            for i in range(3):
                nc.gpsimd.memset(half6[:, i], -0.5)
            nc.gpsimd.memset(half32[:], -0.5)
            nc.gpsimd.memset(ld[:], 0.0).then_inc(set_ready, 1)
            for b in range(2):
                norm_scale(b, False)
                keep_residual(b)
            qkv_scale(0)
            decayed(0)
            steps(pool, body)
            out_scale(B - 1)

        @block.tensor
        def _(pe):
            def transpose_x(b):
                pe.wait_ge(xn_ready, b + 1)
                for k in range(KD):
                    for t in range(NT):
                        last = nc.tensor.transpose(ps_f[0][:, k * T + t * P:k * T + (t + 1) * P],
                                                   xn[:, t, k * P:(k + 1) * P], ident[:])
                last.then_inc(xT_done, 1)

            def project(b, t, w, bank, done):
                for k in range(KD):
                    last = nc.tensor.matmul(ps_f[bank][:], xT[:, k, t * P:(t + 1) * P], w[:, k], start=k == 0, stop=k == KD - 1)
                last.then_inc(done, 1)

            def gates(b):
                for t in range(NT):
                    for k in range(KD):
                        last = nc.tensor.matmul(c_z[:, t * H:(t + 1) * H], xT[:, k, t * P:(t + 1) * P], wgt[:, k],
                                                start=k == 0, stop=k == KD - 1)
                last.then_inc(z_done, 1)

            def running_sums(b):
                pe.wait_ge(ld_ready, b + 1)
                nc.tensor.matmul(c_bc[:, 0:H], upto[:], ld[:, 1, 0, 0:H], start=True, stop=True)
                nc.tensor.matmul(c_bc[:, H:2 * H], after[:], ld[:, 0, 0, 0:H], start=True, stop=True).then_inc(bc_done, 1)
                for c in range(NT):
                    last = nc.tensor.matmul(c_bcT[:, c * P:(c + 1) * P], ld[:, c].rearrange("p s h -> p (s h)"), upto[:],
                                            start=True, stop=True)
                last.then_inc(bcT_done, 1)

            def transpose_qk(b, c, bank):
                pe.wait_ge(qk_ready, b + 1)
                for w in range(2):
                    for hf in range(2):
                        last = nc.tensor.transpose(ps_f[bank][:, (w * 2 + hf) * P:(w * 2 + hf + 1) * P],
                                                   qk[:, c, w, hf * P:(hf + 1) * P], ident[:])
                last.then_inc(qkT_done, 1)

            def transpose_qd(b):
                pe.wait_ge(kqd_ready, b + 1)
                for hf in range(2):
                    last = nc.tensor.transpose(ps_f[1][:, hf * P:(hf + 1) * P], qd[:, hf * P:(hf + 1) * P], ident[:])
                last.then_inc(qdT_done, 1)

            def exponents(b, n):
                c, r = n // 2, n % 2
                for bank in range(2):
                    pl = r * HT + bank * 4
                    nc.tensor.matmul(ps_e[:, bank], F[:, c], nsel[:, pl:pl + 4], start=True, stop=False)
                    for i in range(4):
                        last = nc.tensor.matmul(ps_e[:, bank, i * P:(i + 1) * P], sel[:, pl + i], F[:, c], start=False, stop=i == 3)
                last.then_inc(e_done, 1)

            def products(b, n):
                c, r = n // 2, n % 2
                for bank in range(2):
                    rows = slice(32 * (2 * r + bank), 32 * (2 * r + bank) + 32)
                    for hf in range(2):
                        last = nc.tensor.matmul(ps_s[:, bank, hf * T:(hf + 1) * T], kT[rows, c, hf],
                                                q2T[rows, c, hf].rearrange("p e i -> p (e i)"), start=True, stop=True)
                last.then_inc(s_done, 1)

            def values(b, n):
                c, r = n // 2, n % 2
                pe.wait_ge(att_ready, b * U + n + 1)
                for i in range(HT):
                    h = retention_head(r * HT + i)
                    last = nc.tensor.matmul(ps_o[:, c, h * HD:(h + 1) * HD], att[:, n % 2, i], v[:, c, h * HD:(h + 1) * HD],
                                            start=n == 0 and i == 0, stop=n == U - 1 and i == HT - 1, skip_group_check=True)
                last.then_inc(av_done, 1)

            def state_update(b):
                for hf in range(2):
                    last = nc.tensor.matmul(ps_f[0][:, hf * P:(hf + 1) * P], kd[:, hf * P:(hf + 1) * P], v[:, 0, hf * P:(hf + 1) * P],
                                            start=True, stop=True)
                last.then_inc(st_done, 1)

            def cross(b):
                pe.wait_ge(state_ready, b + 1)
                for hf in range(2):
                    nc.tensor.matmul(ps_o[:, 1, hf * P:(hf + 1) * P], qdT[:, hf], state[:, hf], start=False, stop=False,
                                     skip_group_check=True)

            def transpose_y(b):
                pe.wait_ge(y_ready, b + 1)
                for k in range(KD):
                    for t in range(NT):
                        last = nc.tensor.transpose(ps_f[0][:, k * T + t * P:k * T + (t + 1) * P],
                                                   y[:, t, k * P:(k + 1) * P], ident[:])
                last.then_inc(yT_done, 1)

            def project_out(b):
                pe.wait_ge(yT_ready, b + 1)
                for t in range(NT):
                    for k in range(KD):
                        last = nc.tensor.matmul(ps_f[0][:, t * D:(t + 1) * D], yT[:, k, t * P:(t + 1) * P], wo[:, k],
                                                start=k == 0, stop=k == KD - 1)
                last.then_inc(w_done, 1)

            def body(b, prev, nxt, nxt2):
                nb = b + 1
                pe.wait_ge(f_ready, b + 1)
                exponents(b, 0)
                pe.wait_ge(qkT_ready, b * 2 + 2)
                products(b, 0)
                if nxt:
                    transpose_x(nb)
                pe.wait_ge(exp_ready, b * U + 1)
                exponents(b, 1)
                if nxt:
                    pe.wait_ge(xT_ready, nb + 1)
                    project(nb, 0, wqk, 0, qk_done)
                    pe.wait_ge(dec_ready, b + 1)
                    gates(nb)
                pe.wait_ge(att_raw, b * U + 1)
                products(b, 1)
                pe.wait_ge(qdT_ready, b + 1)
                if nxt:
                    project(nb, 1, wqk, 1, qk_done)
                pe.wait_ge(v_ready, b + 1)
                if prev:
                    pe.wait_ge(o_ready, b)
                values(b, 0)
                pe.wait_ge(exp_ready, b * U + 2)
                exponents(b, 2)
                if nxt:
                    pe.wait_ge(qk_raw, b * 2 + 3)
                    project(nb, 0, wvg, 0, vg_done)
                pe.wait_ge(att_raw, b * U + 2)
                products(b, 2)
                values(b, 1)
                if nxt:
                    pe.wait_ge(qk_raw, b * 2 + 4)
                    project(nb, 1, wvg, 1, vg_done)
                    running_sums(nb)
                if prev:
                    if nxt:
                        pe.wait_ge(vg_raw, b * 2 + 3)
                    transpose_y(b - 1)
                pe.wait_ge(exp_ready, b * U + 3)
                exponents(b, 3)
                pe.wait_ge(att_raw, b * U + 3)
                products(b, 3)
                if prev:
                    project_out(b - 1)
                values(b, 2)
                pe.wait_ge(kqd_ready, b + 1)
                if prev:
                    pe.wait_ge(res_ready, b)
                elif nxt:
                    pe.wait_ge(vg_raw, b * 2 + 3)
                state_update(b)
                if nxt:
                    pe.wait_ge(vg_raw, b * 2 + 4)
                    transpose_qk(nb, 0, 1)
                cross(b)
                values(b, 3)
                if nxt:
                    transpose_qk(nb, 1, 0)
                    pe.wait_ge(qkT_ready, b * 2 + 3)
                    transpose_qd(nb)

            pe.wait_ge(w_loaded, LOADED)
            pe.wait_ge(set_ready, 1)
            transpose_x(0)
            pe.wait_ge(xT_ready, 1)
            project(0, 0, wqk, 0, qk_done)
            project(0, 1, wqk, 1, qk_done)
            pe.wait_ge(qk_raw, 1)
            project(0, 0, wvg, 0, vg_done)
            pe.wait_ge(qk_raw, 2)
            project(0, 1, wvg, 1, vg_done)
            gates(0)
            running_sums(0)
            pe.wait_ge(vg_raw, 2)
            transpose_qk(0, 0, 1)
            transpose_qk(0, 1, 0)
            pe.wait_ge(qkT_ready, 1)
            transpose_qd(0)
            steps(pe, body)
            transpose_y(B - 1)
            project_out(B - 1)

        @block.scalar
        def _(act):
            def exponential(b, n):
                act.wait_ge(e_done, b * U + n + 1)
                nc.scalar.activation(dexp[:, n % 2], ps_e[:].rearrange("p a n -> p (a n)"), ACT.Exp).then_inc(exp_ready, 1)

            def copy_x(b):
                act.wait_ge(xT_done, b + 1)
                nc.scalar.activation(xT[:].rearrange("p k t -> p (k t)"), ps_f[0][:], ACT.Copy).then_inc(xT_ready, 1)

            def copy_qk(b, t):
                act.wait_ge(qk_done, b * 2 + t + 1)
                nc.scalar.activation(qk[:, t].rearrange("p w d -> p (w d)"), ps_f[t][:], ACT.Copy).then_inc(qk_raw, 1)

            def squares_qk(b, t):
                act.wait_ge(qk_raw, b * 2 + t + 1)
                for w in range(2):
                    nc.scalar.activation(sq[:, w, t], qk[:, t, w], ACT.Square, accum_out=ssq[:, w, t:t + 1]).then_inc(ssq_ready, 1)

            def copy_vg(b, t):
                act.wait_ge(vg_done, b * 2 + t + 1)
                nc.scalar.activation(v_raw[:, t], ps_f[t][:, 0:D], ACT.Copy)
                nc.scalar.activation(g_raw[:, t], ps_f[t][:, D:2 * D], ACT.Copy).then_inc(vg_raw, 1)

            def squares_v(b, t):
                act.wait_ge(vg_raw, b * 2 + t + 1)
                nc.scalar.activation(sq[:, 2, t], v_raw[:, t], ACT.Square, accum_out=ssq[:, 2, t:t + 1]).then_inc(ssq_ready, 1)

            def softplus(b):
                act.wait_ge(z_ready, b + 1)
                nc.scalar.activation(ze[:], za[:], ACT.Exp, scale=-1.0).then_inc(ze_ready, 1)
                act.wait_ge(ze_ready, b + 1)
                nc.scalar.activation(zl[:], ze[:], ACT.Ln, bias=1.0).then_inc(zl_ready, 1)

            def border_decay(b):
                act.wait_ge(bcT_done, b + 1)
                nc.scalar.activation(dec[:].rearrange("p n h -> p (n h)"), c_bc, ACT.Exp).then_inc(dec_ready, 1)

            def copy_qkT(b, c, bank):
                act.wait_ge(qkT_done, b * 2 + c + 1)
                ps = ps_f[bank][:].rearrange("p (w f i) -> p w f i", w=2, f=2)
                for e in range(2):
                    nc.scalar.activation(q2T[:, c, :, e], ps[:, 0], ACT.Copy, scale=head_mask[:, e:e + 1])
                nc.scalar.activation(kT[:, c], ps[:, 1], ACT.Copy).then_inc(qkT_ready, 1)

            def copy_qdT(b):
                act.wait_ge(qdT_done, b + 1)
                nc.scalar.activation(qdT[:].rearrange("p f i -> p (f i)"), ps_f[1][:, 0:2 * P], ACT.Copy).then_inc(qdT_ready, 1)

            def out_squares(b):
                act.wait_ge(av_done, b * U + U)
                nc.scalar.activation(osq[:].rearrange("p t h d -> p (t h d)"), ps_o[:].rearrange("p t d -> p (t d)"),
                                     ACT.Square).then_inc(osq_ready, 1)

            def copy_o(b):
                nc.scalar.activation(o_raw[:].rearrange("p t d -> p (t d)"), ps_o[:].rearrange("p t d -> p (t d)"),
                                     ACT.Copy).then_inc(o_ready, 1)

            def gate_exp(b):
                nc.scalar.activation(eg[:], g_raw[:], ACT.Exp, scale=-1.0).then_inc(eg_ready, 1)

            def copy_y(b):
                act.wait_ge(yT_done, b + 1)
                nc.scalar.activation(yT[:].rearrange("p k t -> p (k t)"), ps_f[0][:], ACT.Copy).then_inc(yT_ready, 1)

            def body(b, prev, nxt, nxt2):
                nb = b + 1
                if prev:
                    out_squares(b - 1)
                    copy_o(b - 1)
                exponential(b, 0)
                if nxt:
                    copy_x(nb)
                exponential(b, 1)
                act.wait_ge(vg_raw, b * 2 + 2)
                gate_exp(b)
                if nxt:
                    act.wait_ge(kqd_ready, b + 1)
                    copy_qk(nb, 0)
                    squares_qk(nb, 0)
                    copy_qk(nb, 1)
                    softplus(nb)
                act.wait_ge(att_raw, b * U + 1)
                exponential(b, 2)
                if nxt:
                    squares_qk(nb, 1)
                    act.wait_ge(sg_ready, b + 1)
                    copy_vg(nb, 0)
                    squares_v(nb, 0)
                    copy_vg(nb, 1)
                    squares_v(nb, 1)
                    border_decay(nb)
                if prev:
                    copy_y(b - 1)
                act.wait_ge(att_raw, b * U + 2)
                exponential(b, 3)
                if nxt:
                    copy_qkT(nb, 0, 1)
                    copy_qkT(nb, 1, 0)
                    copy_qdT(nb)

            act.wait_ge(w_loaded, LOADED)
            copy_x(0)
            for t in range(NT):
                copy_qk(0, t)
                squares_qk(0, t)
            for t in range(NT):
                copy_vg(0, t)
                squares_v(0, t)
            softplus(0)
            border_decay(0)
            copy_qkT(0, 0, 1)
            copy_qkT(0, 1, 0)
            copy_qdT(0)
            steps(act, body)
            out_squares(B - 1)
            copy_o(B - 1)
            copy_y(B - 1)

        @block.vector
        def _(dve):
            def norm_stats(b):
                for t in range(NT):
                    last = nc.vector.bn_stats(st[:, t], res[:, b, t])
                last.then_inc(stats, 1)
                dve.wait_ge(stats, b + 1)
                dve.sem_inc(seen)
                for t in range(NT):
                    last = nc.vector.bn_aggr(mv[:, t], st[:, t])
                last.then_inc(aggr, 1)

            def norm_apply(b):
                dve.wait_ge(rstd_ready, b + 1)
                dve.wait_ge(xT_done, b)
                dve.wait_ge(resid_ready, b)
                for t in range(NT):
                    last = nc.vector.tensor_scalar(xn[:, t], res[:, b, t], mv[:, t, 0:1], rstd[:, t:t + 1], ALU.subtract, ALU.mult)
                last.then_inc(xn_ready, 1)

            def scale_qk(b):
                dve.wait_ge(rms_ready, b + 1)
                for t in range(NT):
                    for w in range(2):
                        last = nc.vector.tensor_scalar(qk[:, t, w], qk[:, t, w], rms[:, w, t:t + 1], None, ALU.mult)
                last.then_inc(qk_ready, 1)

            def scale_v(b):
                for t in range(NT):
                    last = nc.vector.tensor_scalar(v[:, t], v_raw[:, t], rms[:, 2, t:t + 1], None, ALU.mult)
                last.then_inc(v_ready, 1)

            def gate_parts(b):
                dve.wait_ge(z_done, b + 1)
                nc.vector.tensor_scalar(zm[:].rearrange("p t h -> p (t h)"), c_z, 0.0, None, ALU.min).then_inc(z_step, 1)
                dve.wait_ge(z_step, b + 1)
                nc.vector.scalar_tensor_tensor(za[:].rearrange("p t h -> p (t h)"), c_z, 0.0, zm[:].rearrange("p t h -> p (t h)"),
                                               ALU.max, ALU.subtract).then_inc(z_ready, 1)

            def log_decay(b):
                dve.wait_ge(zl_ready, b + 1)
                dve.wait_ge(z_ready, b + 1)
                for s in (0, 2, 3):
                    last = nc.vector.tensor_tensor(ld[:, :, s, 0:H], zm[:], zl[:], ALU.subtract)
                last.then_inc(ld_ready, 1)

            def split_sums(b):
                f, fr = F[:].rearrange("p c i -> p (c i)"), Fr[:].rearrange("p c i -> p (c i)")
                dve.wait_ge(dec_ready, b + 1)
                dve.wait_ge(bcT_done, b + 1)
                nc.vector.tensor_copy(f, c_bcT).then_inc(f_step, 1)
                dve.wait_ge(f_step, b * 3 + 1)
                nc.vector.tensor_tensor(fr[64:P], c_bcT[64:P], f[64:P], ALU.subtract).then_inc(f_step, 1)
                dve.wait_ge(f_step, b * 3 + 2)
                nc.vector.tensor_copy(f[64:P], fr[64:P]).then_inc(f_step, 1)
                dve.wait_ge(f_step, b * 3 + 3)
                nc.vector.tensor_tensor(f[96:P], fr[96:P], f[96:P], ALU.subtract).then_inc(f_ready, 1)

            def attend(b, n):
                dve.wait_ge(exp_ready, b * U + n + 1)
                dve.wait_ge(s_done, b * U + n + 1)
                nc.vector.tensor_tensor(att[:, n % 2].rearrange("p h i -> p (h i)"), ps_s[:].rearrange("p a n -> p (a n)"),
                                        dexp[:, n % 2], ALU.mult).then_inc(att_raw, 1)

            def copy_state(b):
                dve.wait_ge(st_done, b + 1)
                nc.vector.tensor_tensor(state[:], ps_f[0][:, 0:2 * P].rearrange("p (f n) -> p f n", f=2),
                                        block_mask[:].unsqueeze(1).to_broadcast([P, 2, P]), ALU.mult).then_inc(state_ready, 1)

            def out_sums(b):
                dve.wait_ge(osq_ready, b + 1)
                nc.vector.tensor_reduce(oss[:], osq[:], AX.X, ALU.add).then_inc(oss_ready, 1)

            def gated_out(b):
                dve.wait_ge(orms_ready, b + 1)
                dve.wait_ge(o_ready, b + 1)
                dve.wait_ge(yT_done, b)
                nc.vector.tensor_tensor(y[:].rearrange("p t (h d) -> p (t h) d", d=HD),
                                        o_raw[:].rearrange("p t (h d) -> p (t h) d", d=HD),
                                        orms[:].rearrange("p t h -> p (t h)").unsqueeze(2).to_broadcast([P, NT * H, HD]),
                                        ALU.mult).then_inc(y_step, 1)
                dve.wait_ge(y_step, b + 1)
                nc.vector.tensor_tensor(y[:], y[:], sg[:], ALU.mult).then_inc(y_ready, 1)

            def silu_inverse(b):
                dve.wait_ge(eg_ready, b + 1)
                nc.vector.tensor_scalar(eg[:], eg[:], 1.0, None, ALU.add).then_inc(sg_step, 1)
                dve.wait_ge(sg_step, b * 2 + 1)
                nc.vector.reciprocal(eg[:], eg[:]).then_inc(sg_step, 1)

            def silu_gate(b):
                dve.wait_ge(sg_step, b * 2 + 2)
                nc.vector.tensor_tensor(sg[:], g_raw[:], eg[:], ALU.mult).then_inc(sg_ready, 1)

            def add_out(b):
                dve.wait_ge(resid_ready, b + 1)
                dve.wait_ge(w_done, b + 1)
                nc.vector.tensor_tensor(res[:, b], res[:, b], ps_f[0][:].rearrange("p (t d) -> p t d", t=NT), ALU.add)\
                    .then_inc(res_ready, 1)

            def body(b, prev, nxt, nxt2):
                nb = b + 1
                if prev:
                    out_sums(b - 1)
                attend(b, 0)
                if nxt2:
                    norm_stats(b + 2)
                silu_inverse(b)
                attend(b, 1)
                if nxt:
                    gate_parts(nb)
                if prev:
                    gated_out(b - 1)
                    dve.wait_ge(y_ready, b)
                silu_gate(b)
                if nxt:
                    log_decay(nb)
                dve.wait_ge(av_done, b * U + 1)
                attend(b, 2)
                if nxt2:
                    norm_apply(b + 2)
                if nxt:
                    scale_qk(nb)
                dve.wait_ge(av_done, b * U + 2)
                attend(b, 3)
                if prev:
                    add_out(b - 1)
                copy_state(b)
                if nxt:
                    dve.wait_ge(e_done, b * U + 4)
                    split_sums(nb)
                    dve.wait_ge(av_done, b * U + 4)
                    scale_v(nb)

            for b in range(2):
                norm_stats(b)
                norm_apply(b)
            dve.wait_ge(set_ready, 1)
            gate_parts(0)
            log_decay(0)
            scale_qk(0)
            split_sums(0)
            scale_v(0)
            dve.wait_ge(w_loaded, LOADED)
            steps(dve, body)
            out_sums(B - 1)
            gated_out(B - 1)
            add_out(B - 1)


def cross_attention_and_tokens(nc, res, ident, ctxT, wqT_d, bq_d, wk_d, bk_d, wv_d, bv_d, logits, gammaT, betaT, gateT, x5_d, out):
    S = ctxT.shape[2]
    E = logits.shape[2]
    EPS = 1e-5
    GROUP = 4
    with ExitStack() as ctx:
        def sb(name, shape, dt=F32):
            return ctx.enter_context(nc.sbuf_tensor("E_" + name, shape, dt))

        def psum(name, shape):
            return ctx.enter_context(nc.psum_tensor("E_" + name, shape, F32))

        def sem(name):
            return ctx.enter_context(nc.semaphore("E_" + name))

        wqT = sb("wqT", [P, KD, D])
        wk = sb("wk", [P, D])
        wv = sb("wv", [P, D])
        bq = sb("bq", [P, KD])
        bk = sb("bk", [P, KD])
        bv = sb("bv", [S, D])
        bq_rows = sb("bq_rows", [P, KD, P])
        half = sb("half", [P, 2, NT])
        eps = sb("eps", [P, 2, NT])
        eps_n = sb("eps_n", [P, 2, NT])
        st = sb("st", [P, 2, NT, 6])
        mv = sb("mv", [P, 2, NT, 2])
        veps = sb("veps", [P, 2, NT])
        rstd = sb("rstd", [P, 2, NT])
        r2 = sb("r2", [P, NT])
        v5 = sb("v5", [P, NT])
        v5eps = sb("v5eps", [P, 2, NT])
        rn = sb("rn", [P, 2, NT])
        scale_n = sb("scale_n", [P, 2, NT])
        xn = sb("xn", [P, NT, D])
        xT = sb("xT", [P, KD, T])
        ctx_cur = sb("ctx_cur", [P, S])
        kT = sb("kT", [P, KD, S])
        kq = sb("kq", [P, KD, S])
        v = sb("v", [S, D])
        nmx = sb("nmx", [P, NT])
        prob = sb("prob", [P, NT, S])
        rsum = sb("rsum", [P, NT])
        rinv = sb("rinv", [P, NT])
        pT = sb("pT", [S, NT, P])
        n5 = sb("n5", [P, NT, D])
        tokT = sb("tokT", [P, KD, T])
        fin = sb("fin", [P, B, NT, D])
        ps_x = psum("ps_x", [P, KD, T])
        ps_k = psum("ps_k", [P, 512])
        ps_kq = psum("ps_kq", [P, 512])
        ps_v = psum("ps_v", [P, 512])
        ps_s = psum("ps_s", [P, 512])
        ps_p = psum("ps_p", [P, 512])
        ps_o = psum("ps_o", [P, NT, D])
        ps_n = psum("ps_n", [P, KD, T])
        k_out, kq_out, s_out = (x[:, 0:2 * S].rearrange("p (k s) -> p k s", k=2) for x in (ps_k, ps_kq, ps_s))
        l_out = ps_k[:, 256:256 + NT * E].rearrange("p (t e) -> p t e", t=NT)

        w_loaded, set_ready, bias_ready, stats, seen, aggr, var_eps, rstd_ready, xn_ready, resid_ready, ctx_ready = map(
            sem, "w_loaded set_ready bias_ready stats seen aggr var_eps rstd_ready xn_ready resid_ready ctx_ready".split())
        xT_done, k_done, kq_done, v_done, s_done, pT_done, o_done, nT_done, l_done = map(
            sem, "xT_done k_done kq_done v_done s_done pT_done o_done nT_done l_done".split())
        xT_ready, k_ready, kq_ready, v_ready, max_ready, exp_ready, pT_ready, inv_ready, res_ready = map(
            sem, "xT_ready k_ready kq_ready v_ready max_ready exp_ready pT_ready inv_ready res_ready".split())
        scale_step, scale_ready, n5_ready, x5_ready, tok_ready, l_ready, x5_out, fin_out = map(
            sem, "scale_step scale_ready n5_ready x5_ready tok_ready l_ready x5_out fin_out".split())

        block = ctx.enter_context(nc.Block())

        def steps(engine, body):
            def parts(b):
                return dict(att=b < B, nxt=b + 1 < B, nxt2=b + 2 < B, sums=1 <= b <= B, x5=2 <= b <= B + 1, tok=b >= 3)
            for b in range(3):
                body(b, **parts(b))
            with engine.Fori(3, B - 2) as b:
                body(b, att=True, nxt=True, nxt2=True, sums=True, x5=True, tok=True)
            for b in range(B - 2, B + 3):
                body(b, **parts(b))

        @block.sync
        def _(sp):
            with nc.allow_non_contiguous_dma("biases, one element a partition"):
                sp.dma_start(bq[:], bq_d.rearrange("(k p) -> p k", p=P)).then_inc(w_loaded, 16)
                sp.dma_start(bk[:], bk_d.rearrange("(k p) -> p k", p=P)).then_inc(w_loaded, 16)
            sp.dma_start(wqT[:], wqT_d.rearrange("(k p) n -> p k n", p=P)).then_inc(w_loaded, 16)
            sp.dma_start(wk[:], wk_d).then_inc(w_loaded, 16)
            sp.dma_start(wv[:], wv_d).then_inc(w_loaded, 16)
            sp.dma_start(bv[:], bv_d.rearrange("(a n) -> a n", a=1).partition_broadcast(S)).then_inc(w_loaded, 16)
            for g in range(B // GROUP):
                group = slice(g * GROUP, (g + 1) * GROUP)
                sp.wait_ge(x5_ready, (g + 1) * GROUP)
                sp.dma_start(x5_d.rearrange("(b t p) d -> p b t d", p=P, t=NT)[:, group], res[:, group]).then_inc(x5_out, 16)
                sp.dma_start(out.rearrange("b (t p) d -> p b t d", p=P)[:, group], fin[:, group]).then_inc(fin_out, 16)
            for s in (x5_out, fin_out):
                sp.wait_ge(s, B // GROUP * 16)
        LOADED = 96

        @block.gpsimd
        def _(pool):
            def stage_context(b):
                pool.wait_ge(v_done, b)
                nc.gpsimd.tensor_copy(ctx_cur[:], ctxT[:, b]).then_inc(ctx_ready, 1)

            def norm_scale(n, lo, hi):
                pool.wait_ge(aggr, n + 1)
                nc.gpsimd.tensor_tensor(veps[:, lo:hi], mv[:, lo:hi, :, 1], eps[:, lo:hi], ALU.add).then_inc(var_eps, 1)
                pool.wait_ge(var_eps, n + 1)
                nc.gpsimd.tensor_tensor(rstd[:, lo:hi], veps[:, lo:hi], half[:, lo:hi], ALU.pow).then_inc(rstd_ready, 1)

            def x5_scales(b, n):
                pool.wait_ge(rstd_ready, n + 1)
                nc.gpsimd.tensor_tensor(r2[:], rstd[:, 1], rstd[:, 1], ALU.mult).then_inc(scale_step, 1)
                pool.wait_ge(scale_step, b * 4 + 1)
                nc.gpsimd.tensor_tensor(v5[:], r2[:], mv[:, 1, :, 1], ALU.mult).then_inc(scale_step, 1)
                pool.wait_ge(scale_step, b * 4 + 2)
                nc.gpsimd.tensor_tensor(v5eps[:], v5[:].unsqueeze(1).to_broadcast([P, 2, NT]), eps_n[:], ALU.add).then_inc(scale_step, 1)
                pool.wait_ge(scale_step, b * 4 + 3)
                nc.gpsimd.tensor_tensor(rn[:], v5eps[:], half[:], ALU.pow).then_inc(scale_step, 1)
                pool.wait_ge(scale_step, b * 4 + 4)
                nc.gpsimd.tensor_tensor(scale_n[:], rn[:], rstd[:, 1].unsqueeze(1).to_broadcast([P, 2, NT]), ALU.mult)\
                    .then_inc(scale_ready, 1)

            def keep_residual(b):
                pool.wait_ge(xn_ready, b + 1)
                nc.gpsimd.tensor_copy(res[:, b], xn[:]).then_inc(resid_ready, 1)

            def body(b, att, nxt, nxt2, sums, x5, tok):
                if nxt2 or sums:
                    norm_scale(b + 2, 0 if nxt2 else 1, 2 if sums else 1)
                if nxt2:
                    stage_context(b + 2)
                if sums:
                    x5_scales(b - 1, b + 2)
                if nxt2:
                    keep_residual(b + 2)

            nc.gpsimd.memset(half[:], -0.5)
            nc.gpsimd.memset(eps[:], EPS)
            nc.gpsimd.memset(eps_n[:, 0], EPS)
            nc.gpsimd.memset(eps_n[:, 1], EPS / 4).then_inc(set_ready, 1)
            pool.wait_ge(set_ready, 1)
            stage_context(0)
            for b in range(2):
                norm_scale(b, 0, 1)
                keep_residual(b)
            stage_context(1)
            steps(pool, body)

        @block.tensor
        def _(pe):
            def transpose_x(b):
                pe.wait_ge(xn_ready, b + 1)
                for k in range(KD):
                    for t in range(NT):
                        last = nc.tensor.transpose(ps_x[:, k, t * P:(t + 1) * P], xn[:, t, k * P:(k + 1) * P], ident[:])
                last.then_inc(xT_done, 1)

            def project_k(b):
                pe.wait_ge(ctx_ready, b + 1)
                for m in range(KD):
                    last = nc.tensor.matmul(k_out[:, m], wk[:, m * P:(m + 1) * P], ctx_cur[:], start=True, stop=True)
                last.then_inc(k_done, 1)

            def fold_q(b):
                pe.wait_ge(k_ready, b + 1)
                for m in range(KD):
                    for k in range(KD):
                        last = nc.tensor.matmul(kq_out[:, m], wqT[:, k, m * P:(m + 1) * P], kT[:, k], start=k == 0, stop=k == KD - 1)
                last.then_inc(kq_done, 1)

            def project_v(b):
                nc.tensor.matmul(ps_v[0:S, 0:D], ctx_cur[:], wv[:], start=True, stop=True).then_inc(v_done, 1)

            def scores(b):
                pe.wait_ge(xT_ready, b + 1)
                pe.wait_ge(kq_ready, b + 1)
                for t in range(NT):
                    for k in range(KD):
                        nc.tensor.matmul(s_out[:, t], xT[:, k, t * P:(t + 1) * P], kq[:, k], start=k == 0, stop=False)
                    for k in range(KD):
                        last = nc.tensor.matmul(s_out[:, t], bq_rows[:, k], kT[:, k], start=False, stop=k == KD - 1)
                last.then_inc(s_done, 1)

            def transpose_probs(b):
                pe.wait_ge(exp_ready, b * NT + NT)
                for t in range(NT):
                    last = nc.tensor.transpose(ps_p[0:S, t * P:(t + 1) * P], prob[:, t], ident[:])
                last.then_inc(pT_done, 1)

            def values(b):
                pe.wait_ge(pT_ready, b + 1)
                pe.wait_ge(v_ready, b + 1)
                pe.wait_ge(res_ready, b * NT)
                for t in range(NT):
                    last = nc.tensor.matmul(ps_o[:, t], pT[:, t], v[:], start=True, stop=True)
                last.then_inc(o_done, 1)

            def transpose_n5(b):
                pe.wait_ge(n5_ready, b + 1)
                for k in range(KD):
                    for t in range(NT):
                        last = nc.tensor.transpose(ps_n[:, k, t * P:(t + 1) * P], n5[:, t, k * P:(k + 1) * P], ident[:])
                last.then_inc(nT_done, 1)

            def route_logits(b):
                pe.wait_ge(tok_ready, b + 1)
                for t in range(NT):
                    for k in range(KD):
                        last = nc.tensor.matmul(l_out[:, t], tokT[:, k, t * P:(t + 1) * P], gateT[:, k], start=k == 0, stop=k == KD - 1)
                last.then_inc(l_done, 1)

            def body(b, att, nxt, nxt2, sums, x5, tok):
                if att:
                    scores(b)
                if tok:
                    transpose_n5(b - 3)
                if nxt:
                    transpose_x(b + 1)
                if tok:
                    pe.wait_ge(l_ready, b - 3)
                if nxt:
                    project_k(b + 1)
                if att:
                    transpose_probs(b)
                if nxt:
                    fold_q(b + 1)
                if tok:
                    route_logits(b - 3)
                if att:
                    values(b)
                if nxt:
                    project_v(b + 1)

            pe.wait_ge(w_loaded, LOADED)
            pe.wait_ge(bias_ready, 1)
            transpose_x(0)
            project_k(0)
            fold_q(0)
            project_v(0)
            steps(pe, body)

        @block.scalar
        def _(act):
            def copy_x(b):
                act.wait_ge(xT_done, b + 1)
                nc.scalar.activation(xT[:], ps_x[:], ACT.Copy).then_inc(xT_ready, 1)

            def copy_k(b):
                act.wait_ge(k_done, b + 1)
                for m in range(KD):
                    last = nc.scalar.activation(kT[:, m], k_out[:, m], ACT.Identity, bias=bk[:, m:m + 1])
                last.then_inc(k_ready, 1)

            def copy_kq(b):
                act.wait_ge(kq_done, b + 1)
                nc.scalar.activation(kq[:], kq_out, ACT.Copy).then_inc(kq_ready, 1)

            def exponential(b):
                act.wait_ge(max_ready, b + 1)
                for t in range(NT):
                    nc.scalar.activation(prob[:, t], s_out[:, t], ACT.Exp, bias=nmx[:, t:t + 1],
                                         accum_out=rsum[:, t:t + 1]).then_inc(exp_ready, 1)

            def copy_pT(b):
                act.wait_ge(pT_done, b + 1)
                nc.scalar.activation(pT[:].rearrange("s t i -> s (t i)"), ps_p[0:S, 0:NT * P], ACT.Copy).then_inc(pT_ready, 1)

            def tokens(b):
                act.wait_ge(nT_done, b + 1)
                for k in range(KD):
                    last = nc.scalar.activation(tokT[:, k], ps_n[:, k], ACT.Identity, scale=gammaT[:, k:k + 1], bias=betaT[:, k:k + 1])
                last.then_inc(tok_ready, 1)

            def body(b, att, nxt, nxt2, sums, x5, tok):
                if att:
                    exponential(b)
                if nxt:
                    copy_k(b + 1)
                if tok:
                    tokens(b - 3)
                if att:
                    copy_pT(b)
                if nxt:
                    copy_x(b + 1)
                    copy_kq(b + 1)

            act.wait_ge(w_loaded, LOADED)
            copy_x(0)
            copy_k(0)
            copy_kq(0)
            steps(act, body)

        @block.vector
        def _(dve):
            def norm_stats(n, first, last_of):
                for i, b in enumerate((first, last_of)):
                    if b is not None:
                        for t in range(NT):
                            last = nc.vector.bn_stats(st[:, i, t], res[:, b, t])
                last.then_inc(stats, 1)
                dve.wait_ge(stats, n + 1)
                dve.sem_inc(seen)
                for i, b in enumerate((first, last_of)):
                    if b is not None:
                        for t in range(NT):
                            last = nc.vector.bn_aggr(mv[:, i, t], st[:, i, t])
                last.then_inc(aggr, 1)

            def norm_apply(b):
                dve.wait_ge(rstd_ready, b + 1)
                dve.wait_ge(xT_done, b)
                dve.wait_ge(resid_ready, b)
                for t in range(NT):
                    last = nc.vector.tensor_scalar(xn[:, t], res[:, b, t], mv[:, 0, t, 0:1], rstd[:, 0, t:t + 1],
                                                   ALU.subtract, ALU.mult)
                last.then_inc(xn_ready, 1)

            def maxima(b):
                dve.wait_ge(s_done, b + 1)
                nc.vector.tensor_reduce(nmx[:], s_out, AX.X, ALU.max, negate=True).then_inc(max_ready, 1)

            def copy_v(b):
                dve.wait_ge(v_done, b + 1)
                nc.vector.tensor_tensor(v[:], ps_v[0:S, 0:D], bv[:], ALU.add).then_inc(v_ready, 1)

            def invert_sums(b):
                dve.wait_ge(exp_ready, b * NT + NT)
                nc.vector.reciprocal(rinv[:], rsum[:]).then_inc(inv_ready, 1)

            def add_out(b):
                dve.wait_ge(inv_ready, b + 1)
                dve.wait_ge(resid_ready, b + 1)
                dve.wait_ge(o_done, b + 1)
                for t in range(NT):
                    nc.vector.scalar_tensor_tensor(res[:, b, t], ps_o[:, t], rinv[:, t:t + 1], res[:, b, t],
                                                   ALU.mult, ALU.add).then_inc(res_ready, 1)

            def x5_apply(b):
                def scaled(dst, factor):
                    for t in range(NT):
                        last = nc.vector.tensor_scalar(dst[t], res[:, b, t], mv[:, 1, t, 0:1], factor[:, t:t + 1],
                                                       ALU.subtract, ALU.mult)
                    return last

                dve.wait_ge(scale_ready, b + 1)
                scaled([fin[:, b, t] for t in range(NT)], scale_n[:, 1])
                dve.wait_ge(nT_done, b)
                scaled([n5[:, t] for t in range(NT)], scale_n[:, 0]).then_inc(n5_ready, 1)
                scaled([res[:, b, t] for t in range(NT)], rstd[:, 1]).then_inc(x5_ready, 1)

            def copy_logits(b):
                dve.wait_ge(l_done, b + 1)
                nc.vector.tensor_copy(logits[:, bass.ds(b * NT, NT)], l_out).then_inc(l_ready, 1)

            def body(b, att, nxt, nxt2, sums, x5, tok):
                if att:
                    maxima(b)
                if x5:
                    x5_apply(b - 2)
                if sums:
                    dve.wait_ge(res_ready, b * NT)
                if nxt2 or sums:
                    norm_stats(b + 2, b + 2 if nxt2 else None, b - 1 if sums else None)
                if att:
                    invert_sums(b)
                if tok:
                    copy_logits(b - 3)
                if att:
                    add_out(b)
                if nxt:
                    copy_v(b + 1)
                if nxt2:
                    norm_apply(b + 2)

            dve.wait_ge(w_loaded, LOADED)
            nc.vector.tensor_copy(bq_rows[:], bq[:].unsqueeze(2).to_broadcast([P, KD, P])).then_inc(bias_ready, 1)
            for b in range(2):
                norm_stats(b, b, None)
                norm_apply(b)
            copy_v(0)
            steps(dve, body)


def route(nc, ones, logits, before, table_d, capacity):
    NTILE, E = logits.shape[1], logits.shape[2]
    NONE = 1 << 20
    with ExitStack() as ctx:
        def sb(name, shape, dt=F32):
            return ctx.enter_context(nc.sbuf_tensor("G_" + name, shape, dt))

        def sem(name):
            return ctx.enter_context(nc.semaphore("G_" + name))

        none = sb("none", [P, E * capacity // P, 2], I32)
        no_i = sb("no_i", [P, E], I32)
        no = sb("no", [P, E])
        no8 = sb("no8", [P, E])
        top = sb("top", [P, NTILE])
        is_top = sb("is_top", [P, NTILE, E])
        cand = sb("cand", [P, NTILE, E])
        first = sb("first", [P, NTILE])
        onehot = sb("onehot", [P, NTILE, E])
        shifted = sb("shifted", [P, NTILE, E])
        expo = sb("expo", [P, NTILE, E])
        esum = sb("esum", [P, NTILE])
        prob = sb("prob", [P, NTILE])
        run = [sb(f"run{i}", [P, NTILE, E]) for i in range(2)]
        tot = sb("tot", [P, NTILE, E])
        offset = sb("offset", [P, NTILE, E])
        ahead = sb("ahead", [P, NTILE, E])
        rank = sb("rank", [P, NTILE])
        over = sb("over", [P, NTILE])
        slot = sb("slot", [P, NTILE])
        slot_i = sb("slot_i", [P, NTILE], I32)
        entry = sb("entry", [P, NTILE, 2], I32)
        ps_in = ctx.enter_context(nc.psum_tensor("G_ps_in", [P, NTILE, E], F32))
        ps_tot = ctx.enter_context(nc.psum_tensor("G_ps_tot", [P, NTILE, E], F32))
        consts, none_out, chain, shifted_ready, expo_ready, onehot_ready, counted, entry_ready, scattered = map(
            sem, "consts none_out chain shifted_ready expo_ready onehot_ready counted entry_ready scattered".split())
        block = ctx.enter_context(nc.Block())

        @block.gpsimd
        def _(pool):
            nc.gpsimd.iota(none[:], [[0, E * capacity // P], [0, 2]], base=NONE, channel_multiplier=0).then_inc(consts, 1)
            nc.gpsimd.iota(no_i[:], [[1, E]], base=0, channel_multiplier=0).then_inc(consts, 1)
            nc.gpsimd.iota(entry[:, :, 0], [[P, NTILE]], base=0, channel_multiplier=1).then_inc(consts, 1)
            pool.wait_ge(none_out, 16)
            pool.wait_ge(entry_ready, 1)
            for i in range(NTILE):
                nc.gpsimd.indirect_dma_start(out=table_d, out_offset=bass.IndirectOffsetOnAxis(ap=slot_i[:, i:i + 1], axis=0),
                                             in_=entry[:, i], in_offset=None, bounds_check=E * capacity - 1,
                                             oob_is_err=False).then_inc(scattered, 16)
            pool.wait_ge(scattered, 16 * NTILE)

        @block.sync
        def _(sp):
            sp.wait_ge(consts, 3)
            sp.dma_start(table_d.rearrange("(s p) k -> p s k", p=P), none[:]).then_inc(none_out, 16)
            sp.wait_ge(none_out, 16)

        @block.tensor
        def _(pe):
            pe.wait_ge(onehot_ready, 1)
            nc.tensor.matmul(ps_in[:], before[:], onehot[:], start=True, stop=True)
            nc.tensor.matmul(ps_tot[:], ones[:], onehot[:], start=True, stop=True).then_inc(counted, 1)

        @block.scalar
        def _(act):
            act.wait_ge(shifted_ready, 1)
            nc.scalar.activation(expo[:], shifted[:], ACT.Exp).then_inc(expo_ready, 1)

        @block.vector
        def _(dve):
            count = [0]

            def then(ins):
                count[0] += 1
                ins.then_inc(chain, 1)
                dve.wait_ge(chain, count[0])

            def per_tile(x):
                return x[:].unsqueeze(2).to_broadcast([P, NTILE, E])

            def per_expert(x):
                return x[:].unsqueeze(1).to_broadcast([P, NTILE, E])

            dve.wait_ge(consts, 3)
            then(nc.vector.tensor_copy(no[:], no_i[:]))
            nc.vector.tensor_scalar(no8[:], no[:], float(E), None, ALU.add)
            then(nc.vector.tensor_reduce(top[:], logits[:], AX.X, ALU.max))
            nc.vector.tensor_tensor(shifted[:], logits[:], per_tile(top), ALU.subtract).then_inc(shifted_ready, 1)
            then(nc.vector.tensor_tensor(is_top[:], logits[:], per_tile(top), ALU.is_ge))
            then(nc.vector.scalar_tensor_tensor(cand[:], is_top[:], -float(E), per_expert(no8), ALU.mult, ALU.add))
            then(nc.vector.tensor_reduce(first[:], cand[:], AX.X, ALU.min))
            nc.vector.tensor_tensor(onehot[:], per_expert(no), per_tile(first), ALU.is_equal).then_inc(onehot_ready, 1)
            dve.wait_ge(expo_ready, 1)
            then(nc.vector.tensor_reduce(esum[:], expo[:], AX.X, ALU.add))
            then(nc.vector.reciprocal(prob[:], esum[:]))
            nc.vector.tensor_scalar(entry[:, :, 1].bitcast(F32), prob[:], 0.5, None, ALU.mult)
            dve.wait_ge(counted, 1)
            then(nc.vector.tensor_copy(tot[:], ps_tot[:]))
            then(nc.vector.tensor_copy(run[0][:], tot[:]))
            k, i = 1, 0
            while k < NTILE:
                nc.vector.tensor_copy(run[1 - i][:, 0:k], run[i][:, 0:k])
                then(nc.vector.tensor_tensor(run[1 - i][:, k:], run[i][:, k:], run[i][:, 0:NTILE - k], ALU.add))
                k, i = 2 * k, 1 - i
            then(nc.vector.tensor_tensor(offset[:], run[i][:], tot[:], ALU.subtract))
            then(nc.vector.tensor_tensor(ahead[:], ps_in[:], offset[:], ALU.add))
            then(nc.vector.tensor_tensor(ahead[:], ahead[:], onehot[:], ALU.mult))
            then(nc.vector.tensor_reduce(rank[:], ahead[:], AX.X, ALU.add))
            then(nc.vector.tensor_scalar(over[:], rank[:], float(capacity), float(NONE), ALU.is_ge, ALU.mult))
            then(nc.vector.scalar_tensor_tensor(slot[:], first[:], float(capacity), rank[:], ALU.mult, ALU.add))
            nc.vector.tensor_tensor(slot_i[:], slot[:], over[:], ALU.add).then_inc(entry_ready, 1)


def moe_ffn(nc, ident, half, gammaT, betaT, table_d, x5_d, wi_d, wo_d, out, capacity):
    E, _, I = wi_d.shape
    NTOK = x5_d.shape[0]
    TI, MI = capacity // P, I // P
    EPS = 1e-5
    rows = out.rearrange("b t d -> (b t) d")
    with ExitStack() as ctx:
        def sb(name, shape, dt=F32):
            return ctx.enter_context(nc.sbuf_tensor("H_" + name, shape, dt))

        def psum(name, shape):
            return ctx.enter_context(nc.psum_tensor("H_" + name, shape, F32))

        def sem(name):
            return ctx.enter_context(nc.semaphore("H_" + name))

        table = sb("table", [P, E * TI, 2], I32)
        slots = sb("slots", [P, 2, TI, 2], I32)
        to_slots = sb("to_slots", [P, TI, 2], I32)
        wi = sb("wi", [P, 2, KD, I])
        wo = sb("wo", [P, 2, MI, D])
        xg = sb("xg", [P, 2, TI, D])
        ng = sb("ng", [P, TI, D])
        tokT = sb("tokT", [P, KD, capacity])
        hT = sb("hT", [P, MI, capacity])
        fin = sb("fin", [P, TI, D])
        st = sb("st", [P, TI, 6])
        mv = sb("mv", [P, TI, 2])
        veps = sb("veps", [P, TI])
        rstd = sb("rstd", [P, TI])
        ps_x = [psum(f"ps_x{i}", [P, capacity]) for i in range(KD)]
        ps_h = [psum(f"ps_h{i}", [P, capacity]) for i in range(2)]
        ps_d = [psum(f"ps_d{i}", [P, 2, D]) for i in range(TI // 2)]
        table_in, w_in0, w_in1, gathered0, gathered1, clear, staged, kept, scattered = map(
            sem, "table_in w_in0 w_in1 gathered0 gathered1 clear staged kept scattered".split())
        stats, seen, aggr, var_eps, rstd_ready, ng_ready, xT_done, tok_ready, h_done, h_ready, d_done, sum_ready, fin_ready = map(
            sem, "stats seen aggr var_eps rstd_ready ng_ready xT_done tok_ready h_done h_ready d_done sum_ready fin_ready".split())
        w_in, gathered = (w_in0, w_in1), (gathered0, gathered1)

        block = ctx.enter_context(nc.Block())

        @block.sync
        def _(sp):
            sp.dma_start(table[:], table_d.rearrange("(s p) k -> p s k", p=P)).then_inc(table_in, 16)

            def load(e, u):
                sp.dma_start(wi[:, u], wi_d[e].rearrange("(k p) n -> p k n", p=P)).then_inc(w_in[u], 16)
                sp.dma_start(wo[:, u], wo_d[e].rearrange("(k p) n -> p k n", p=P)).then_inc(w_in[u], 16)
            load(0, 0)
            load(1, 1)
            with sp.Fori(0, E // 2 - 1) as j:
                for u in range(2):
                    sp.wait_ge(d_done, j * 2 * TI + (u + 1) * TI)
                    load(j * 2 + (2 + u), u)

        @block.gpsimd
        def _(pool):
            def norm_scale(n, eps):
                pool.wait_ge(aggr, n + 1)
                pool.sem_inc(seen)
                nc.gpsimd.tensor_scalar(veps[:], mv[:, :, 1], eps, None, ALU.add).then_inc(var_eps, 1)
                pool.wait_ge(var_eps, n + 1)
                for i in range(TI // NT):
                    last = nc.gpsimd.tensor_tensor(rstd[:, i * NT:(i + 1) * NT], veps[:, i * NT:(i + 1) * NT], half[:], ALU.pow)
                last.then_inc(rstd_ready, 1)

            def gather(e, u, n):
                if n is None:
                    pool.wait_ge(kept, e - 1)
                    pool.sem_inc(seen)
                nc.gpsimd.tensor_copy(slots[:, u], table[:, bass.ds(e * TI, TI)] if n is None else table[:, n * TI:(n + 1) * TI])\
                    .then_inc(staged, 1)
                pool.wait_ge(staged, e + 1)
                pool.sem_inc(seen)
                for i in range(TI):
                    nc.gpsimd.indirect_dma_start(out=xg[:, u, i], out_offset=None, in_=x5_d,
                                                 in_offset=bass.IndirectOffsetOnAxis(ap=slots[:, u, i, 0:1], axis=0),
                                                 bounds_check=NTOK - 1, oob_is_err=False).then_inc(gathered[u], 16)

            def keep_slots(e, u):
                pool.wait_ge(fin_ready, e + 1)
                pool.wait_ge(scattered, e * TI * 16)
                pool.sem_inc(seen)
                nc.gpsimd.tensor_copy(to_slots[:], slots[:, u]).then_inc(kept, 1)

            def scatter(e):
                pool.wait_ge(kept, e + 1)
                pool.sem_inc(seen)
                for i in range(TI):
                    nc.gpsimd.indirect_dma_start(out=rows, out_offset=bass.IndirectOffsetOnAxis(ap=to_slots[:, i, 0:1], axis=0),
                                                 in_=fin[:, i], in_offset=None, bounds_check=NTOK - 1,
                                                 oob_is_err=False).then_inc(scattered, 16)

            def body(e, u, more, more2):
                if more:
                    norm_scale(e * 2 + 1, EPS)
                norm_scale(e * 2 + 2 if more else E * 2 - 1, EPS / 4)
                keep_slots(e, u)
                if more2:
                    gather(e + 2, u, None)
                scatter(e)

            nc.gpsimd.memset(xg[:], 0.0).then_inc(clear, 1)
            pool.wait_ge(clear, 1)
            pool.wait_ge(table_in, 16)
            gather(0, 0, 0)
            gather(1, 1, 1)
            norm_scale(0, EPS)
            with pool.Fori(0, E // 2 - 1) as j:
                body(j * 2, 0, True, True)
                body(j * 2 + 1, 1, True, True)
            body(E - 2, 0, True, False)
            body(E - 1, 1, False, False)
            pool.wait_ge(scattered, 16 * TI * E)

        @block.tensor
        def _(pe):
            def transpose(e):
                pe.wait_ge(ng_ready, e + 1)
                for k in range(KD):
                    for t in range(TI):
                        last = nc.tensor.transpose(ps_x[k][:, t * P:(t + 1) * P], ng[:, t, k * P:(k + 1) * P], ident[:])
                last.then_inc(xT_done, 1)

            def hidden(e, u, m, first):
                if not (first and m < 2):
                    pe.wait_ge(h_ready, e * MI + (m - 1))
                for k in range(KD):
                    last = nc.tensor.matmul(ps_h[m % 2][:], wi[:, u, k, m * P:(m + 1) * P], tokT[:, k], start=k == 0, stop=k == KD - 1)
                last.then_inc(h_done, 1)

            def down(e, u, first, tiles):
                for t in tiles:
                    if t % 2 == 0 and not first:
                        pe.wait_ge(sum_ready, e * TI + (t + 2 - TI))
                    for m in range(MI):
                        if t == 0 and m >= MI - 2:
                            pe.wait_ge(h_ready, e * MI + m + 1)
                        elif t == 0 and m == 0:
                            pe.wait_ge(h_ready, e * MI + MI - 2)
                        last = nc.tensor.matmul(ps_d[t // 2][:, t % 2], hT[:, m, t * P:(t + 1) * P], wo[:, u, m],
                                                start=m == 0, stop=m == MI - 1)
                    last.then_inc(d_done, 1)

            def body(e, u, j, first=False, more=True):
                pe.wait_ge(w_in[u], j * 32 + 32)
                pe.wait_ge(tok_ready, e + 1)
                for m in range(MI):
                    hidden(e, u, m, first)
                down(e, u, first, range(TI // 2))
                if more:
                    transpose(e + 1)
                down(e, u, first, range(TI // 2, TI))

            transpose(0)
            body(0, 0, 0, first=True)
            body(1, 1, 0)
            with pe.Fori(1, E // 2 - 1) as j:
                body(j * 2, 0, j)
                body(j * 2 + 1, 1, j)
            body(E - 2, 0, E // 2 - 1)
            body(E - 1, 1, E // 2 - 1, more=False)

        @block.scalar
        def _(act):
            def tokens(e):
                act.wait_ge(xT_done, e + 1)
                for k in range(KD):
                    last = nc.scalar.activation(tokT[:, k], ps_x[k][:], ACT.Identity, scale=gammaT[:, k:k + 1], bias=betaT[:, k:k + 1])
                last.then_inc(tok_ready, 1)

            def body(e, more):
                for m in range(MI):
                    act.wait_ge(h_done, e * MI + m + 1)
                    nc.scalar.activation(hT[:, m], ps_h[m % 2][:], ACT.Gelu).then_inc(h_ready, 1)
                if more:
                    tokens(e + 1)

            tokens(0)
            with act.Fori(0, E - 1) as e:
                body(e, True)
            body(E - 1, False)

        @block.vector
        def _(dve):
            def norm(src, dst, n, ready):
                for t in range(TI):
                    last = nc.vector.bn_stats(st[:, t], src[:, t])
                last.then_inc(stats, 1)
                dve.wait_ge(stats, n + 1)
                dve.sem_inc(seen)
                for t in range(TI):
                    last = nc.vector.bn_aggr(mv[:, t], st[:, t])
                last.then_inc(aggr, 1)
                dve.wait_ge(rstd_ready, n + 1)
                for t in range(TI):
                    last = nc.vector.tensor_scalar(dst[:, t], src[:, t], mv[:, t, 0:1], rstd[:, t:t + 1], ALU.subtract, ALU.mult)
                last.then_inc(ready, 1)

            def before(e, u, j, n):
                dve.wait_ge(gathered[u], j * TI * 16 + TI * 16)
                dve.wait_ge(xT_done, e)
                norm(xg[:, u], ng[:], n, ng_ready)

            def after(e, u, n, first):
                for t in range(TI):
                    dve.wait_ge(d_done, e * TI + 2 * (t // 2) + 2)
                    nc.vector.scalar_tensor_tensor(xg[:, u, t], ps_d[t // 2][:, t % 2], slots[:, u, t, 1:2].bitcast(F32), xg[:, u, t],
                                                   ALU.mult, ALU.add).then_inc(sum_ready, 1)
                dve.wait_ge(sum_ready, e * TI + TI)
                if not first:
                    dve.wait_ge(scattered, e * TI * 16)
                norm(xg[:, u], fin[:], n, fin_ready)

            before(0, 0, 0, 0)
            before(1, 1, 0, 1)
            after(0, 0, 2, True)
            with dve.Fori(1, E // 2) as j:
                before(j * 2, 0, j, j * 4 - 1)
                after(j * 2 - 1, 1, j * 4, False)
                before(j * 2 + 1, 1, j, j * 4 + 1)
                after(j * 2, 0, j * 4 + 2, False)
            after(E - 1, 1, E * 2 - 1, False)


def clear_used_semaphores(nc):
    used = sorted(nc.released_uncleared_semaphores)
    with nc.Block() as block:
        @block.gpsimd
        def _(pool):
            start = 0
            for n in range(1, len(used) + 1):
                if n == len(used) or used[n] != used[n - 1] + 1:
                    pool.sem_clear(range(used[start], used[n - 1] + 1))
                    start = n


def program(nc, i, out, stop):
    with ExitStack() as ctx:
        res = ctx.enter_context(nc.sbuf_tensor("res", [P, B, NT, D], F32))
        ident = ctx.enter_context(nc.sbuf_tensor("ident", [P, P], F32))
        ones = ctx.enter_context(nc.sbuf_tensor("ones", [P, P], F32))
        half = ctx.enter_context(nc.sbuf_tensor("half", [P, NT], F32))
        eps = ctx.enter_context(nc.sbuf_tensor("eps", [P, NT], F32))
        ctxT = ctx.enter_context(nc.sbuf_tensor("ctxT", [P, B, i["ctxT"].shape[2]], F32))
        set_ready = ctx.enter_context(nc.semaphore("set_ready"))
        ctx_loaded = ctx.enter_context(nc.semaphore("ctx_loaded"))
        with nc.Block() as block:
            @block.sync
            def _(sp):
                sp.dma_start(ctxT[:], i["ctxT"].rearrange("b p s -> p b s")).then_inc(ctx_loaded, 16)

            @block.gpsimd
            def _(pool):
                nc.gpsimd.memset(half[:], -0.5)
                nc.gpsimd.memset(eps[:], 1e-5)
                nc.gpsimd.memset(ones[:], 1.0).then_inc(set_ready, 1)
                pool.wait_ge(set_ready, 1)
                nc.gpsimd.affine_select(out=ident[:], in_=ones[:], compare_op=ALU.is_equal, fill=0.0, base=0,
                                        pattern=[[-1, P]], channel_multiplier=1)
        linear_attention(nc, res, ident, i["x"], i["L0_attn_W_thetaT"], i["L0_attn_W_phiT"], i["L0_attn_W_gT"])
        if stop > 0:
            cross_attention(nc, res, ident, half, eps, ctxT, ctx_loaded, i["L0_xattn_Wq"], i["L0_xattn_Wk"], i["L0_xattn_Wv"], i["L0_xattn_Wo"],
                            i["L0_xattn_bo"])
        if stop > 1:
            expert_ffn(nc, res, ident, half, eps, i["L0_ffn_router_indices"], i["L0_ffn_routing_weights"], i["L0_ffn_gate_up"],
                       i["L0_ffn_gate_up_bias"], i["L0_ffn_down_proj"], i["L0_ffn_down_proj_bias"])
        if stop > 2:
            gated_retention(nc, res, ident, half, eps, {k: i["L1_attn_" + k] for k in ("wqk", "wvg", "wgt", "wo")}, i)
        if stop > 4:
            NTOK, E = B * T, i["L1_ffn_wi"].shape[0]
            x5_d = nc.dram_tensor("x5_d", (NTOK, D), F32, kind="Internal").ap()
            table_d = nc.dram_tensor("table_d", (E * CAPACITY, 2), I32, kind="Internal").ap()
            logits = ctx.enter_context(nc.sbuf_tensor("logits", [P, NTOK // P, E], F32))
            before = ctx.enter_context(nc.sbuf_tensor("before", [P, P], F32))
            gateT = ctx.enter_context(nc.sbuf_tensor("gateT", [P, KD, E], F32))
            gammaT = ctx.enter_context(nc.sbuf_tensor("gammaT", [P, KD], F32))
            betaT = ctx.enter_context(nc.sbuf_tensor("betaT", [P, KD], F32))
            gate_loaded = ctx.enter_context(nc.semaphore("gate_loaded"))
            with nc.Block() as block:
                @block.sync
                def _(sp):
                    sp.dma_start(before[:], i["before"]).then_inc(gate_loaded, 16)
                    with nc.allow_non_contiguous_dma("small: the router's weights, one element a partition"):
                        sp.dma_start(gateT[:], i["L1_ffn_gateT"].rearrange("(k p) e -> p k e", p=P)).then_inc(gate_loaded, 16)
                        sp.dma_start(gammaT[:], i["L1_ffn_ln_gamma"].rearrange("(k p) -> p k", p=P)).then_inc(gate_loaded, 16)
                        sp.dma_start(betaT[:], i["L1_ffn_ln_beta"].rearrange("(k p) -> p k", p=P)).then_inc(gate_loaded, 16)
                    sp.wait_ge(gate_loaded, 64)
            clear_used_semaphores(nc)
            cross_attention_and_tokens(nc, res, ident, ctxT, i["L1_xattn_WqT"], i["L1_xattn_bq"], i["L1_xattn_Wk"],
                                       i["L1_xattn_bk"], i["L1_xattn_Wv"], i["L1_xattn_bv"],
                                       logits, gammaT, betaT, gateT, x5_d, out)
            route(nc, ones, logits, before, table_d, CAPACITY)
            moe_ffn(nc, ident, half, gammaT, betaT, table_d, x5_d, i["L1_ffn_wi"], i["L1_ffn_wo"], out, CAPACITY)
            return
        s_out = ctx.enter_context(nc.semaphore("s_out"))
        with nc.Block() as block:
            @block.sync
            def _(sp):
                sp.dma_start(out.rearrange("b (t p) d -> p b t d", p=P), res[:]).then_inc(s_out, 16)
                sp.wait_ge(s_out, 16)


CAPACITY = 512
STOP = 6


def kernel(**inputs):
    import ml_dtypes
    import numpy as np
    import concourse.bacc as bacc
    from concourse.bass_utils import run_bass_kernel_spmd

    nc = bacc.Bacc("TRN2", target_bir_lowering=False, num_devices=1)
    given = {k: np.asarray(v) for k, v in inputs.items()}
    arrays = {k: given[k] for k in ("x", "L0_xattn_Wq", "L0_xattn_Wk", "L0_xattn_Wv", "L0_xattn_Wo", "L0_xattn_bo")}
    arrays["ctxT"] = given["ctx_512"].transpose(0, 2, 1)
    for k in ("L0_attn_W_theta", "L0_attn_W_phi", "L0_attn_W_g"):
        arrays[k + "T"] = given[k].T
    for k in ("L0_ffn_router_indices", "L0_ffn_routing_weights", "L0_ffn_down_proj", "L0_ffn_down_proj_bias"):
        arrays[k] = given[k]
    w, bias = given["L0_ffn_gate_up_proj"], given["L0_ffn_gate_up_proj_bias"]
    arrays["L0_ffn_gate_up"] = np.concatenate([w[..., ::2], w[..., 1::2]], -1)
    arrays["L0_ffn_gate_up_bias"] = np.concatenate([bias[:, ::2], bias[:, 1::2]], -1).reshape(len(bias), -1, P).transpose(2, 0, 1)
    for k in ("L1_xattn_bq", "L1_xattn_Wk", "L1_xattn_bk", "L1_xattn_Wv", "L1_xattn_bv", "L1_ffn_ln_gamma", "L1_ffn_ln_beta",
              "L1_ffn_wi", "L1_ffn_wo"):
        arrays[k] = given[k]
    arrays["L1_xattn_WqT"], arrays["L1_ffn_gateT"] = given["L1_xattn_Wq"].T, given["L1_ffn_gate_weight"].T
    arrays["L1_attn_wqk"] = np.concatenate([given["L1_attn_Wq"], given["L1_attn_Wk"]], 1)
    arrays["L1_attn_wvg"] = np.concatenate([given["L1_attn_Wv"], given["L1_attn_Wg"]], 1)
    arrays["L1_attn_wgt"], arrays["L1_attn_wo"] = given["L1_attn_Wgt"], given["L1_attn_Wo"]
    row, col = np.arange(P)[:, None], np.arange(P)[None, :]
    arrays["before"] = (row < col).astype(np.float32)
    arrays["upto"] = ((row <= col) / 16).astype(np.float32)
    arrays["after"] = ((row > col) / 16).astype(np.float32)
    arrays["head_mask"] = ((row // RET_D % 2 == np.arange(2)) / 4).astype(np.float32)
    arrays["block_mask"] = ((row // RET_D == col // RET_D) / 4).astype(np.float32)
    heads = np.array([retention_head(p) for p in range(RET_H)])
    of_head = (row % 32 == heads) & (row // 32 != 1)
    arrays["sel"] = np.repeat(of_head[:, :, None], P, 2).astype(ml_dtypes.bfloat16)
    arrays["nsel"] = -arrays["sel"]
    arrays = {k: np.ascontiguousarray(a) for k, a in arrays.items()}
    ins = {k: nc.dram_tensor("in_" + k, a.shape, mybir.dt.from_np(a.dtype), kind="ExternalInput").ap() for k, a in arrays.items()}
    out = nc.dram_tensor("out", (B, T, D), F32, kind="ExternalOutput").ap()
    program(nc, ins, out, STOP)
    r = run_bass_kernel_spmd(nc, [{"in_" + k: a for k, a in arrays.items()}], core_ids=[0])
    return r.results[0]["out"]
```

```python
from contextlib import ExitStack
import concourse.bass as bass
from concourse import mybir

ALU = mybir.AluOpType
ACT = mybir.ActivationFunctionType
AX = mybir.AxisListType
F32 = mybir.dt.float32
BF16 = mybir.dt.bfloat16
I32 = mybir.dt.int32

P = 128
B, T, D = 32, 256, 256
NT = T // P
KD = D // P
LATENT = 64


def linear_attention(nc, res, ident, x_in, wthT, wphT, wgT, prefetch):
    L2 = 2 * LATENT
    with ExitStack() as ctx:
        def sb(name, shape, dt=F32):
            return ctx.enter_context(nc.sbuf_tensor("A_" + name, shape, dt))

        def psum(name, shape):
            return ctx.enter_context(nc.psum_tensor("A_" + name, shape, F32))

        def sem(name):
            return ctx.enter_context(nc.semaphore("A_" + name))

        tp_w = sb("tp_w", [P, KD, L2])
        g_w = sb("g_w", [P, KD, D])
        xn = sb("xn", [P, 2, NT, D])
        xT = sb("xT", [P, KD, T])
        tp = sb("tp", [P, 2, NT, L2])
        thetaT = sb("thetaT", [LATENT, T])
        u = sb("u", [P, KD, LATENT])
        v = sb("v", [LATENT, D])
        ps_xT = psum("ps_xT", [P, KD, T])
        ps_tp = psum("ps_tp", [P, NT, L2])
        ps_tT = psum("ps_tT", [L2, T])
        ps_u = psum("ps_u", [P, KD, LATENT])
        ps_v = psum("ps_v", [LATENT, D])
        ps_out = psum("ps_out", [P, NT, D])
        weights, x_loaded, xn_ready, xT_done, xT_ready, tp_done, tp_ready = map(
            sem, "weights x_loaded xn_ready xT_done xT_ready tp_done tp_ready".split())
        tT_done, tT_ready, u_done, u_ready, v_done, v_ready, out_done, out_added = map(
            sem, "tT_done tT_ready u_done u_ready v_done v_ready out_done out_added".split())

        block = ctx.enter_context(nc.Block())

        @block.sync
        def _(sp):
            sp.dma_start(tp_w[:, :, 0:LATENT], wthT.rearrange("(k p) l -> p k l", p=P)).then_inc(weights, 16)
            sp.dma_start(tp_w[:, :, LATENT:L2], wphT.rearrange("(k p) l -> p k l", p=P)).then_inc(weights, 16)
            for c in range(B // 2):
                if c:
                    sp.wait_ge(x_loaded, 16 * c)
                sp.dma_start(res[:, 2 * c:2 * c + 2], x_in[2 * c:2 * c + 2].rearrange("b (t p) d -> p b t d", p=P)).then_inc(x_loaded, 16)
                if c == 0:
                    sp.dma_start(g_w[:], wgT.rearrange("(k p) l -> p k l", p=P)).then_inc(weights, 16)
            prefetch(sp)

        @block.gpsimd
        def _(pool):
            def copy_x(b, i):
                if i is not None:
                    pool.wait_ge(u_done, b - 1)
                nc.gpsimd.tensor_copy(xn[:, b % 2 if i is None else i], res[:, b]).then_inc(xn_ready, 1)

            pool.wait_ge(x_loaded, 16)
            copy_x(0, None)
            copy_x(1, None)
            with pool.Fori(1, B // 2) as j:
                pool.wait_ge(x_loaded, j * 16 + 16)
                copy_x(j * 2, 0)
                copy_x(j * 2 + 1, 1)

        @block.tensor
        def _(pe):
            def transpose_x(b, i):
                pe.wait_ge(xn_ready, b + 1)
                for k in range(KD):
                    for t in range(NT):
                        last = nc.tensor.transpose(ps_xT[:, k, t * P:(t + 1) * P], xn[:, i, t, k * P:(k + 1) * P], ident[:])
                last.then_inc(xT_done, 1)

            def project(b):
                pe.wait_ge(xT_ready, b + 1)
                pe.wait_ge(tp_ready, b)
                for t in range(NT):
                    for k in range(KD):
                        last = nc.tensor.matmul(ps_tp[:, t], xT[:, k, t * P:(t + 1) * P], tp_w[:, k], start=k == 0, stop=k == KD - 1)
                last.then_inc(tp_done, 1)

            def transpose_theta(b, i):
                pe.wait_ge(tp_ready, b + 1)
                pe.wait_ge(tT_ready, b)
                for t in range(NT):
                    last = nc.tensor.transpose(ps_tT[:, t * P:(t + 1) * P], tp[:, i, t], ident[:])
                last.then_inc(tT_done, 1)

            def u_mm(b, i):
                pe.wait_ge(u_ready, b)
                for m in range(KD):
                    for t in range(NT):
                        last = nc.tensor.matmul(ps_u[:, m], xn[:, i, t, m * P:(m + 1) * P], tp[:, i, t, LATENT:L2],
                                                start=t == 0, stop=t == NT - 1)
                last.then_inc(u_done, 1)

            def v_mm(b):
                pe.wait_ge(u_ready, b + 1)
                for k in range(KD):
                    last = nc.tensor.matmul(ps_v[:], u[:, k], g_w[:, k], start=k == 0, stop=k == KD - 1)
                last.then_inc(v_done, 1)

            def out_mm(b):
                pe.wait_ge(v_ready, b + 1)
                pe.wait_ge(tT_ready, b + 1)
                pe.wait_ge(out_added, b)
                for t in range(NT):
                    last = nc.tensor.matmul(ps_out[:, t], thetaT[:, t * P:(t + 1) * P], v[:], start=True, stop=True)
                last.then_inc(out_done, 1)

            def step(b, i, first=False):
                transpose_x(b + 1, 1 - i)
                u_mm(b, i)
                if not first:
                    out_mm(b - 1)
                project(b + 1)
                v_mm(b)
                transpose_theta(b + 1, 1 - i)

            pe.wait_ge(weights, 48)
            transpose_x(0, 0)
            project(0)
            transpose_theta(0, 0)
            step(0, 0, first=True)
            step(1, 1)
            with pe.Fori(1, B // 2 - 1) as j:
                step(j * 2, 0)
                step(j * 2 + 1, 1)
            step(B - 2, 0)
            u_mm(B - 1, 1)
            out_mm(B - 2)
            v_mm(B - 1)
            out_mm(B - 1)

        @block.scalar
        def _(act):
            def copy_x(b):
                act.wait_ge(xT_done, b + 1)
                nc.scalar.activation(xT[:], ps_xT[:], ACT.Copy).then_inc(xT_ready, 1)

            def copy_theta(b):
                act.wait_ge(tT_done, b + 1)
                act.wait_ge(out_done, b)
                nc.scalar.activation(thetaT[:], ps_tT[0:LATENT], ACT.Copy).then_inc(tT_ready, 1)

            def copy_u(b):
                act.wait_ge(u_done, b + 1)
                nc.scalar.activation(u[:], ps_u[:], ACT.Copy).then_inc(u_ready, 1)

            def copy_v(b):
                act.wait_ge(v_done, b + 1)
                nc.scalar.activation(v[:], ps_v[:], ACT.Copy, scale=D ** -0.5).then_inc(v_ready, 1)

            copy_x(0)
            with act.Fori(0, B - 1) as b:
                copy_x(b + 1)
                copy_u(b)
                copy_theta(b)
                copy_v(b)
            copy_u(B - 1)
            copy_theta(B - 1)
            copy_v(B - 1)

        @block.vector
        def _(dve):
            def copy_tp(b, i):
                dve.wait_ge(tp_done, b + 1)
                nc.vector.tensor_copy(tp[:, i], ps_tp[:]).then_inc(tp_ready, 1)

            def add_out(b):
                dve.wait_ge(out_done, b + 1)
                nc.vector.tensor_tensor(res[:, b], res[:, b], ps_out[:], ALU.add).then_inc(out_added, 1)

            copy_tp(0, 0)
            copy_tp(1, 1)
            add_out(0)
            copy_tp(2, 0)
            with dve.Fori(1, B // 2 - 1) as j:
                for i in range(2):
                    add_out(j * 2 + (i - 1))
                    copy_tp(j * 2 + (i + 1), 1 - i)
            add_out(B - 3)
            copy_tp(B - 1, 1)
            add_out(B - 2)
            add_out(B - 1)


def cross_attention_weights(nc, ctx, inner):
    shapes = {"wq": [P, KD, inner], "wk": [P, inner], "wv": [P, inner], "wo": [P, inner // P, D], "bo": [P, D]}
    w = {k: ctx.enter_context(nc.sbuf_tensor("B_" + k, shape, F32)) for k, shape in shapes.items()}
    return w, ctx.enter_context(nc.semaphore("B_w_loaded"))


def load_cross_attention_weights(sp, w, w_loaded, i):
    sp.dma_start(w["wq"][:], i["L0_xattn_Wq"].rearrange("(k p) n -> p k n", p=P)).then_inc(w_loaded, 16)
    sp.dma_start(w["wk"][:], i["L0_xattn_Wk"]).then_inc(w_loaded, 16)
    sp.dma_start(w["wv"][:], i["L0_xattn_Wv"]).then_inc(w_loaded, 16)
    sp.dma_start(w["wo"][:], i["L0_xattn_Wo"].rearrange("(k p) n -> p k n", p=P)).then_inc(w_loaded, 16)
    sp.dma_start(w["bo"][:], i["L0_xattn_bo"].rearrange("(a n) -> a n", a=1).partition_broadcast(P)).then_inc(w_loaded, 16)


def cross_attention(nc, res, ident, half, eps, ctxT, ctx_loaded, w, w_loaded):
    H, HD, S = 16, 64, ctxT.shape[2]
    INNER = H * HD
    MT = INNER // P
    HU = 8
    HB = 4
    UNITS = [(g, t) for g in range(H // HU) for t in range(NT)]
    U = len(UNITS)
    with ExitStack() as ctx:
        def sb(name, shape, dt=F32):
            return ctx.enter_context(nc.sbuf_tensor("B_" + name, shape, dt))

        def psum(name, shape):
            return ctx.enter_context(nc.psum_tensor("B_" + name, shape, F32))

        wq, wk, wv, wo, bo = (w[k] for k in ("wq", "wk", "wv", "wo", "bo"))
        st = sb("st", [P, NT, 6])
        mv = sb("mv", [P, NT, 2])
        veps = sb("veps", [P, NT])
        rstd = sb("rstd", [P, NT])
        xn = sb("xn", [P, NT, D])
        xT = sb("xT", [P, KD, T])
        ctx_cur = sb("ctx_cur", [P, S])
        qT = sb("qT", [P, MT, T])
        kT = sb("kT", [P, MT, S])
        v = sb("v", [S, INNER])
        mx = sb("mx", [P, 2, HU])
        prob = sb("prob", [P, 2, HU * S])
        rsum = sb("rsum", [P, U, HU])
        rinv = sb("rinv", [P, U, HU])
        pT = sb("pT", [S, 2, HU, P])
        oT = sb("oT", [P, MT, T])
        ps_s = [psum(f"ps_s{i}", [P, 2, 512]) for i in range(2)]
        ps_p = [psum(f"ps_p{i}", [P, 512]) for i in range(2)]
        ps_m = [psum(f"ps_m{i}", [P, 512]) for i in range(2)]

        def sem(name):
            return ctx.enter_context(nc.semaphore("B_" + name))

        stats, stats_seen, aggr, var_eps, rstd_ready, xn_ready, resid_ready, ctx_ready = map(
            sem, "stats stats_seen aggr var_eps rstd_ready xn_ready resid_ready ctx_ready".split())
        s_done, pT_done, av_done, q_done, k_done, v_done, xT_done, w_done = map(
            sem, "s_done pT_done av_done q_done k_done v_done xT_done w_done".split())
        exp_ready, pT_ready, oT_ready, q_ready, k_ready, v_ready, xT_ready = map(
            sem, "exp_ready pT_ready oT_ready q_ready k_ready v_ready xT_ready".split())
        max_ready, sub_ready, sum_ready, inv_ready, prob_ready, res_ready = map(
            sem, "max_ready sub_ready sum_ready inv_ready prob_ready res_ready".split())

        block = ctx.enter_context(nc.Block())

        @block.gpsimd
        def _(pool):
            def norm_scale(b):
                pool.wait_ge(aggr, b + 1)
                nc.gpsimd.tensor_tensor(veps[:], mv[:, :, 1], eps[:], ALU.add).then_inc(var_eps, 1)
                pool.wait_ge(var_eps, b + 1)
                nc.gpsimd.tensor_tensor(rstd[:], veps[:], half[:], ALU.pow).then_inc(rstd_ready, 1)

            def keep_residual(b):
                pool.wait_ge(xn_ready, b + 1)
                for t in range(NT):
                    last = nc.gpsimd.tensor_tensor(res[:, b, t], xn[:, t], bo[:], ALU.add)
                last.then_inc(resid_ready, 1)

            def stage_context(b):
                pool.wait_ge(v_done, b * 2)
                nc.gpsimd.tensor_copy(ctx_cur[:], ctxT[:, b]).then_inc(ctx_ready, 1)

            pool.wait_ge(w_loaded, 80)
            pool.wait_ge(ctx_loaded, 16)
            with pool.Fori(0, B) as b:
                stage_context(b)
                norm_scale(b)
                keep_residual(b)

        @block.tensor
        def _(pe):
            def scores(b, n):
                g, t = UNITS[n]
                for h in range(HU):
                    r = h % 2 * HD
                    m = g * HU // 2 + h // 2
                    last = nc.tensor.matmul(ps_s[n % 2][:, h % 2, h // 2 * S:(h // 2 + 1) * S],
                                            qT[r:r + HD, m, t * P:(t + 1) * P], kT[r:r + HD, m],
                                            start=True, stop=True)
                last.then_inc(s_done, 1)

            def transpose_probs(b, n):
                pe.wait_ge(prob_ready, b * U + n + 1)
                for h in range(HU):
                    if h % HB == 0 and n % 2:
                        pe.wait_ge(pT_ready, b * 2 * U + 2 * n + h // HB - 1)
                    last = nc.tensor.transpose(ps_p[h // HB][0:S, h % HB * P:(h % HB + 1) * P],
                                               prob[:, n % 2, h * S:(h + 1) * S], ident[:])
                    if h % HB == HB - 1:
                        last.then_inc(pT_done, 1)

            def values(b, n, bank):
                pe.wait_ge(pT_ready, b * 2 * U + 2 * n + 2)
                for h in range(HU):
                    head = UNITS[n][0] * HU + h
                    r = h % 2 * HD
                    last = nc.tensor.matmul(ps_m[bank][r:r + HD, h // 2 * P:(h // 2 + 1) * P], v[:, head * HD:(head + 1) * HD],
                                            pT[:, n % 2, h % 2 * HB + h // 2], start=True, stop=True)
                last.then_inc(av_done, 1)

            def transpose_x(b, bank):
                pe.wait_ge(xn_ready, b + 1)
                for k in range(KD):
                    for t in range(NT):
                        last = nc.tensor.transpose(ps_m[bank][:, k * T + t * P:k * T + (t + 1) * P],
                                                   xn[:, t, k * P:(k + 1) * P], ident[:])
                last.then_inc(xT_done, 1)

            def project_q(b, c, bank):
                for m in range(2):
                    for k in range(KD):
                        last = nc.tensor.matmul(ps_m[bank][:, m * T:(m + 1) * T], wq[:, k, (2 * c + m) * P:(2 * c + m + 1) * P],
                                                xT[:, k], start=k == 0, stop=k == KD - 1)
                last.then_inc(q_done, 1)

            def project_k(b, c, bank):
                for m in range(HB):
                    last = nc.tensor.matmul(ps_m[bank][:, m * S:(m + 1) * S], wk[:, (HB * c + m) * P:(HB * c + m + 1) * P],
                                            ctx_cur[:], start=True, stop=True)
                last.then_inc(k_done, 1)

            def project_v(b, c, bank):
                nc.tensor.matmul(ps_m[bank][0:S], ctx_cur[:], wv[:, c * 512:(c + 1) * 512],
                                 start=True, stop=True).then_inc(v_done, 1)

            def project_out(b, t, bank):
                for m in range(MT):
                    last = nc.tensor.matmul(ps_m[bank][:, 0:D], oT[:, m, t * P:(t + 1) * P], wo[:, m],
                                            start=m == 0, stop=m == MT - 1)
                last.then_inc(w_done, 1)

            def body(b, more):
                nb = b + 1
                transpose_probs(b, 0)
                pe.wait_ge(sub_ready, b * U + 1)
                scores(b, 2)
                transpose_probs(b, 1)
                pe.wait_ge(sub_ready, b * U + 2)
                scores(b, 3)
                pe.wait_ge(res_ready, b * 2)
                if more:
                    pe.wait_ge(ctx_ready, nb + 1)
                    project_k(nb, 0, 0)
                    project_k(nb, 1, 1)
                    pe.wait_ge(k_ready, b * 2 + 3)
                values(b, 0, 0)
                if more:
                    pe.wait_ge(k_ready, b * 2 + 4)
                    transpose_x(nb, 1)
                pe.wait_ge(oT_ready, b * U + 1)
                values(b, 1, 0)
                transpose_probs(b, 2)
                if more:
                    pe.wait_ge(xT_ready, b + 2)
                    project_q(nb, 0, 1)
                transpose_probs(b, 3)
                pe.wait_ge(oT_ready, b * U + 2)
                if more:
                    project_q(nb, 1, 0)
                    pe.wait_ge(q_ready, b * U + 5)
                values(b, 2, 1)
                if more:
                    pe.wait_ge(q_ready, b * U + 6)
                    project_q(nb, 2, 0)
                pe.wait_ge(oT_ready, b * U + 3)
                values(b, 3, 1)
                if more:
                    pe.wait_ge(q_ready, b * U + 7)
                    project_q(nb, 3, 0)
                pe.wait_ge(oT_ready, b * U + 4)
                if more:
                    project_v(nb, 0, 1)
                    pe.wait_ge(q_ready, b * U + 8)
                    project_v(nb, 1, 0)
                    pe.wait_ge(sub_ready, b * U + 3)
                    scores(nb, 0)
                    pe.wait_ge(v_ready, b * 2 + 3)
                project_out(b, 0, 1)
                if more:
                    pe.wait_ge(sub_ready, b * U + 4)
                    scores(nb, 1)
                    pe.wait_ge(v_ready, b * 2 + 4)
                project_out(b, 1, 0)

            pe.wait_ge(w_loaded, 80)
            pe.wait_ge(ctx_ready, 1)
            project_k(0, 0, 0)
            project_k(0, 1, 1)
            pe.wait_ge(k_ready, 2)
            transpose_x(0, 1)
            pe.wait_ge(xT_ready, 1)
            project_q(0, 0, 0)
            project_q(0, 1, 1)
            pe.wait_ge(q_ready, 2)
            project_q(0, 2, 0)
            project_q(0, 3, 1)
            pe.wait_ge(q_ready, 4)
            project_v(0, 0, 0)
            project_v(0, 1, 1)
            scores(0, 0)
            scores(0, 1)
            pe.wait_ge(v_ready, 2)
            with pe.Fori(0, B - 1) as b:
                body(b, True)
            body(B - 1, False)

        @block.scalar
        def _(act):
            def copy_pT(b, n):
                for i in range(2):
                    act.wait_ge(pT_done, b * 2 * U + 2 * n + i + 1)
                    nc.scalar.activation(pT[:, n % 2, i * HB:(i + 1) * HB], ps_p[i][0:S], ACT.Copy).then_inc(pT_ready, 1)

            def exponential(b, n):
                act.wait_ge(sub_ready, b * U + n + 1)
                nc.scalar.activation(prob[:, n % 2], prob[:, n % 2], ACT.Exp, scale=HD ** -0.5).then_inc(exp_ready, 1)

            def copy_k(b, c, bank):
                act.wait_ge(k_done, b * 2 + c + 1)
                nc.scalar.activation(kT[:, c * HB:(c + 1) * HB], ps_m[bank][:, 0:HB * S], ACT.Copy).then_inc(k_ready, 1)

            def copy_x(b, bank):
                act.wait_ge(xT_done, b + 1)
                nc.scalar.activation(xT[:], ps_m[bank][:], ACT.Copy).then_inc(xT_ready, 1)

            def copy_q(b, c, bank):
                act.wait_ge(q_done, b * 4 + c + 1)
                nc.scalar.activation(qT[:, 2 * c:2 * c + 2], ps_m[bank][:], ACT.Copy).then_inc(q_ready, 1)

            def copy_v(b, c, bank):
                act.wait_ge(v_done, b * 2 + c + 1)
                nc.scalar.activation(v[:, c * 512:(c + 1) * 512], ps_m[bank][0:S], ACT.Copy).then_inc(v_ready, 1)

            def copy_oT(b, n, bank):
                g, t = UNITS[n]
                act.wait_ge(av_done, b * U + n + 1)
                nc.scalar.activation(oT[:, g * 4:(g + 1) * 4, t * P:(t + 1) * P],
                                     ps_m[bank][:].rearrange("p (c i) -> p c i", c=4), ACT.Copy).then_inc(oT_ready, 1)

            def body(b, more):
                nb = b + 1
                copy_pT(b, 0)
                copy_pT(b, 1)
                exponential(b, 2)
                if more:
                    copy_k(nb, 0, 0)
                    copy_k(nb, 1, 1)
                exponential(b, 3)
                copy_oT(b, 0, 0)
                if more:
                    copy_x(nb, 1)
                copy_oT(b, 1, 0)
                copy_pT(b, 2)
                if more:
                    copy_q(nb, 0, 1)
                copy_pT(b, 3)
                if more:
                    copy_q(nb, 1, 0)
                copy_oT(b, 2, 1)
                if more:
                    copy_q(nb, 2, 0)
                copy_oT(b, 3, 1)
                if more:
                    copy_q(nb, 3, 0)
                    copy_v(nb, 0, 1)
                    copy_v(nb, 1, 0)
                    exponential(nb, 0)
                    exponential(nb, 1)

            copy_k(0, 0, 0)
            copy_k(0, 1, 1)
            copy_x(0, 1)
            for c in range(4):
                copy_q(0, c, c % 2)
            copy_v(0, 0, 0)
            copy_v(0, 1, 1)
            exponential(0, 0)
            exponential(0, 1)
            with act.Fori(0, B - 1) as b:
                body(b, True)
            body(B - 1, False)

        @block.vector
        def _(dve):
            def norm_stats(b):
                for t in range(NT):
                    last = nc.vector.bn_stats(st[:, t], res[:, b, t])
                last.then_inc(stats, 1)
                dve.wait_ge(stats, b + 1)
                dve.sem_inc(stats_seen)
                for t in range(NT):
                    last = nc.vector.bn_aggr(mv[:, t], st[:, t])
                last.then_inc(aggr, 1)

            def norm_apply(b):
                dve.wait_ge(rstd_ready, b + 1)
                dve.wait_ge(xT_done, b)
                dve.wait_ge(resid_ready, b)
                for t in range(NT):
                    last = nc.vector.tensor_scalar(xn[:, t], res[:, b, t], mv[:, t, 0:1], rstd[:, t:t + 1],
                                                   ALU.subtract, ALU.mult)
                last.then_inc(xn_ready, 1)

            def shift(b, n):
                sc = ps_s[n % 2][:, :, 0:HB * S].rearrange("p a (h k) -> p a h k", k=S)
                m = mx[:, n % 2]
                dve.wait_ge(s_done, b * U + n + 1)
                nc.vector.tensor_reduce(m.rearrange("p (a h) -> p a h", a=2), sc, AX.X, ALU.max).then_inc(max_ready, 1)
                dve.wait_ge(max_ready, b * U + n + 1)
                nc.vector.tensor_tensor(prob[:, n % 2].rearrange("p (a h k) -> p a h k", a=2, k=S), sc,
                                        m.rearrange("p (a h) -> p a h", a=2).unsqueeze(3).to_broadcast([P, 2, HB, S]),
                                        ALU.subtract).then_inc(sub_ready, 1)

            def normalise(b, n):
                p = prob[:, n % 2].rearrange("p (h k) -> p h k", k=S)
                dve.wait_ge(exp_ready, b * U + n + 1)
                nc.vector.tensor_reduce(rsum[:, n], p, AX.X, ALU.add).then_inc(sum_ready, 1)
                dve.wait_ge(sum_ready, b * U + n + 1)
                nc.vector.reciprocal(rinv[:, n], rsum[:, n]).then_inc(inv_ready, 1)
                dve.wait_ge(inv_ready, b * U + n + 1)
                nc.vector.tensor_tensor(p, p, rinv[:, n].unsqueeze(2).to_broadcast([P, HU, S]), ALU.mult).then_inc(prob_ready, 1)

            def add_out(b, t, bank):
                dve.wait_ge(w_done, b * 2 + t + 1)
                nc.vector.tensor_tensor(res[:, b, t], res[:, b, t], ps_m[bank][:, 0:D], ALU.add).then_inc(res_ready, 1)

            def body(b, more):
                nb = b + 1
                dve.wait_ge(pT_done, b * 2 * U + 2)
                shift(b, 2)
                if more:
                    norm_stats(nb)
                dve.wait_ge(pT_done, b * 2 * U + 4)
                shift(b, 3)
                if more:
                    norm_apply(nb)
                normalise(b, 2)
                normalise(b, 3)
                if more:
                    dve.wait_ge(pT_done, b * 2 * U + 6)
                    shift(nb, 0)
                    normalise(nb, 0)
                dve.wait_ge(resid_ready, b + 1)
                add_out(b, 0, 1)
                if more:
                    dve.wait_ge(pT_done, b * 2 * U + 8)
                    shift(nb, 1)
                    normalise(nb, 1)
                add_out(b, 1, 0)

            norm_stats(0)
            norm_apply(0)
            shift(0, 0)
            shift(0, 1)
            normalise(0, 0)
            normalise(0, 1)
            with dve.Fori(0, B - 1) as b:
                body(b, True)
            body(B - 1, False)


def expert_ffn(nc, res, ident, half, idx_d, rw_d, wgu_d, bgu_d, wdn_d, bdn_d, prefetch):
    E, NTOK = wgu_d.shape[0], idx_d.shape[0]
    TI = NTOK // P
    NB = NTOK // T
    with ExitStack() as ctx:
        def sb(name, shape, dt=F32):
            return ctx.enter_context(nc.sbuf_tensor("C_" + name, shape, dt))

        def psum(name, shape):
            return ctx.enter_context(nc.psum_tensor("C_" + name, shape, F32))

        idx = sb("idx", [P, TI, 2], I32)
        idxf = sb("idxf", [P, TI, 2])
        rw = sb("rw", [P, TI, E])
        expert_no = sb("expert_no", [P, E])
        hit = sb("hit", [P, 2, TI, E])
        hits = sb("hits", [P, TI, E])
        coef = sb("coef", [P, TI, E])
        coefT = sb("coefT", [E, TI, P])
        bdn = sb("bdn", [E, D])
        bgu = sb("bgu", [P, E, 2 * KD])
        wgu = sb("wgu", [P, 2, KD, 2 * D])
        wdn = sb("wdn", [P, 2, KD, D])
        st = sb("st", [P, TI, 6])
        mv = sb("mv", [P, TI, 2])
        veps = sb("veps", [P, TI])
        rstd = sb("rstd", [P, TI])
        xn = sb("xn", [P, TI, D])
        xT = sb("xT", [P, KD, NTOK])
        gate = sb("gate", [P, KD, NTOK])
        up = sb("up", [P, KD, NTOK])
        sig = sb("sig", [P, KD, NTOK])
        inter = sb("inter", [P, KD, NTOK])
        ps_h = [psum(f"ps_h{i}", [P, NTOK]) for i in range(2 * KD)]
        ps_d = [psum(f"ps_d{i}", [P, 2, D]) for i in range(TI // 2)]

        def sem(name):
            return ctx.enter_context(nc.semaphore("C_" + name))

        in_loaded, gu_loaded0, gu_loaded1, dn_loaded0, dn_loaded1, step, stats, aggr, var_eps, rstd_ready, xn_ready = map(
            sem, "in_loaded gu_loaded0 gu_loaded1 dn_loaded0 dn_loaded1 step stats aggr var_eps rstd_ready xn_ready".split())
        xT_done, xT_ready, coef_ready, cT_done, cT_ready, bias_done, acc_init = map(
            sem, "xT_done xT_ready coef_ready cT_done cT_ready bias_done acc_init".split())
        h_done, h_read, sig_ready, inter_step, inter_ready, d_done, d_read = map(
            sem, "h_done h_read sig_ready inter_step inter_ready d_done d_read".split())
        gu_loaded, dn_loaded = (gu_loaded0, gu_loaded1), (dn_loaded0, dn_loaded1)

        block = ctx.enter_context(nc.Block())

        @block.sync
        def _(sp):
            sp.dma_start(idx[:], idx_d.rearrange("(t p) k -> p t k", p=P)).then_inc(in_loaded, 16)
            sp.dma_start(rw[:], rw_d.rearrange("(t p) e -> p t e", p=P)).then_inc(in_loaded, 16)
            sp.dma_start(bdn[:], bdn_d).then_inc(in_loaded, 16)
            sp.dma_start(bgu[:], bgu_d).then_inc(in_loaded, 16)

            def load_gu(e, u):
                sp.dma_start(wgu[:, u], wgu_d[e].rearrange("(k p) n -> p k n", p=P)).then_inc(gu_loaded[u], 16)

            def load_dn(e, u):
                sp.dma_start(wdn[:, u], wdn_d[e].rearrange("(k p) n -> p k n", p=P)).then_inc(dn_loaded[u], 16)

            def refill(e, u, gu=True):
                if gu:
                    sp.wait_ge(h_done, (e + 1) * 2 * KD)
                    load_gu(e + 2, u)
                sp.wait_ge(d_done, e * TI)
                load_dn(e + 1, 1 - u)
            load_gu(0, 0)
            load_gu(1, 1)
            load_dn(0, 0)
            load_dn(1, 1)
            sp.wait_ge(h_done, 2 * KD)
            load_gu(2, 0)
            with sp.Fori(0, E // 2 - 2) as j:
                refill(j * 2 + 1, 1)
                refill(j * 2 + 2, 0)
            refill(E - 3, 1)
            refill(E - 2, 0, gu=False)
            prefetch(sp)

        @block.gpsimd
        def _(pool):
            nc.gpsimd.iota(hits[:, 0].bitcast(I32), [[1, E]], base=0, channel_multiplier=0).then_inc(step, 1)
            pool.wait_ge(step, 1)
            nc.gpsimd.tensor_copy(expert_no[:], hits[:, 0].bitcast(I32)).then_inc(step, 1)
            pool.wait_ge(aggr, 1)
            nc.gpsimd.tensor_scalar(veps[:], mv[:, :, 1], 1e-5, None, ALU.add).then_inc(var_eps, 1)
            pool.wait_ge(var_eps, 1)
            for i in range(TI // NT):
                last = nc.gpsimd.tensor_tensor(rstd[:, i * NT:(i + 1) * NT], veps[:, i * NT:(i + 1) * NT], half[:], ALU.pow)
            last.then_inc(rstd_ready, 1)

        @block.tensor
        def _(pe):
            pe.wait_ge(xn_ready, 1)
            for k in range(KD):
                for t in range(TI):
                    last = nc.tensor.transpose(ps_h[k][:, t * P:(t + 1) * P], xn[:, t, k * P:(k + 1) * P], ident[:])
            last.then_inc(xT_done, 1)
            pe.wait_ge(coef_ready, 1)
            for t in range(TI):
                last = nc.tensor.transpose(ps_h[2][0:E, t * P:(t + 1) * P], coef[:, t], ident[:])
            last.then_inc(cT_done, 1)
            pe.wait_ge(cT_ready, 1)
            for t in range(TI):
                last = nc.tensor.matmul(ps_d[t // 2][:, t % 2], coefT[:, t], bdn[:], start=True, stop=True)
            last.then_inc(bias_done, 1)
            pe.wait_ge(xT_ready, 1)

            def hidden(e, u, first=False):
                for m in range(2 * KD):
                    if not first:
                        pe.wait_ge(h_read, e * 2 * KD + (m + 1 - 2 * KD))
                    for k in range(KD):
                        last = nc.tensor.matmul(ps_h[m][:], wgu[:, u, k, m * P:(m + 1) * P], xT[:, k], start=k == 0, stop=k == KD - 1)
                    last.then_inc(h_done, 1)

            def down(e, u, first=False):
                pe.wait_ge(inter_ready, e + 1)
                for t in range(TI):
                    if t % 2 == 0 and not first:
                        pe.wait_ge(d_read, e * TI + (t + 2 - TI))
                    for k in range(KD):
                        last = nc.tensor.matmul(ps_d[t // 2][:, t % 2], inter[:, k, t * P:(t + 1) * P], wdn[:, u, k],
                                                start=k == 0, stop=k == KD - 1)
                    last.then_inc(d_done, 1)

            pe.wait_ge(gu_loaded[0], 16)
            hidden(0, 0, first=True)
            pe.wait_ge(acc_init, 1)
            pe.wait_ge(gu_loaded[1], 16)
            hidden(1, 1)
            pe.wait_ge(dn_loaded[0], 16)
            down(0, 0, first=True)
            with pe.Fori(0, E // 2 - 1) as j:
                pe.wait_ge(gu_loaded[0], j * 16 + 32)
                hidden(j * 2 + 2, 0)
                pe.wait_ge(dn_loaded[1], j * 16 + 16)
                down(j * 2 + 1, 1)
                pe.wait_ge(gu_loaded[1], j * 16 + 32)
                hidden(j * 2 + 3, 1)
                pe.wait_ge(dn_loaded[0], j * 16 + 32)
                down(j * 2 + 2, 0)
            pe.wait_ge(dn_loaded[1], E // 2 * 16)
            down(E - 1, 1)

        @block.scalar
        def _(act):
            act.wait_ge(xT_done, 1)
            for k in range(KD):
                last = nc.scalar.activation(xT[:, k], ps_h[k][:], ACT.Copy)
            last.then_inc(xT_ready, 1)
            act.wait_ge(cT_done, 1)
            nc.scalar.activation(coefT[:], ps_h[2][0:E].rearrange("e (t p) -> e t p", p=P), ACT.Copy).then_inc(cT_ready, 1)
            with act.Fori(0, E) as e:
                act.wait_ge(h_read, e * 2 * KD + KD)
                nc.scalar.activation(sig[:], gate[:], ACT.Sigmoid, scale=1.702).then_inc(sig_ready, 1)

        @block.vector
        def _(dve):
            for t in range(TI):
                last = nc.vector.bn_stats(st[:, t], res[:, t // NT, t % NT])
            last.then_inc(stats, 1)
            dve.wait_ge(stats, 1)
            for t in range(TI):
                last = nc.vector.bn_aggr(mv[:, t], st[:, t])
            last.then_inc(aggr, 1)
            dve.wait_ge(rstd_ready, 1)
            for t in range(TI):
                last = nc.vector.tensor_scalar(xn[:, t], res[:, t // NT, t % NT], mv[:, t, 0:1], rstd[:, t:t + 1],
                                               ALU.subtract, ALU.mult)
            last.then_inc(xn_ready, 1)
            dve.wait_ge(in_loaded, 64)
            nc.vector.tensor_copy(idxf[:], idx[:]).then_inc(step, 1)
            dve.wait_ge(step, 3)
            for k in range(2):
                last = nc.vector.tensor_tensor(hit[:, k], idxf[:, :, k].unsqueeze(2).to_broadcast([P, TI, E]),
                                               expert_no[:].unsqueeze(1).to_broadcast([P, TI, E]), ALU.is_equal)
            last.then_inc(step, 1)
            dve.wait_ge(step, 4)
            nc.vector.tensor_tensor(hits[:], hit[:, 0], hit[:, 1], ALU.add).then_inc(step, 1)
            dve.wait_ge(step, 5)
            nc.vector.tensor_tensor(coef[:], hits[:], rw[:], ALU.mult).then_inc(coef_ready, 1)
            dve.wait_ge(bias_done, 1)
            dve.wait_ge(xn_ready, 1)
            for i in range(NB):
                last = nc.vector.tensor_tensor(res[:, i], xn[:, i * NT:(i + 1) * NT], ps_d[i][:], ALU.add)
            last.then_inc(acc_init, 1)
            dve.wait_ge(acc_init, 1)

            def swiglu(e):
                for m in range(2 * KD):
                    if m == KD:
                        dve.wait_ge(inter_ready, e)
                    dve.wait_ge(h_done, e * 2 * KD + m + 1)
                    nc.vector.tensor_scalar((gate if m < KD else up)[:, m % KD], ps_h[m][:], bgu[:, e, m:m + 1], 7.0,
                                            ALU.add, ALU.min).then_inc(h_read, 1)
                dve.wait_ge(h_read, e * 2 * KD + 2 * KD)
                nc.vector.tensor_scalar(up[:], up[:], -7.0, 1.0, ALU.max, ALU.add).then_inc(inter_step, 1)
                dve.wait_ge(inter_step, e * 2 + 1)
                nc.vector.tensor_tensor(up[:], up[:], gate[:], ALU.mult).then_inc(inter_step, 1)
                dve.wait_ge(inter_step, e * 2 + 2)
                dve.wait_ge(sig_ready, e + 1)
                dve.wait_ge(d_done, e * TI)
                nc.vector.tensor_tensor(inter[:], up[:], sig[:], ALU.mult).then_inc(inter_ready, 1)

            def accumulate(e):
                for t in range(TI):
                    r = res[:, t // NT, t % NT]
                    if t == 0:
                        dve.wait_ge(d_read, e * TI)
                    dve.wait_ge(d_done, e * TI + 2 * (t // 2) + 2)
                    nc.vector.scalar_tensor_tensor(r, ps_d[t // 2][:, t % 2], coef[:, t, bass.ds(e, 1)], r,
                                                   ALU.mult, ALU.add).then_inc(d_read, 1)

            swiglu(0)
            with dve.Fori(0, E - 1) as e:
                swiglu(e + 1)
                accumulate(e)
            accumulate(E - 1)


RET_H, RET_D = 16, 16
RET_U = 4


def retention_head(p):
    r, rg, half, e = p // 8, p // 4 % 2, p // 2 % 2, p % 2
    return half * 8 + (2 * r + rg) * 2 + e


RET_LOADS = 10


def retention_weights(nc, ctx):
    shapes = {"wqk": [P, KD, 2 * D], "wvg": [P, KD, 2 * D], "wgt": [P, KD, RET_H], "wo": [P, KD, D], "upto": [P, P],
              "after": [P, P], "head_mask": [P, 2], "block_mask": [P, P], "sel": [P, RET_H, P], "nsel": [P, RET_H, P]}
    w = {k: ctx.enter_context(nc.sbuf_tensor("D_" + k, shape, BF16 if k in ("sel", "nsel") else F32)) for k, shape in shapes.items()}
    return w, ctx.enter_context(nc.semaphore("D_w_loaded"))


def load_retention_weights(sp, w, w_loaded, i):
    for name in ("wqk", "wvg", "wgt", "wo"):
        sp.dma_start(w[name][:], i["L1_attn_" + name].rearrange("(k p) n -> p k n", p=P)).then_inc(w_loaded, 16)
    for name in ("upto", "after", "head_mask", "block_mask", "sel", "nsel"):
        sp.dma_start(w[name][:], i[name]).then_inc(w_loaded, 16)


def gated_retention(nc, res, ident, half, eps, w, w_loaded, prefetch):
    H, HD, U = RET_H, RET_D, RET_U
    HT = H // 2
    with ExitStack() as ctx:
        def sb(name, shape, dt=F32):
            return ctx.enter_context(nc.sbuf_tensor("D_" + name, shape, dt))

        def psum(name, shape):
            return ctx.enter_context(nc.psum_tensor("D_" + name, shape, F32))

        wqk, wvg, wgt, wo, upto, after, head_mask, block_mask, sel, nsel = (w[k] for k in (
            "wqk", "wvg", "wgt", "wo",
            "upto",
            "after",
            "head_mask",
            "block_mask",
            "sel",
            "nsel"))
        st = sb("st", [P, NT, 6])
        mv = sb("mv", [P, NT, 2])
        veps = sb("veps", [P, NT])
        r1 = sb("r1", [P, NT])
        r1sq = sb("r1sq", [P, NT])
        var1 = sb("var1", [P, NT])
        var1_eps = sb("var1_eps", [P, NT])
        r2 = sb("r2", [P, NT])
        rstd = sb("rstd", [P, NT])
        xn = sb("xn", [P, NT, D])
        xT = sb("xT", [P, KD, T])
        qk = sb("qk", [P, NT, 2, D])
        v_raw = sb("v_raw", [P, NT, D])
        g_raw = sb("g_raw", [P, NT, D])
        v = sb("v", [P, NT, D])
        sq = sb("sq", [P, 3, NT, D])
        ssq = sb("ssq", [P, 3, NT])
        msq = sb("msq", [P, 3, NT])
        half6 = sb("half6", [P, 3, NT])
        half32 = sb("half32", [P, NT, H])
        rms = sb("rms", [P, 3, NT])
        za = sb("za", [P, NT, H])
        zm = sb("zm", [P, NT, H])
        ze = sb("ze", [P, NT, H])
        zl = sb("zl", [P, NT, H])
        ld = sb("ld", [P, NT, 4, 32])
        dec = sb("dec", [P, 2, H])
        F = sb("F", [P, NT, P], BF16)
        Fr = sb("Fr", [P, NT, P])
        q2T = sb("q2T", [P, NT, 2, 2, P])
        kT = sb("kT", [P, NT, 2, P])
        qd = sb("qd", [P, D])
        kd = sb("kd", [P, D])
        qdT = sb("qdT", [P, 2, P])
        state = sb("state", [P, 2, P])
        dexp = sb("dexp", [P, 2, HT * P])
        att = sb("att", [P, 2, HT, P])
        o_raw = sb("o_raw", [P, NT, D])
        osq = sb("osq", [P, NT, H, HD])
        oss = sb("oss", [P, NT, H])
        oms = sb("oms", [P, NT, H])
        orms = sb("orms", [P, NT, H])
        eg = sb("eg", [P, NT, D])
        sg = sb("sg", [P, NT, D])
        y = sb("y", [P, NT, D])
        yT = sb("yT", [P, KD, T])
        ps_e = psum("ps_e", [P, 2, 512])
        ps_s = psum("ps_s", [P, 2, 512])
        ps_f = [psum(f"ps_f{i}", [P, 512]) for i in range(2)]
        ps_c = psum("ps_c", [P, 512])
        ps_o = psum("ps_o", [P, NT, D])
        c_bc, c_bcT, c_z = ps_c[:, 0:2 * H], ps_c[:, 64:64 + T], ps_c[:, 384:384 + NT * H]

        def sem(name):
            return ctx.enter_context(nc.semaphore("D_" + name))

        set_ready, stats, seen, aggr, var_eps, rstd_ready, xn_ready, resid_ready = map(
            sem, "set_ready stats seen aggr var_eps rstd_ready xn_ready resid_ready".split())
        xT_done, qk_done, vg_done, z_done, bc_done, bcT_done, qkT_done, qdT_done = map(
            sem, "xT_done qk_done vg_done z_done bc_done bcT_done qkT_done qdT_done".split())
        e_done, s_done, st_done, av_done, yT_done, w_done = map(
            sem, "e_done s_done st_done av_done yT_done w_done".split())
        xT_ready, qk_raw, vg_raw, ssq_ready, ze_ready, zl_ready, dec_ready, qkT_ready, qdT_ready = map(
            sem, "xT_ready qk_raw vg_raw ssq_ready ze_ready zl_ready dec_ready qkT_ready qdT_ready".split())
        exp_ready, osq_ready, o_ready, eg_ready, yT_ready, norm_step = map(
            sem, "exp_ready osq_ready o_ready eg_ready yT_ready norm_step".split())
        z_step, z_ready, ld_ready, f_step, f_ready, qk_ready, v_ready, att_raw, state_ready, oss_ready = map(
            sem, "z_step z_ready ld_ready f_step f_ready qk_ready v_ready att_raw state_ready oss_ready".split())
        y_step, y_ready, sg_step, sg_ready, res_ready = map(sem, "y_step y_ready sg_step sg_ready res_ready".split())
        msq_ready, rms_ready, kqd_ready, att_ready, oms_ready, orms_ready = map(
            sem, "msq_ready rms_ready kqd_ready att_ready oms_ready orms_ready".split())

        block = ctx.enter_context(nc.Block())

        def steps(engine, body):
            body(0, prev=False, nxt=True, nxt2=True)
            with engine.Fori(1, B - 2) as b:
                body(b, prev=True, nxt=True, nxt2=True)
            body(B - 2, prev=True, nxt=True, nxt2=False)
            body(B - 1, prev=True, nxt=False, nxt2=False)

        @block.sync
        def _(sp):
            prefetch(sp)
        LOADED = 16 * RET_LOADS

        @block.gpsimd
        def _(pool):
            def norm_scale(b, double):
                pool.wait_ge(aggr, b + 1)
                nc.gpsimd.tensor_tensor(veps[:], mv[:, :, 1], eps[:], ALU.add).then_inc(var_eps, 1)
                pool.wait_ge(var_eps, b + 1)
                if not double:
                    nc.gpsimd.tensor_tensor(rstd[:], veps[:], half[:], ALU.pow).then_inc(rstd_ready, 1)
                    return
                n = (b - 2) * 5
                nc.gpsimd.tensor_tensor(r1[:], veps[:], half[:], ALU.pow).then_inc(norm_step, 1)
                pool.wait_ge(norm_step, n + 1)
                nc.gpsimd.tensor_tensor(r1sq[:], r1[:], r1[:], ALU.mult).then_inc(norm_step, 1)
                pool.wait_ge(norm_step, n + 2)
                nc.gpsimd.tensor_tensor(var1[:], r1sq[:], mv[:, :, 1], ALU.mult).then_inc(norm_step, 1)
                pool.wait_ge(norm_step, n + 3)
                nc.gpsimd.tensor_tensor(var1_eps[:], var1[:], eps[:], ALU.add).then_inc(norm_step, 1)
                pool.wait_ge(norm_step, n + 4)
                nc.gpsimd.tensor_tensor(r2[:], var1_eps[:], half[:], ALU.pow).then_inc(norm_step, 1)
                pool.wait_ge(norm_step, n + 5)
                nc.gpsimd.tensor_tensor(rstd[:], r1[:], r2[:], ALU.mult).then_inc(rstd_ready, 1)

            def keep_residual(b):
                pool.wait_ge(xn_ready, b + 1)
                nc.gpsimd.tensor_copy(res[:, b], xn[:]).then_inc(resid_ready, 1)

            def qkv_scale(b):
                pool.wait_ge(ssq_ready, b * 6 + 6)
                pool.sem_inc(seen)
                nc.gpsimd.tensor_scalar(msq[:], ssq[:], 1.0 / D, 1e-6, ALU.mult, ALU.add).then_inc(msq_ready, 1)
                pool.wait_ge(msq_ready, b + 1)
                nc.gpsimd.tensor_tensor(rms[:], msq[:], half6[:], ALU.pow).then_inc(rms_ready, 1)

            def decayed(b):
                pool.wait_ge(qk_ready, b + 1)
                pool.wait_ge(dec_ready, b + 1)
                for dst, c, w, n in ((qd, 1, 0, 0), (kd, 0, 1, 1)):
                    last = nc.gpsimd.tensor_tensor(dst[:].rearrange("p (h d) -> p h d", d=HD),
                                                   qk[:, c, w].rearrange("p (h d) -> p h d", d=HD),
                                                   dec[:, n].unsqueeze(2).to_broadcast([P, H, HD]), ALU.mult)
                last.then_inc(kqd_ready, 1)

            def causal(b, n):
                pool.wait_ge(att_raw, b * U + n + 1)
                pool.sem_inc(seen)
                nc.gpsimd.affine_select(out=att[:, n % 2], in_=att[:, n % 2], compare_op=ALU.is_ge, fill=0.0, base=0,
                                        pattern=[[0, HT], [1, P]], channel_multiplier=-1).then_inc(att_ready, 1)

            def out_scale(b):
                pool.wait_ge(oss_ready, b + 1)
                pool.sem_inc(seen)
                nc.gpsimd.tensor_scalar(oms[:], oss[:], 1.0 / HD, 1e-6, ALU.mult, ALU.add).then_inc(oms_ready, 1)
                pool.wait_ge(oms_ready, b + 1)
                nc.gpsimd.tensor_tensor(orms[:], oms[:], half32[:], ALU.pow).then_inc(orms_ready, 1)

            def body(b, prev, nxt, nxt2):
                if prev:
                    out_scale(b - 1)
                causal(b, 0)
                if nxt2:
                    norm_scale(b + 2, True)
                causal(b, 1)
                if nxt2:
                    keep_residual(b + 2)
                causal(b, 2)
                if nxt:
                    qkv_scale(b + 1)
                causal(b, 3)
                if nxt:
                    pool.wait_ge(st_done, b + 1)
                    decayed(b + 1)

            for i in range(3):
                nc.gpsimd.memset(half6[:, i], -0.5)
            nc.gpsimd.memset(half32[:], -0.5)
            nc.gpsimd.memset(ld[:], 0.0).then_inc(set_ready, 1)
            for b in range(2):
                norm_scale(b, False)
                keep_residual(b)
            qkv_scale(0)
            decayed(0)
            steps(pool, body)
            out_scale(B - 1)

        @block.tensor
        def _(pe):
            def transpose_x(b):
                pe.wait_ge(xn_ready, b + 1)
                for k in range(KD):
                    for t in range(NT):
                        last = nc.tensor.transpose(ps_f[0][:, k * T + t * P:k * T + (t + 1) * P],
                                                   xn[:, t, k * P:(k + 1) * P], ident[:])
                last.then_inc(xT_done, 1)

            def project(b, t, w, bank, done):
                for k in range(KD):
                    last = nc.tensor.matmul(ps_f[bank][:], xT[:, k, t * P:(t + 1) * P], w[:, k], start=k == 0, stop=k == KD - 1)
                last.then_inc(done, 1)

            def gates(b):
                for t in range(NT):
                    for k in range(KD):
                        last = nc.tensor.matmul(c_z[:, t * H:(t + 1) * H], xT[:, k, t * P:(t + 1) * P], wgt[:, k],
                                                start=k == 0, stop=k == KD - 1)
                last.then_inc(z_done, 1)

            def running_sums(b):
                pe.wait_ge(ld_ready, b + 1)
                nc.tensor.matmul(c_bc[:, 0:H], upto[:], ld[:, 1, 0, 0:H], start=True, stop=True)
                nc.tensor.matmul(c_bc[:, H:2 * H], after[:], ld[:, 0, 0, 0:H], start=True, stop=True).then_inc(bc_done, 1)
                for c in range(NT):
                    last = nc.tensor.matmul(c_bcT[:, c * P:(c + 1) * P], ld[:, c].rearrange("p s h -> p (s h)"), upto[:],
                                            start=True, stop=True)
                last.then_inc(bcT_done, 1)

            def transpose_qk(b, c, bank):
                pe.wait_ge(qk_ready, b + 1)
                for w in range(2):
                    for hf in range(2):
                        last = nc.tensor.transpose(ps_f[bank][:, (w * 2 + hf) * P:(w * 2 + hf + 1) * P],
                                                   qk[:, c, w, hf * P:(hf + 1) * P], ident[:])
                last.then_inc(qkT_done, 1)

            def transpose_qd(b):
                pe.wait_ge(kqd_ready, b + 1)
                for hf in range(2):
                    last = nc.tensor.transpose(ps_f[1][:, hf * P:(hf + 1) * P], qd[:, hf * P:(hf + 1) * P], ident[:])
                last.then_inc(qdT_done, 1)

            def exponents(b, n):
                c, r = n // 2, n % 2
                for bank in range(2):
                    pl = r * HT + bank * 4
                    nc.tensor.matmul(ps_e[:, bank], F[:, c], nsel[:, pl:pl + 4], start=True, stop=False)
                    for i in range(4):
                        last = nc.tensor.matmul(ps_e[:, bank, i * P:(i + 1) * P], sel[:, pl + i], F[:, c], start=False, stop=i == 3)
                last.then_inc(e_done, 1)

            def products(b, n):
                c, r = n // 2, n % 2
                for bank in range(2):
                    rows = slice(32 * (2 * r + bank), 32 * (2 * r + bank) + 32)
                    for hf in range(2):
                        last = nc.tensor.matmul(ps_s[:, bank, hf * T:(hf + 1) * T], kT[rows, c, hf],
                                                q2T[rows, c, hf].rearrange("p e i -> p (e i)"), start=True, stop=True)
                last.then_inc(s_done, 1)

            def values(b, n):
                c, r = n // 2, n % 2
                pe.wait_ge(att_ready, b * U + n + 1)
                for i in range(HT):
                    h = retention_head(r * HT + i)
                    last = nc.tensor.matmul(ps_o[:, c, h * HD:(h + 1) * HD], att[:, n % 2, i], v[:, c, h * HD:(h + 1) * HD],
                                            start=n == 0 and i == 0, stop=n == U - 1 and i == HT - 1, skip_group_check=True)
                last.then_inc(av_done, 1)

            def state_update(b):
                for hf in range(2):
                    last = nc.tensor.matmul(ps_f[0][:, hf * P:(hf + 1) * P], kd[:, hf * P:(hf + 1) * P], v[:, 0, hf * P:(hf + 1) * P],
                                            start=True, stop=True)
                last.then_inc(st_done, 1)

            def cross(b):
                pe.wait_ge(state_ready, b + 1)
                for hf in range(2):
                    nc.tensor.matmul(ps_o[:, 1, hf * P:(hf + 1) * P], qdT[:, hf], state[:, hf], start=False, stop=False,
                                     skip_group_check=True)

            def transpose_y(b):
                pe.wait_ge(y_ready, b + 1)
                for k in range(KD):
                    for t in range(NT):
                        last = nc.tensor.transpose(ps_f[0][:, k * T + t * P:k * T + (t + 1) * P],
                                                   y[:, t, k * P:(k + 1) * P], ident[:])
                last.then_inc(yT_done, 1)

            def project_out(b):
                pe.wait_ge(yT_ready, b + 1)
                for t in range(NT):
                    for k in range(KD):
                        last = nc.tensor.matmul(ps_f[0][:, t * D:(t + 1) * D], yT[:, k, t * P:(t + 1) * P], wo[:, k],
                                                start=k == 0, stop=k == KD - 1)
                last.then_inc(w_done, 1)

            def body(b, prev, nxt, nxt2):
                nb = b + 1
                pe.wait_ge(f_ready, b + 1)
                exponents(b, 0)
                pe.wait_ge(qkT_ready, b * 2 + 2)
                products(b, 0)
                if nxt:
                    transpose_x(nb)
                pe.wait_ge(exp_ready, b * U + 1)
                exponents(b, 1)
                if nxt:
                    pe.wait_ge(xT_ready, nb + 1)
                    project(nb, 0, wqk, 0, qk_done)
                    pe.wait_ge(dec_ready, b + 1)
                    gates(nb)
                pe.wait_ge(att_raw, b * U + 1)
                products(b, 1)
                pe.wait_ge(qdT_ready, b + 1)
                if nxt:
                    project(nb, 1, wqk, 1, qk_done)
                pe.wait_ge(v_ready, b + 1)
                if prev:
                    pe.wait_ge(o_ready, b)
                values(b, 0)
                pe.wait_ge(exp_ready, b * U + 2)
                exponents(b, 2)
                if nxt:
                    pe.wait_ge(qk_raw, b * 2 + 3)
                    project(nb, 0, wvg, 0, vg_done)
                pe.wait_ge(att_raw, b * U + 2)
                products(b, 2)
                values(b, 1)
                if nxt:
                    pe.wait_ge(qk_raw, b * 2 + 4)
                    project(nb, 1, wvg, 1, vg_done)
                    running_sums(nb)
                if prev:
                    if nxt:
                        pe.wait_ge(vg_raw, b * 2 + 3)
                    transpose_y(b - 1)
                pe.wait_ge(exp_ready, b * U + 3)
                exponents(b, 3)
                pe.wait_ge(att_raw, b * U + 3)
                products(b, 3)
                if prev:
                    project_out(b - 1)
                values(b, 2)
                pe.wait_ge(kqd_ready, b + 1)
                if prev:
                    pe.wait_ge(res_ready, b)
                elif nxt:
                    pe.wait_ge(vg_raw, b * 2 + 3)
                state_update(b)
                if nxt:
                    pe.wait_ge(vg_raw, b * 2 + 4)
                    transpose_qk(nb, 0, 1)
                cross(b)
                values(b, 3)
                if nxt:
                    transpose_qk(nb, 1, 0)
                    pe.wait_ge(qkT_ready, b * 2 + 3)
                    transpose_qd(nb)

            pe.wait_ge(w_loaded, LOADED)
            pe.wait_ge(set_ready, 1)
            transpose_x(0)
            pe.wait_ge(xT_ready, 1)
            project(0, 0, wqk, 0, qk_done)
            project(0, 1, wqk, 1, qk_done)
            pe.wait_ge(qk_raw, 1)
            project(0, 0, wvg, 0, vg_done)
            pe.wait_ge(qk_raw, 2)
            project(0, 1, wvg, 1, vg_done)
            gates(0)
            running_sums(0)
            pe.wait_ge(vg_raw, 2)
            transpose_qk(0, 0, 1)
            transpose_qk(0, 1, 0)
            pe.wait_ge(qkT_ready, 1)
            transpose_qd(0)
            steps(pe, body)
            transpose_y(B - 1)
            project_out(B - 1)

        @block.scalar
        def _(act):
            def exponential(b, n):
                act.wait_ge(e_done, b * U + n + 1)
                nc.scalar.activation(dexp[:, n % 2], ps_e[:].rearrange("p a n -> p (a n)"), ACT.Exp).then_inc(exp_ready, 1)

            def copy_x(b):
                act.wait_ge(xT_done, b + 1)
                nc.scalar.activation(xT[:].rearrange("p k t -> p (k t)"), ps_f[0][:], ACT.Copy).then_inc(xT_ready, 1)

            def copy_qk(b, t):
                act.wait_ge(qk_done, b * 2 + t + 1)
                nc.scalar.activation(qk[:, t].rearrange("p w d -> p (w d)"), ps_f[t][:], ACT.Copy).then_inc(qk_raw, 1)

            def squares_qk(b, t):
                act.wait_ge(qk_raw, b * 2 + t + 1)
                for w in range(2):
                    nc.scalar.activation(sq[:, w, t], qk[:, t, w], ACT.Square, accum_out=ssq[:, w, t:t + 1]).then_inc(ssq_ready, 1)

            def copy_vg(b, t):
                act.wait_ge(vg_done, b * 2 + t + 1)
                nc.scalar.activation(v_raw[:, t], ps_f[t][:, 0:D], ACT.Copy)
                nc.scalar.activation(g_raw[:, t], ps_f[t][:, D:2 * D], ACT.Copy).then_inc(vg_raw, 1)

            def squares_v(b, t):
                act.wait_ge(vg_raw, b * 2 + t + 1)
                nc.scalar.activation(sq[:, 2, t], v_raw[:, t], ACT.Square, accum_out=ssq[:, 2, t:t + 1]).then_inc(ssq_ready, 1)

            def softplus(b):
                act.wait_ge(z_ready, b + 1)
                nc.scalar.activation(ze[:], za[:], ACT.Exp, scale=-1.0).then_inc(ze_ready, 1)
                act.wait_ge(ze_ready, b + 1)
                nc.scalar.activation(zl[:], ze[:], ACT.Ln, bias=1.0).then_inc(zl_ready, 1)

            def border_decay(b):
                act.wait_ge(bcT_done, b + 1)
                nc.scalar.activation(dec[:].rearrange("p n h -> p (n h)"), c_bc, ACT.Exp).then_inc(dec_ready, 1)

            def copy_qkT(b, c, bank):
                act.wait_ge(qkT_done, b * 2 + c + 1)
                ps = ps_f[bank][:].rearrange("p (w f i) -> p w f i", w=2, f=2)
                for e in range(2):
                    nc.scalar.activation(q2T[:, c, :, e], ps[:, 0], ACT.Copy, scale=head_mask[:, e:e + 1])
                nc.scalar.activation(kT[:, c], ps[:, 1], ACT.Copy).then_inc(qkT_ready, 1)

            def copy_qdT(b):
                act.wait_ge(qdT_done, b + 1)
                nc.scalar.activation(qdT[:].rearrange("p f i -> p (f i)"), ps_f[1][:, 0:2 * P], ACT.Copy).then_inc(qdT_ready, 1)

            def out_squares(b):
                act.wait_ge(av_done, b * U + U)
                nc.scalar.activation(osq[:].rearrange("p t h d -> p (t h d)"), ps_o[:].rearrange("p t d -> p (t d)"),
                                     ACT.Square).then_inc(osq_ready, 1)

            def copy_o(b):
                nc.scalar.activation(o_raw[:].rearrange("p t d -> p (t d)"), ps_o[:].rearrange("p t d -> p (t d)"),
                                     ACT.Copy).then_inc(o_ready, 1)

            def gate_exp(b):
                nc.scalar.activation(eg[:], g_raw[:], ACT.Exp, scale=-1.0).then_inc(eg_ready, 1)

            def copy_y(b):
                act.wait_ge(yT_done, b + 1)
                nc.scalar.activation(yT[:].rearrange("p k t -> p (k t)"), ps_f[0][:], ACT.Copy).then_inc(yT_ready, 1)

            def body(b, prev, nxt, nxt2):
                nb = b + 1
                if prev:
                    out_squares(b - 1)
                    copy_o(b - 1)
                exponential(b, 0)
                if nxt:
                    copy_x(nb)
                exponential(b, 1)
                act.wait_ge(vg_raw, b * 2 + 2)
                gate_exp(b)
                if nxt:
                    act.wait_ge(kqd_ready, b + 1)
                    copy_qk(nb, 0)
                    squares_qk(nb, 0)
                    copy_qk(nb, 1)
                    softplus(nb)
                act.wait_ge(att_raw, b * U + 1)
                exponential(b, 2)
                if nxt:
                    squares_qk(nb, 1)
                    act.wait_ge(sg_ready, b + 1)
                    copy_vg(nb, 0)
                    squares_v(nb, 0)
                    copy_vg(nb, 1)
                    squares_v(nb, 1)
                    border_decay(nb)
                if prev:
                    copy_y(b - 1)
                act.wait_ge(att_raw, b * U + 2)
                exponential(b, 3)
                if nxt:
                    copy_qkT(nb, 0, 1)
                    copy_qkT(nb, 1, 0)
                    copy_qdT(nb)

            act.wait_ge(w_loaded, LOADED)
            copy_x(0)
            for t in range(NT):
                copy_qk(0, t)
                squares_qk(0, t)
            for t in range(NT):
                copy_vg(0, t)
                squares_v(0, t)
            softplus(0)
            border_decay(0)
            copy_qkT(0, 0, 1)
            copy_qkT(0, 1, 0)
            copy_qdT(0)
            steps(act, body)
            out_squares(B - 1)
            copy_o(B - 1)
            copy_y(B - 1)

        @block.vector
        def _(dve):
            def norm_stats(b):
                for t in range(NT):
                    last = nc.vector.bn_stats(st[:, t], res[:, b, t])
                last.then_inc(stats, 1)
                dve.wait_ge(stats, b + 1)
                dve.sem_inc(seen)
                for t in range(NT):
                    last = nc.vector.bn_aggr(mv[:, t], st[:, t])
                last.then_inc(aggr, 1)

            def norm_apply(b):
                dve.wait_ge(rstd_ready, b + 1)
                dve.wait_ge(xT_done, b)
                dve.wait_ge(resid_ready, b)
                for t in range(NT):
                    last = nc.vector.tensor_scalar(xn[:, t], res[:, b, t], mv[:, t, 0:1], rstd[:, t:t + 1], ALU.subtract, ALU.mult)
                last.then_inc(xn_ready, 1)

            def scale_qk(b):
                dve.wait_ge(rms_ready, b + 1)
                for t in range(NT):
                    for w in range(2):
                        last = nc.vector.tensor_scalar(qk[:, t, w], qk[:, t, w], rms[:, w, t:t + 1], None, ALU.mult)
                last.then_inc(qk_ready, 1)

            def scale_v(b):
                for t in range(NT):
                    last = nc.vector.tensor_scalar(v[:, t], v_raw[:, t], rms[:, 2, t:t + 1], None, ALU.mult)
                last.then_inc(v_ready, 1)

            def gate_parts(b):
                dve.wait_ge(z_done, b + 1)
                nc.vector.tensor_scalar(zm[:].rearrange("p t h -> p (t h)"), c_z, 0.0, None, ALU.min).then_inc(z_step, 1)
                dve.wait_ge(z_step, b + 1)
                nc.vector.scalar_tensor_tensor(za[:].rearrange("p t h -> p (t h)"), c_z, 0.0, zm[:].rearrange("p t h -> p (t h)"),
                                               ALU.max, ALU.subtract).then_inc(z_ready, 1)

            def log_decay(b):
                dve.wait_ge(zl_ready, b + 1)
                dve.wait_ge(z_ready, b + 1)
                for s in (0, 2, 3):
                    last = nc.vector.tensor_tensor(ld[:, :, s, 0:H], zm[:], zl[:], ALU.subtract)
                last.then_inc(ld_ready, 1)

            def split_sums(b):
                f, fr = F[:].rearrange("p c i -> p (c i)"), Fr[:].rearrange("p c i -> p (c i)")
                dve.wait_ge(dec_ready, b + 1)
                dve.wait_ge(bcT_done, b + 1)
                nc.vector.tensor_copy(f, c_bcT).then_inc(f_step, 1)
                dve.wait_ge(f_step, b * 3 + 1)
                nc.vector.tensor_tensor(fr[64:P], c_bcT[64:P], f[64:P], ALU.subtract).then_inc(f_step, 1)
                dve.wait_ge(f_step, b * 3 + 2)
                nc.vector.tensor_copy(f[64:P], fr[64:P]).then_inc(f_step, 1)
                dve.wait_ge(f_step, b * 3 + 3)
                nc.vector.tensor_tensor(f[96:P], fr[96:P], f[96:P], ALU.subtract).then_inc(f_ready, 1)

            def attend(b, n):
                dve.wait_ge(exp_ready, b * U + n + 1)
                dve.wait_ge(s_done, b * U + n + 1)
                nc.vector.tensor_tensor(att[:, n % 2].rearrange("p h i -> p (h i)"), ps_s[:].rearrange("p a n -> p (a n)"),
                                        dexp[:, n % 2], ALU.mult).then_inc(att_raw, 1)

            def copy_state(b):
                dve.wait_ge(st_done, b + 1)
                nc.vector.tensor_tensor(state[:], ps_f[0][:, 0:2 * P].rearrange("p (f n) -> p f n", f=2),
                                        block_mask[:].unsqueeze(1).to_broadcast([P, 2, P]), ALU.mult).then_inc(state_ready, 1)

            def out_sums(b):
                dve.wait_ge(osq_ready, b + 1)
                nc.vector.tensor_reduce(oss[:], osq[:], AX.X, ALU.add).then_inc(oss_ready, 1)

            def gated_out(b):
                dve.wait_ge(orms_ready, b + 1)
                dve.wait_ge(o_ready, b + 1)
                dve.wait_ge(yT_done, b)
                nc.vector.tensor_tensor(y[:].rearrange("p t (h d) -> p (t h) d", d=HD),
                                        o_raw[:].rearrange("p t (h d) -> p (t h) d", d=HD),
                                        orms[:].rearrange("p t h -> p (t h)").unsqueeze(2).to_broadcast([P, NT * H, HD]),
                                        ALU.mult).then_inc(y_step, 1)
                dve.wait_ge(y_step, b + 1)
                nc.vector.tensor_tensor(y[:], y[:], sg[:], ALU.mult).then_inc(y_ready, 1)

            def silu_inverse(b):
                dve.wait_ge(eg_ready, b + 1)
                nc.vector.tensor_scalar(eg[:], eg[:], 1.0, None, ALU.add).then_inc(sg_step, 1)
                dve.wait_ge(sg_step, b * 2 + 1)
                nc.vector.reciprocal(eg[:], eg[:]).then_inc(sg_step, 1)

            def silu_gate(b):
                dve.wait_ge(sg_step, b * 2 + 2)
                nc.vector.tensor_tensor(sg[:], g_raw[:], eg[:], ALU.mult).then_inc(sg_ready, 1)

            def add_out(b):
                dve.wait_ge(resid_ready, b + 1)
                dve.wait_ge(w_done, b + 1)
                nc.vector.tensor_tensor(res[:, b], res[:, b], ps_f[0][:].rearrange("p (t d) -> p t d", t=NT), ALU.add)\
                    .then_inc(res_ready, 1)

            def body(b, prev, nxt, nxt2):
                nb = b + 1
                if prev:
                    out_sums(b - 1)
                attend(b, 0)
                if nxt2:
                    norm_stats(b + 2)
                silu_inverse(b)
                attend(b, 1)
                if nxt:
                    gate_parts(nb)
                if prev:
                    gated_out(b - 1)
                    dve.wait_ge(y_ready, b)
                silu_gate(b)
                if nxt:
                    log_decay(nb)
                dve.wait_ge(av_done, b * U + 1)
                attend(b, 2)
                if nxt2:
                    norm_apply(b + 2)
                if nxt:
                    scale_qk(nb)
                dve.wait_ge(av_done, b * U + 2)
                attend(b, 3)
                if prev:
                    add_out(b - 1)
                copy_state(b)
                if nxt:
                    dve.wait_ge(e_done, b * U + 4)
                    split_sums(nb)
                    dve.wait_ge(av_done, b * U + 4)
                    scale_v(nb)

            for b in range(2):
                norm_stats(b)
                norm_apply(b)
            dve.wait_ge(set_ready, 1)
            gate_parts(0)
            log_decay(0)
            scale_qk(0)
            split_sums(0)
            scale_v(0)
            dve.wait_ge(w_loaded, LOADED)
            steps(dve, body)
            out_sums(B - 1)
            gated_out(B - 1)
            add_out(B - 1)


def single_attention_weights(nc, ctx, S):
    shapes = {"bq": [P, KD], "bk": [P, KD], "wqT": [P, KD, D], "wk": [P, D], "wv": [P, D], "bv": [S, D]}
    w = {k: ctx.enter_context(nc.sbuf_tensor("E_" + k, shape, F32)) for k, shape in shapes.items()}
    return w, ctx.enter_context(nc.semaphore("E_w_loaded"))


def load_single_attention_weights(sp, nc, w, w_loaded, i):
    with nc.allow_non_contiguous_dma("biases, one element a partition"):
        sp.dma_start(w["bq"][:], i["L1_xattn_bq"].rearrange("(k p) -> p k", p=P)).then_inc(w_loaded, 16)
        sp.dma_start(w["bk"][:], i["L1_xattn_bk"].rearrange("(k p) -> p k", p=P)).then_inc(w_loaded, 16)
    sp.dma_start(w["wqT"][:], i["L1_xattn_WqT"].rearrange("(k p) n -> p k n", p=P)).then_inc(w_loaded, 16)
    sp.dma_start(w["wk"][:], i["L1_xattn_Wk"]).then_inc(w_loaded, 16)
    sp.dma_start(w["wv"][:], i["L1_xattn_Wv"]).then_inc(w_loaded, 16)
    S = w["bv"].shape[0]
    sp.dma_start(w["bv"][:], i["L1_xattn_bv"].rearrange("(a n) -> a n", a=1).partition_broadcast(S)).then_inc(w_loaded, 16)


def cross_attention_and_tokens(nc, res, ident, ctxT, w, w_loaded, logits, gammaT, betaT, gateT, x5_d, out):
    S = ctxT.shape[2]
    E = logits.shape[2]
    EPS = 1e-5
    GROUP = 4
    with ExitStack() as ctx:
        def sb(name, shape, dt=F32):
            return ctx.enter_context(nc.sbuf_tensor("E_" + name, shape, dt))

        def psum(name, shape):
            return ctx.enter_context(nc.psum_tensor("E_" + name, shape, F32))

        def sem(name):
            return ctx.enter_context(nc.semaphore("E_" + name))

        wqT, wk, wv, bq, bk, bv = (w[k] for k in ("wqT", "wk", "wv", "bq", "bk", "bv"))
        bq_rows = sb("bq_rows", [P, KD, P])
        half = sb("half", [P, 2, NT])
        eps = sb("eps", [P, 2, NT])
        eps_n = sb("eps_n", [P, 2, NT])
        st = sb("st", [P, 2, NT, 6])
        mv = sb("mv", [P, 2, NT, 2])
        veps = sb("veps", [P, 2, NT])
        rstd = sb("rstd", [P, 2, NT])
        r2 = sb("r2", [P, NT])
        v5 = sb("v5", [P, NT])
        v5eps = sb("v5eps", [P, 2, NT])
        rn = sb("rn", [P, 2, NT])
        scale_n = sb("scale_n", [P, 2, NT])
        xn = sb("xn", [P, NT, D])
        xT = sb("xT", [P, KD, T])
        ctx_cur = sb("ctx_cur", [P, S])
        kT = sb("kT", [P, KD, S])
        kq = sb("kq", [P, KD, S])
        v = sb("v", [S, D])
        nmx = sb("nmx", [P, NT])
        prob = sb("prob", [P, NT, S])
        rsum = sb("rsum", [P, NT])
        rinv = sb("rinv", [P, NT])
        pT = sb("pT", [S, NT, P])
        n5 = sb("n5", [P, NT, D])
        tokT = sb("tokT", [P, KD, T])
        fin = sb("fin", [P, B, NT, D])
        ps_x = psum("ps_x", [P, KD, T])
        ps_k = psum("ps_k", [P, 512])
        ps_kq = psum("ps_kq", [P, 512])
        ps_v = psum("ps_v", [P, 512])
        ps_s = psum("ps_s", [P, 512])
        ps_p = psum("ps_p", [P, 512])
        ps_o = psum("ps_o", [P, NT, D])
        ps_n = psum("ps_n", [P, KD, T])
        k_out, kq_out, s_out = (x[:, 0:2 * S].rearrange("p (k s) -> p k s", k=2) for x in (ps_k, ps_kq, ps_s))
        l_out = ps_k[:, 256:256 + NT * E].rearrange("p (t e) -> p t e", t=NT)

        set_ready, bias_ready, stats, seen, aggr, var_eps, rstd_ready, xn_ready, resid_ready, ctx_ready = map(
            sem, "set_ready bias_ready stats seen aggr var_eps rstd_ready xn_ready resid_ready ctx_ready".split())
        xT_done, k_done, kq_done, v_done, s_done, pT_done, o_done, nT_done, l_done = map(
            sem, "xT_done k_done kq_done v_done s_done pT_done o_done nT_done l_done".split())
        xT_ready, k_ready, kq_ready, v_ready, max_ready, exp_ready, pT_ready, inv_ready, res_ready = map(
            sem, "xT_ready k_ready kq_ready v_ready max_ready exp_ready pT_ready inv_ready res_ready".split())
        scale_step, scale_ready, n5_ready, x5_ready, tok_ready, l_ready, x5_out, fin_out = map(
            sem, "scale_step scale_ready n5_ready x5_ready tok_ready l_ready x5_out fin_out".split())

        block = ctx.enter_context(nc.Block())

        def steps(engine, body):
            def parts(b):
                return dict(att=b < B, nxt=b + 1 < B, nxt2=b + 2 < B, sums=1 <= b <= B, x5=2 <= b <= B + 1, tok=b >= 3)
            for b in range(3):
                body(b, **parts(b))
            with engine.Fori(3, B - 2) as b:
                body(b, att=True, nxt=True, nxt2=True, sums=True, x5=True, tok=True)
            for b in range(B - 2, B + 3):
                body(b, **parts(b))

        @block.sync
        def _(sp):
            for g in range(B // GROUP):
                group = slice(g * GROUP, (g + 1) * GROUP)
                sp.wait_ge(x5_ready, (g + 1) * GROUP)
                sp.dma_start(x5_d.rearrange("(b t p) d -> p b t d", p=P, t=NT)[:, group], res[:, group]).then_inc(x5_out, 16)
                sp.dma_start(out.rearrange("b (t p) d -> p b t d", p=P)[:, group], fin[:, group]).then_inc(fin_out, 16)
            for s in (x5_out, fin_out):
                sp.wait_ge(s, B // GROUP * 16)
        LOADED = 96

        @block.gpsimd
        def _(pool):
            def stage_context(b):
                pool.wait_ge(v_done, b)
                nc.gpsimd.tensor_copy(ctx_cur[:], ctxT[:, b]).then_inc(ctx_ready, 1)

            def norm_scale(n, lo, hi):
                pool.wait_ge(aggr, n + 1)
                nc.gpsimd.tensor_tensor(veps[:, lo:hi], mv[:, lo:hi, :, 1], eps[:, lo:hi], ALU.add).then_inc(var_eps, 1)
                pool.wait_ge(var_eps, n + 1)
                nc.gpsimd.tensor_tensor(rstd[:, lo:hi], veps[:, lo:hi], half[:, lo:hi], ALU.pow).then_inc(rstd_ready, 1)

            def x5_scales(b, n):
                pool.wait_ge(rstd_ready, n + 1)
                nc.gpsimd.tensor_tensor(r2[:], rstd[:, 1], rstd[:, 1], ALU.mult).then_inc(scale_step, 1)
                pool.wait_ge(scale_step, b * 4 + 1)
                nc.gpsimd.tensor_tensor(v5[:], r2[:], mv[:, 1, :, 1], ALU.mult).then_inc(scale_step, 1)
                pool.wait_ge(scale_step, b * 4 + 2)
                nc.gpsimd.tensor_tensor(v5eps[:], v5[:].unsqueeze(1).to_broadcast([P, 2, NT]), eps_n[:], ALU.add).then_inc(scale_step, 1)
                pool.wait_ge(scale_step, b * 4 + 3)
                nc.gpsimd.tensor_tensor(rn[:], v5eps[:], half[:], ALU.pow).then_inc(scale_step, 1)
                pool.wait_ge(scale_step, b * 4 + 4)
                nc.gpsimd.tensor_tensor(scale_n[:], rn[:], rstd[:, 1].unsqueeze(1).to_broadcast([P, 2, NT]), ALU.mult)\
                    .then_inc(scale_ready, 1)

            def keep_residual(b):
                pool.wait_ge(xn_ready, b + 1)
                nc.gpsimd.tensor_copy(res[:, b], xn[:]).then_inc(resid_ready, 1)

            def body(b, att, nxt, nxt2, sums, x5, tok):
                if nxt2:
                    stage_context(b + 2)
                if nxt2 or sums:
                    norm_scale(b + 2, 0 if nxt2 else 1, 2 if sums else 1)
                if sums:
                    x5_scales(b - 1, b + 2)
                if nxt2:
                    keep_residual(b + 2)

            nc.gpsimd.memset(half[:], -0.5)
            nc.gpsimd.memset(eps[:], EPS)
            nc.gpsimd.memset(eps_n[:, 0], EPS)
            nc.gpsimd.memset(eps_n[:, 1], EPS / 4).then_inc(set_ready, 1)
            pool.wait_ge(set_ready, 1)
            stage_context(0)
            for b in range(2):
                norm_scale(b, 0, 1)
                keep_residual(b)
            stage_context(1)
            steps(pool, body)

        @block.tensor
        def _(pe):
            def transpose_x(b):
                pe.wait_ge(xn_ready, b + 1)
                for k in range(KD):
                    for t in range(NT):
                        last = nc.tensor.transpose(ps_x[:, k, t * P:(t + 1) * P], xn[:, t, k * P:(k + 1) * P], ident[:])
                last.then_inc(xT_done, 1)

            def project_k(b):
                pe.wait_ge(ctx_ready, b + 1)
                for m in range(KD):
                    last = nc.tensor.matmul(k_out[:, m], wk[:, m * P:(m + 1) * P], ctx_cur[:], start=True, stop=True)
                last.then_inc(k_done, 1)

            def fold_q(b):
                pe.wait_ge(k_ready, b + 1)
                for m in range(KD):
                    for k in range(KD):
                        last = nc.tensor.matmul(kq_out[:, m], wqT[:, k, m * P:(m + 1) * P], kT[:, k], start=k == 0, stop=k == KD - 1)
                last.then_inc(kq_done, 1)

            def project_v(b):
                pe.wait_ge(v_ready, b)
                nc.tensor.matmul(ps_v[0:S, 0:D], ctx_cur[:], wv[:], start=True, stop=True).then_inc(v_done, 1)

            def scores(b):
                pe.wait_ge(xT_ready, b + 1)
                pe.wait_ge(kq_ready, b + 1)
                for t in range(NT):
                    for k in range(KD):
                        nc.tensor.matmul(s_out[:, t], xT[:, k, t * P:(t + 1) * P], kq[:, k], start=k == 0, stop=False)
                    for k in range(KD):
                        last = nc.tensor.matmul(s_out[:, t], bq_rows[:, k], kT[:, k], start=False, stop=k == KD - 1)
                last.then_inc(s_done, 1)

            def transpose_probs(b):
                pe.wait_ge(exp_ready, b * NT + NT)
                for t in range(NT):
                    last = nc.tensor.transpose(ps_p[0:S, t * P:(t + 1) * P], prob[:, t], ident[:])
                last.then_inc(pT_done, 1)

            def values(b):
                pe.wait_ge(pT_ready, b + 1)
                pe.wait_ge(v_ready, b + 1)
                pe.wait_ge(res_ready, b * NT)
                for t in range(NT):
                    last = nc.tensor.matmul(ps_o[:, t], pT[:, t], v[:], start=True, stop=True)
                last.then_inc(o_done, 1)

            def transpose_n5(b):
                pe.wait_ge(n5_ready, b + 1)
                for k in range(KD):
                    for t in range(NT):
                        last = nc.tensor.transpose(ps_n[:, k, t * P:(t + 1) * P], n5[:, t, k * P:(k + 1) * P], ident[:])
                last.then_inc(nT_done, 1)

            def route_logits(b):
                pe.wait_ge(tok_ready, b + 1)
                for t in range(NT):
                    for k in range(KD):
                        last = nc.tensor.matmul(l_out[:, t], tokT[:, k, t * P:(t + 1) * P], gateT[:, k], start=k == 0, stop=k == KD - 1)
                last.then_inc(l_done, 1)

            def body(b, att, nxt, nxt2, sums, x5, tok):
                if att:
                    scores(b)
                if tok:
                    pe.wait_ge(l_ready, b - 3)
                if nxt:
                    project_k(b + 1)
                if tok:
                    transpose_n5(b - 3)
                if nxt:
                    transpose_x(b + 1)
                    project_v(b + 1)
                if att:
                    transpose_probs(b)
                if nxt:
                    fold_q(b + 1)
                if tok:
                    route_logits(b - 3)
                if att:
                    values(b)

            pe.wait_ge(w_loaded, LOADED)
            pe.wait_ge(bias_ready, 1)
            transpose_x(0)
            project_k(0)
            fold_q(0)
            project_v(0)
            steps(pe, body)

        @block.scalar
        def _(act):
            def copy_x(b):
                act.wait_ge(xT_done, b + 1)
                nc.scalar.activation(xT[:], ps_x[:], ACT.Copy).then_inc(xT_ready, 1)

            def copy_k(b):
                act.wait_ge(k_done, b + 1)
                for m in range(KD):
                    last = nc.scalar.activation(kT[:, m], k_out[:, m], ACT.Identity, bias=bk[:, m:m + 1])
                last.then_inc(k_ready, 1)

            def copy_kq(b):
                act.wait_ge(kq_done, b + 1)
                nc.scalar.activation(kq[:], kq_out, ACT.Copy).then_inc(kq_ready, 1)

            def exponential(b):
                act.wait_ge(max_ready, b + 1)
                for t in range(NT):
                    nc.scalar.activation(prob[:, t], s_out[:, t], ACT.Exp, bias=nmx[:, t:t + 1],
                                         accum_out=rsum[:, t:t + 1]).then_inc(exp_ready, 1)

            def copy_pT(b):
                act.wait_ge(pT_done, b + 1)
                nc.scalar.activation(pT[:].rearrange("s t i -> s (t i)"), ps_p[0:S, 0:NT * P], ACT.Copy).then_inc(pT_ready, 1)

            def tokens(b):
                act.wait_ge(nT_done, b + 1)
                for k in range(KD):
                    last = nc.scalar.activation(tokT[:, k], ps_n[:, k], ACT.Identity, scale=gammaT[:, k:k + 1], bias=betaT[:, k:k + 1])
                last.then_inc(tok_ready, 1)

            def body(b, att, nxt, nxt2, sums, x5, tok):
                if nxt:
                    copy_k(b + 1)
                if att:
                    exponential(b)
                if tok:
                    tokens(b - 3)
                if att:
                    copy_pT(b)
                if nxt:
                    copy_x(b + 1)
                    copy_kq(b + 1)

            act.wait_ge(w_loaded, LOADED)
            copy_x(0)
            copy_k(0)
            copy_kq(0)
            steps(act, body)

        @block.vector
        def _(dve):
            def norm_stats(first, last_of):
                for i, b in enumerate((first, last_of)):
                    if b is not None:
                        for t in range(NT):
                            last = nc.vector.bn_stats(st[:, i, t], res[:, b, t])
                last.then_inc(stats, 1)

            def norm_aggregate(n, first, last_of):
                dve.wait_ge(stats, n + 1)
                dve.sem_inc(seen)
                for i, b in enumerate((first, last_of)):
                    if b is not None:
                        for t in range(NT):
                            last = nc.vector.bn_aggr(mv[:, i, t], st[:, i, t])
                last.then_inc(aggr, 1)

            def norm_apply(b):
                dve.wait_ge(rstd_ready, b + 1)
                dve.wait_ge(xT_done, b)
                dve.wait_ge(resid_ready, b)
                for t in range(NT):
                    last = nc.vector.tensor_scalar(xn[:, t], res[:, b, t], mv[:, 0, t, 0:1], rstd[:, 0, t:t + 1],
                                                   ALU.subtract, ALU.mult)
                last.then_inc(xn_ready, 1)

            def maxima(b):
                dve.wait_ge(s_done, b + 1)
                nc.vector.tensor_reduce(nmx[:], s_out, AX.X, ALU.max, negate=True).then_inc(max_ready, 1)

            def copy_v(b):
                dve.wait_ge(v_done, b + 1)
                nc.vector.tensor_tensor(v[:], ps_v[0:S, 0:D], bv[:], ALU.add).then_inc(v_ready, 1)

            def invert_sums(b):
                dve.wait_ge(exp_ready, b * NT + NT)
                nc.vector.reciprocal(rinv[:], rsum[:]).then_inc(inv_ready, 1)

            def add_out(b):
                dve.wait_ge(inv_ready, b + 1)
                dve.wait_ge(resid_ready, b + 1)
                dve.wait_ge(o_done, b + 1)
                for t in range(NT):
                    nc.vector.scalar_tensor_tensor(res[:, b, t], ps_o[:, t], rinv[:, t:t + 1], res[:, b, t],
                                                   ALU.mult, ALU.add).then_inc(res_ready, 1)

            def x5_apply(b):
                def scaled(dst, factor):
                    for t in range(NT):
                        last = nc.vector.tensor_scalar(dst[t], res[:, b, t], mv[:, 1, t, 0:1], factor[:, t:t + 1],
                                                       ALU.subtract, ALU.mult)
                    return last

                dve.wait_ge(scale_ready, b + 1)
                scaled([fin[:, b, t] for t in range(NT)], scale_n[:, 1])
                dve.wait_ge(nT_done, b)
                scaled([n5[:, t] for t in range(NT)], scale_n[:, 0]).then_inc(n5_ready, 1)
                scaled([res[:, b, t] for t in range(NT)], rstd[:, 1]).then_inc(x5_ready, 1)

            def copy_logits(b):
                dve.wait_ge(l_done, b + 1)
                nc.vector.tensor_copy(logits[:, bass.ds(b * NT, NT)], l_out).then_inc(l_ready, 1)

            def body(b, att, nxt, nxt2, sums, x5, tok):
                if att:
                    maxima(b)
                batches = (b + 2 if nxt2 else None, b - 1 if sums else None)
                if sums:
                    dve.wait_ge(res_ready, b * NT)
                if nxt2 or sums:
                    norm_stats(*batches)
                if x5:
                    x5_apply(b - 2)
                    dve.wait_ge(x5_ready, b - 1)
                if nxt2 or sums:
                    norm_aggregate(b + 2, *batches)
                if att:
                    invert_sums(b)
                if tok:
                    copy_logits(b - 3)
                if att:
                    add_out(b)
                if nxt:
                    copy_v(b + 1)
                if nxt2:
                    norm_apply(b + 2)

            dve.wait_ge(w_loaded, LOADED)
            nc.vector.tensor_copy(bq_rows[:], bq[:].unsqueeze(2).to_broadcast([P, KD, P])).then_inc(bias_ready, 1)
            for b in range(2):
                norm_stats(b, None)
                norm_aggregate(b, b, None)
                norm_apply(b)
            copy_v(0)
            steps(dve, body)


def load_experts(sp, wi, wo, w_in, wi_d, wo_d, e, u):
    sp.dma_start(wi[:, u], wi_d[e].rearrange("(k p) n -> p k n", p=P)).then_inc(w_in[u], 16)
    sp.dma_start(wo[:, u], wo_d[e].rearrange("(k p) n -> p k n", p=P)).then_inc(w_in[u], 16)


def route(nc, ones, logits, before, table, capacity, xg, prefetch):
    NTILE, E = logits.shape[1], logits.shape[2]
    NONE = 1 << 20
    TI, PARTS = capacity // P, 5
    MATCHES = 8
    with ExitStack() as ctx:
        def sb(name, shape, dt=F32):
            return ctx.enter_context(nc.sbuf_tensor("G_" + name, shape, dt))

        def sem(name):
            return ctx.enter_context(nc.semaphore("G_" + name))

        no_i = sb("no_i", [P, E], I32)
        no = sb("no", [P, E])
        no8 = sb("no8", [P, E])
        top = sb("top", [P, NTILE])
        is_top = sb("is_top", [P, NTILE, E])
        cand = sb("cand", [P, NTILE, E])
        first = sb("first", [P, NTILE])
        onehot = sb("onehot", [P, NTILE, E])
        shifted = sb("shifted", [P, NTILE, E])
        expo = sb("expo", [P, NTILE, E])
        esum = sb("esum", [P, NTILE])
        prob = sb("prob", [P, NTILE])
        run = [sb(f"run{i}", [P, NTILE, E]) for i in range(2)]
        tot = sb("tot", [P, NTILE, E])
        offset = sb("offset", [P, NTILE, E])
        ahead = sb("ahead", [P, NTILE, E])
        rank = sb("rank", [P, NTILE])
        rank_i = sb("rank_i", [P, capacity], I32)
        rank_no = sb("rank_no", [P, capacity], mybir.dt.float16)
        tile_i = sb("tile_i", [P, NTILE], I32)
        place_i = sb("place_i", [P, NTILE], I32)
        part = sb("part", [P, PARTS, NTILE])
        weight = sb("weight", [P, NTILE])
        rest = sb("rest", [P, NTILE])
        head = sb("head", [P, 2, NTILE], BF16)
        content = sb("content", [P, NTILE, PARTS * E], BF16)
        match = sb("match", [P, MATCHES, capacity], BF16)
        placed_f = sb("placed_f", [P, TI, PARTS * E])
        token = sb("token", [P, E, TI])
        empty = sb("empty", [P, E, TI])
        weight2 = sb("weight2", [P, E, TI])
        ps_in = ctx.enter_context(nc.psum_tensor("G_ps_in", [P, NTILE, E], F32))
        ps_tot = ctx.enter_context(nc.psum_tensor("G_ps_tot", [P, NTILE, E], F32))
        ps_place = ctx.enter_context(nc.psum_tensor("G_ps_place", [P, TI, 512], F32))
        consts, chain, shifted_ready, expo_ready, onehot_ready, parts_ready, content_ready, counted, match_ready, placed = map(
            sem, "consts chain shifted_ready expo_ready onehot_ready parts_ready content_ready counted match_ready placed".split())
        block = ctx.enter_context(nc.Block())

        @block.gpsimd
        def _(pool):
            nc.gpsimd.iota(no_i[:], [[1, E]], base=0, channel_multiplier=0).then_inc(consts, 1)
            nc.gpsimd.iota(rank_i[:], [[1, capacity]], base=0, channel_multiplier=0).then_inc(consts, 1)
            nc.gpsimd.iota(tile_i[:], [[1, NTILE]], base=0, channel_multiplier=0).then_inc(consts, 1)
            nc.gpsimd.iota(place_i[:], [[0, NTILE]], base=1, channel_multiplier=1).then_inc(consts, 1)
            nc.gpsimd.memset(xg[:], 0.0)
            pool.wait_ge(onehot_ready, 1)
            pool.wait_ge(parts_ready, 1)
            for k in range(PARTS):
                nc.gpsimd.tensor_tensor(content[:, :, k * E:(k + 1) * E], onehot[:],
                                        part[:, k].unsqueeze(2).to_broadcast([P, NTILE, E]), ALU.mult).then_inc(content_ready, 1)

        @block.sync
        def _(sp):
            prefetch(sp)

        @block.tensor
        def _(pe):
            pe.wait_ge(onehot_ready, 1)
            nc.tensor.matmul(ps_in[:], before[:], onehot[:], start=True, stop=True)
            nc.tensor.matmul(ps_tot[:], ones[:], onehot[:], start=True, stop=True).then_inc(counted, 1)

            def place(i, u, first=False, last=False):
                pe.wait_ge(match_ready, i + 1)
                for c in range(TI):
                    mm = nc.tensor.matmul(ps_place[:, c, 0:PARTS * E], match[:, u, c * P:(c + 1) * P], content[:, i],
                                          start=first, stop=last)
                mm.then_inc(placed, 1)

            pe.wait_ge(content_ready, PARTS)
            for u in range(MATCHES):
                place(u, u, first=u == 0)
            with pe.Fori(1, NTILE // MATCHES - 1) as j:
                for u in range(MATCHES):
                    place(j * MATCHES + u, u)
            for u in range(MATCHES):
                place(NTILE - MATCHES + u, u, last=u == MATCHES - 1)

        @block.scalar
        def _(act):
            act.wait_ge(shifted_ready, 1)
            nc.scalar.activation(expo[:], shifted[:], ACT.Exp).then_inc(expo_ready, 1)

        @block.vector
        def _(dve):
            count = [0]

            def then(ins):
                count[0] += 1
                ins.then_inc(chain, 1)
                dve.wait_ge(chain, count[0])

            def per_tile(x):
                return x[:].unsqueeze(2).to_broadcast([P, NTILE, E])

            def per_expert(x):
                return x[:].unsqueeze(1).to_broadcast([P, NTILE, E])

            dve.wait_ge(consts, 4)
            nc.vector.tensor_copy(rank_no[:], rank_i[:])
            nc.vector.tensor_copy(part[:, 0], tile_i[:])
            nc.vector.tensor_copy(part[:, 1], place_i[:])
            then(nc.vector.tensor_copy(no[:], no_i[:]))
            nc.vector.tensor_scalar(no8[:], no[:], float(E), None, ALU.add)
            then(nc.vector.tensor_reduce(top[:], logits[:], AX.X, ALU.max))
            nc.vector.tensor_tensor(shifted[:], logits[:], per_tile(top), ALU.subtract).then_inc(shifted_ready, 1)
            then(nc.vector.tensor_tensor(is_top[:], logits[:], per_tile(top), ALU.is_ge))
            then(nc.vector.scalar_tensor_tensor(cand[:], is_top[:], -float(E), per_expert(no8), ALU.mult, ALU.add))
            then(nc.vector.tensor_reduce(first[:], cand[:], AX.X, ALU.min))
            nc.vector.tensor_tensor(onehot[:], per_expert(no), per_tile(first), ALU.is_equal).then_inc(onehot_ready, 1)
            dve.wait_ge(expo_ready, 1)
            then(nc.vector.tensor_reduce(esum[:], expo[:], AX.X, ALU.add))
            then(nc.vector.reciprocal(prob[:], esum[:]))
            then(nc.vector.tensor_scalar(weight[:], prob[:], 0.5, None, ALU.mult))
            then(nc.vector.tensor_copy(head[:, 0], weight[:]))
            nc.vector.tensor_copy(part[:, 2], head[:, 0])
            then(nc.vector.tensor_tensor(rest[:], weight[:], head[:, 0], ALU.subtract))
            then(nc.vector.tensor_copy(head[:, 1], rest[:]))
            nc.vector.tensor_copy(part[:, 3], head[:, 1])
            nc.vector.tensor_tensor(part[:, 4], rest[:], head[:, 1], ALU.subtract).then_inc(parts_ready, 1)
            dve.wait_ge(counted, 1)
            then(nc.vector.tensor_copy(tot[:], ps_tot[:]))
            then(nc.vector.tensor_copy(run[0][:], tot[:]))
            k, i = 1, 0
            while k < NTILE:
                nc.vector.tensor_copy(run[1 - i][:, 0:k], run[i][:, 0:k])
                then(nc.vector.tensor_tensor(run[1 - i][:, k:], run[i][:, k:], run[i][:, 0:NTILE - k], ALU.add))
                k, i = 2 * k, 1 - i
            then(nc.vector.tensor_tensor(offset[:], run[i][:], tot[:], ALU.subtract))
            then(nc.vector.tensor_tensor(ahead[:], ps_in[:], offset[:], ALU.add))
            then(nc.vector.tensor_tensor(ahead[:], ahead[:], onehot[:], ALU.mult))
            then(nc.vector.tensor_reduce(rank[:], ahead[:], AX.X, ALU.add))

            def match_tile(i, u, first=False):
                if not first:
                    dve.wait_ge(placed, i - (MATCHES - 1))
                nc.vector.tensor_scalar(match[:, u], rank_no[:], rank[:, bass.ds(i, 1)], None, ALU.is_equal).then_inc(match_ready, 1)

            for u in range(MATCHES):
                match_tile(u, u, first=True)
            with dve.Fori(1, NTILE // MATCHES) as j:
                for u in range(MATCHES):
                    match_tile(j * MATCHES + u, u)
            dve.wait_ge(placed, NTILE)
            then(nc.vector.tensor_copy(placed_f[:], ps_place[:, :, 0:PARTS * E]))
            tile_no, place1, w0, w1, w2 = (placed_f[:, :, k * E:(k + 1) * E].rearrange("p c e -> p e c") for k in range(PARTS))
            slots = table[:].rearrange("p (e c) k -> p e c k", e=E)
            then(nc.vector.scalar_tensor_tensor(token[:], tile_no, float(P), place1, ALU.mult, ALU.add))
            then(nc.vector.tensor_scalar(empty[:], place1, 0.0, float(NONE), ALU.is_equal, ALU.mult))
            nc.vector.scalar_tensor_tensor(slots[:, :, :, 0], token[:], -1.0, empty[:], ALU.add, ALU.add)
            then(nc.vector.tensor_tensor(weight2[:], w0, w1, ALU.add))
            nc.vector.tensor_tensor(slots[:, :, :, 1].bitcast(F32), weight2[:], w2, ALU.add)


def moe_ffn(nc, ident, half, gammaT, betaT, table, x5_d, xg, wi, wo, w_in, wi_d, wo_d, out, capacity):
    E, _, I = wi_d.shape
    NTOK = x5_d.shape[0]
    TI, MI = capacity // P, I // P
    EPS = 1e-5
    rows = out.rearrange("b t d -> (b t) d")
    with ExitStack() as ctx:
        def sb(name, shape, dt=F32):
            return ctx.enter_context(nc.sbuf_tensor("H_" + name, shape, dt))

        def psum(name, shape):
            return ctx.enter_context(nc.psum_tensor("H_" + name, shape, F32))

        def sem(name):
            return ctx.enter_context(nc.semaphore("H_" + name))

        slots = sb("slots", [P, 2, TI, 2], I32)
        to_slots = sb("to_slots", [P, TI, 2], I32)
        ng = sb("ng", [P, TI, D])
        tokT = sb("tokT", [P, KD, capacity])
        hT = sb("hT", [P, MI, capacity])
        fin = sb("fin", [P, TI, D])
        st = sb("st", [P, TI, 6])
        mv = sb("mv", [P, TI, 2])
        veps = sb("veps", [P, TI])
        rstd = sb("rstd", [P, TI])
        ps_x = [psum(f"ps_x{i}", [P, capacity]) for i in range(KD)]
        ps_h = [psum(f"ps_h{i}", [P, capacity]) for i in range(2)]
        ps_d = [psum(f"ps_d{i}", [P, 2, D]) for i in range(TI // 2)]
        gathered0, gathered1, staged, kept, scattered = map(
            sem, "gathered0 gathered1 staged kept scattered".split())
        stats, seen, aggr, var_eps, rstd_ready, ng_ready, xT_done, tok_ready, h_done, h_ready, d_done, sum_ready, fin_ready = map(
            sem, "stats seen aggr var_eps rstd_ready ng_ready xT_done tok_ready h_done h_ready d_done sum_ready fin_ready".split())
        gathered = (gathered0, gathered1)

        block = ctx.enter_context(nc.Block())

        @block.sync
        def _(sp):
            with sp.Fori(0, E // 2 - 1) as j:
                for u in range(2):
                    sp.wait_ge(d_done, j * 2 * TI + (u + 1) * TI)
                    load_experts(sp, wi, wo, w_in, wi_d, wo_d, j * 2 + (2 + u), u)

        @block.gpsimd
        def _(pool):
            def norm_scale(n, eps):
                pool.wait_ge(aggr, n + 1)
                pool.sem_inc(seen)
                nc.gpsimd.tensor_scalar(veps[:], mv[:, :, 1], eps, None, ALU.add).then_inc(var_eps, 1)
                pool.wait_ge(var_eps, n + 1)
                for i in range(TI // NT):
                    last = nc.gpsimd.tensor_tensor(rstd[:, i * NT:(i + 1) * NT], veps[:, i * NT:(i + 1) * NT], half[:], ALU.pow)
                last.then_inc(rstd_ready, 1)

            def gather(e, u, n):
                if n is None:
                    pool.wait_ge(kept, e - 1)
                    pool.sem_inc(seen)
                nc.gpsimd.tensor_copy(slots[:, u], table[:, bass.ds(e * TI, TI)] if n is None else table[:, n * TI:(n + 1) * TI])\
                    .then_inc(staged, 1)
                pool.wait_ge(staged, e + 1)
                pool.sem_inc(seen)
                for i in range(TI):
                    nc.gpsimd.indirect_dma_start(out=xg[:, u, i], out_offset=None, in_=x5_d,
                                                 in_offset=bass.IndirectOffsetOnAxis(ap=slots[:, u, i, 0:1], axis=0),
                                                 bounds_check=NTOK - 1, oob_is_err=False).then_inc(gathered[u], 16)

            def keep_slots(e, u):
                pool.wait_ge(fin_ready, e + 1)
                pool.wait_ge(scattered, e * TI * 16)
                pool.sem_inc(seen)
                nc.gpsimd.tensor_copy(to_slots[:], slots[:, u]).then_inc(kept, 1)

            def scatter(e):
                pool.wait_ge(kept, e + 1)
                pool.sem_inc(seen)
                for i in range(TI):
                    nc.gpsimd.indirect_dma_start(out=rows, out_offset=bass.IndirectOffsetOnAxis(ap=to_slots[:, i, 0:1], axis=0),
                                                 in_=fin[:, i], in_offset=None, bounds_check=NTOK - 1,
                                                 oob_is_err=False).then_inc(scattered, 16)

            def body(e, u, more, more2):
                if more:
                    norm_scale(e * 2 + 1, EPS)
                norm_scale(e * 2 + 2 if more else E * 2 - 1, EPS / 4)
                keep_slots(e, u)
                if more2:
                    gather(e + 2, u, None)
                scatter(e)

            gather(0, 0, 0)
            gather(1, 1, 1)
            norm_scale(0, EPS)
            with pool.Fori(0, E // 2 - 1) as j:
                body(j * 2, 0, True, True)
                body(j * 2 + 1, 1, True, True)
            body(E - 2, 0, True, False)
            body(E - 1, 1, False, False)
            pool.wait_ge(scattered, 16 * TI * E)

        @block.tensor
        def _(pe):
            def transpose(e):
                pe.wait_ge(ng_ready, e + 1)
                for k in range(KD):
                    for t in range(TI):
                        last = nc.tensor.transpose(ps_x[k][:, t * P:(t + 1) * P], ng[:, t, k * P:(k + 1) * P], ident[:])
                last.then_inc(xT_done, 1)

            def hidden(e, u, m, first):
                if not (first and m < 2):
                    pe.wait_ge(h_ready, e * MI + (m - 1))
                for k in range(KD):
                    last = nc.tensor.matmul(ps_h[m % 2][:], wi[:, u, k, m * P:(m + 1) * P], tokT[:, k], start=k == 0, stop=k == KD - 1)
                last.then_inc(h_done, 1)

            def down(e, u, first, tiles):
                for t in tiles:
                    if t % 2 == 0 and not first:
                        pe.wait_ge(sum_ready, e * TI + (t + 2 - TI))
                    for m in range(MI):
                        if t == 0 and m >= MI - 2:
                            pe.wait_ge(h_ready, e * MI + m + 1)
                        elif t == 0 and m == 0:
                            pe.wait_ge(h_ready, e * MI + MI - 2)
                        last = nc.tensor.matmul(ps_d[t // 2][:, t % 2], hT[:, m, t * P:(t + 1) * P], wo[:, u, m],
                                                start=m == 0, stop=m == MI - 1)
                    last.then_inc(d_done, 1)

            def body(e, u, j, first=False, more=True):
                pe.wait_ge(w_in[u], j * 32 + 32)
                pe.wait_ge(tok_ready, e + 1)
                for m in range(MI):
                    hidden(e, u, m, first)
                down(e, u, first, range(TI // 2))
                if more:
                    transpose(e + 1)
                down(e, u, first, range(TI // 2, TI))

            transpose(0)
            body(0, 0, 0, first=True)
            body(1, 1, 0)
            with pe.Fori(1, E // 2 - 1) as j:
                body(j * 2, 0, j)
                body(j * 2 + 1, 1, j)
            body(E - 2, 0, E // 2 - 1)
            body(E - 1, 1, E // 2 - 1, more=False)

        @block.scalar
        def _(act):
            def tokens(e):
                act.wait_ge(xT_done, e + 1)
                for k in range(KD):
                    last = nc.scalar.activation(tokT[:, k], ps_x[k][:], ACT.Identity, scale=gammaT[:, k:k + 1], bias=betaT[:, k:k + 1])
                last.then_inc(tok_ready, 1)

            def body(e, more):
                for m in range(MI):
                    act.wait_ge(h_done, e * MI + m + 1)
                    nc.scalar.activation(hT[:, m], ps_h[m % 2][:], ACT.Gelu).then_inc(h_ready, 1)
                if more:
                    tokens(e + 1)

            tokens(0)
            with act.Fori(0, E - 1) as e:
                body(e, True)
            body(E - 1, False)

        @block.vector
        def _(dve):
            def norm(src, dst, n, ready):
                for t in range(TI):
                    last = nc.vector.bn_stats(st[:, t], src[:, t])
                last.then_inc(stats, 1)
                dve.wait_ge(stats, n + 1)
                dve.sem_inc(seen)
                for t in range(TI):
                    last = nc.vector.bn_aggr(mv[:, t], st[:, t])
                last.then_inc(aggr, 1)
                dve.wait_ge(rstd_ready, n + 1)
                for t in range(TI):
                    last = nc.vector.tensor_scalar(dst[:, t], src[:, t], mv[:, t, 0:1], rstd[:, t:t + 1], ALU.subtract, ALU.mult)
                last.then_inc(ready, 1)

            def before(e, u, j, n):
                dve.wait_ge(gathered[u], j * TI * 16 + TI * 16)
                dve.wait_ge(xT_done, e)
                norm(xg[:, u], ng[:], n, ng_ready)

            def after(e, u, n, first):
                for t in range(TI):
                    dve.wait_ge(d_done, e * TI + 2 * (t // 2) + 2)
                    nc.vector.scalar_tensor_tensor(xg[:, u, t], ps_d[t // 2][:, t % 2], slots[:, u, t, 1:2].bitcast(F32), xg[:, u, t],
                                                   ALU.mult, ALU.add).then_inc(sum_ready, 1)
                dve.wait_ge(sum_ready, e * TI + TI)
                if not first:
                    dve.wait_ge(scattered, e * TI * 16)
                norm(xg[:, u], fin[:], n, fin_ready)

            before(0, 0, 0, 0)
            before(1, 1, 0, 1)
            after(0, 0, 2, True)
            with dve.Fori(1, E // 2) as j:
                before(j * 2, 0, j, j * 4 - 1)
                after(j * 2 - 1, 1, j * 4, False)
                before(j * 2 + 1, 1, j, j * 4 + 1)
                after(j * 2, 0, j * 4 + 2, False)
            after(E - 1, 1, E * 2 - 1, False)


def clear_used_semaphores(nc):
    used = sorted(nc.released_uncleared_semaphores)
    with nc.Block() as block:
        @block.gpsimd
        def _(pool):
            start = 0
            for n in range(1, len(used) + 1):
                if n == len(used) or used[n] != used[n - 1] + 1:
                    pool.sem_clear(range(used[start], used[n - 1] + 1))
                    start = n


def program(nc, i, out):
    with ExitStack() as ctx:
        res = ctx.enter_context(nc.sbuf_tensor("res", [P, B, NT, D], F32))
        ident = ctx.enter_context(nc.sbuf_tensor("ident", [P, P], F32))
        ones = ctx.enter_context(nc.sbuf_tensor("ones", [P, P], F32))
        half = ctx.enter_context(nc.sbuf_tensor("half", [P, NT], F32))
        eps = ctx.enter_context(nc.sbuf_tensor("eps", [P, NT], F32))
        ctxT = ctx.enter_context(nc.sbuf_tensor("ctxT", [P, B, i["ctxT"].shape[2]], F32))
        set_ready = ctx.enter_context(nc.semaphore("set_ready"))
        ctx_loaded = ctx.enter_context(nc.semaphore("ctx_loaded"))
        with nc.Block() as block:
            @block.gpsimd
            def _(pool):
                nc.gpsimd.memset(half[:], -0.5)
                nc.gpsimd.memset(eps[:], 1e-5)
                nc.gpsimd.memset(ones[:], 1.0).then_inc(set_ready, 1)
                pool.wait_ge(set_ready, 1)
                nc.gpsimd.affine_select(out=ident[:], in_=ones[:], compare_op=ALU.is_equal, fill=0.0, base=0,
                                        pattern=[[-1, P]], channel_multiplier=1)

        with ExitStack() as cross:
            w, w_loaded = cross_attention_weights(nc, cross, i["L0_xattn_Wq"].shape[1])

            def prefetch_cross(sp):
                sp.dma_start(ctxT[:], i["ctxT"].rearrange("b p s -> p b s")).then_inc(ctx_loaded, 16)
                load_cross_attention_weights(sp, w, w_loaded, i)
            linear_attention(nc, res, ident, i["x"], i["L0_attn_W_thetaT"], i["L0_attn_W_phiT"], i["L0_attn_W_gT"], prefetch_cross)
            cross_attention(nc, res, ident, half, eps, ctxT, ctx_loaded, w, w_loaded)

        NTOK, E = B * T, i["L1_ffn_wi"].shape[0]
        before = ctx.enter_context(nc.sbuf_tensor("before", [P, P], F32))
        gateT = ctx.enter_context(nc.sbuf_tensor("gateT", [P, KD, E], F32))
        gammaT = ctx.enter_context(nc.sbuf_tensor("gammaT", [P, KD], F32))
        betaT = ctx.enter_context(nc.sbuf_tensor("betaT", [P, KD], F32))
        table = ctx.enter_context(nc.sbuf_tensor("table", [P, E * CAPACITY // P, 2], I32))
        logits = ctx.enter_context(nc.sbuf_tensor("logits", [P, NTOK // P, E], F32))
        with ExitStack() as single:
            w5, w5_loaded = single_attention_weights(nc, single, ctxT.shape[2])
            gate_loaded = single.enter_context(nc.semaphore("gate_loaded"))

            def prefetch_single(sp):
                load_single_attention_weights(sp, nc, w5, w5_loaded, i)
                sp.dma_start(before[:], i["before"]).then_inc(gate_loaded, 16)
                with nc.allow_non_contiguous_dma("small: the router's weights, one element a partition"):
                    sp.dma_start(gateT[:], i["L1_ffn_gateT"].rearrange("(k p) e -> p k e", p=P)).then_inc(gate_loaded, 16)
                    sp.dma_start(gammaT[:], i["L1_ffn_ln_gamma"].rearrange("(k p) -> p k", p=P)).then_inc(gate_loaded, 16)
                    sp.dma_start(betaT[:], i["L1_ffn_ln_beta"].rearrange("(k p) -> p k", p=P)).then_inc(gate_loaded, 16)
                sp.wait_ge(gate_loaded, 64)

            with ExitStack() as retention:
                w, w_loaded = retention_weights(nc, retention)
                expert_ffn(nc, res, ident, half, i["L0_ffn_router_indices"], i["L0_ffn_routing_weights"], i["L0_ffn_gate_up"],
                           i["L0_ffn_gate_up_bias"], i["L0_ffn_down_proj"], i["L0_ffn_down_proj_bias"],
                           lambda sp: load_retention_weights(sp, w, w_loaded, i))
                gated_retention(nc, res, ident, half, eps, w, w_loaded, prefetch_single)

            x5_d = nc.dram_tensor("x5_d", (NTOK, D), F32, kind="Internal").ap()
            clear_used_semaphores(nc)
            cross_attention_and_tokens(nc, res, ident, ctxT, w5, w5_loaded, logits, gammaT, betaT, gateT, x5_d, out)

        wi_d, wo_d = i["L1_ffn_wi"], i["L1_ffn_wo"]
        I = wi_d.shape[2]
        xg = ctx.enter_context(nc.sbuf_tensor("xg", [P, 2, CAPACITY // P, D], F32))
        wi = ctx.enter_context(nc.sbuf_tensor("wi", [P, 2, KD, I], F32))
        wo = ctx.enter_context(nc.sbuf_tensor("wo", [P, 2, I // P, D], F32))
        w_in = [ctx.enter_context(nc.semaphore(f"w_in{u}")) for u in range(2)]

        def prefetch_experts(sp):
            for e in range(2):
                load_experts(sp, wi, wo, w_in, wi_d, wo_d, e, e)
        route(nc, ones, logits, before, table, CAPACITY, xg, prefetch_experts)
        moe_ffn(nc, ident, half, gammaT, betaT, table, x5_d, xg, wi, wo, w_in, wi_d, wo_d, out, CAPACITY)


CAPACITY = 512


def kernel(**inputs):
    import ml_dtypes
    import numpy as np
    import concourse.bacc as bacc
    from concourse.bass_utils import run_bass_kernel_spmd

    nc = bacc.Bacc("TRN2", target_bir_lowering=False, num_devices=1)
    given = {k: np.asarray(v) for k, v in inputs.items()}
    arrays = {k: given[k] for k in ("x", "L0_xattn_Wq", "L0_xattn_Wk", "L0_xattn_Wv", "L0_xattn_Wo", "L0_xattn_bo")}
    arrays["ctxT"] = given["ctx_512"].transpose(0, 2, 1)
    for k in ("L0_attn_W_theta", "L0_attn_W_phi", "L0_attn_W_g"):
        arrays[k + "T"] = given[k].T
    for k in ("L0_ffn_router_indices", "L0_ffn_routing_weights", "L0_ffn_down_proj", "L0_ffn_down_proj_bias"):
        arrays[k] = given[k]
    w, bias = given["L0_ffn_gate_up_proj"], given["L0_ffn_gate_up_proj_bias"]
    arrays["L0_ffn_gate_up"] = np.concatenate([w[..., ::2], w[..., 1::2]], -1)
    arrays["L0_ffn_gate_up_bias"] = np.concatenate([bias[:, ::2], bias[:, 1::2]], -1).reshape(len(bias), -1, P).transpose(2, 0, 1)
    for k in ("L1_xattn_bq", "L1_xattn_Wk", "L1_xattn_bk", "L1_xattn_Wv", "L1_xattn_bv", "L1_ffn_ln_gamma", "L1_ffn_ln_beta",
              "L1_ffn_wi", "L1_ffn_wo"):
        arrays[k] = given[k]
    arrays["L1_xattn_WqT"], arrays["L1_ffn_gateT"] = given["L1_xattn_Wq"].T, given["L1_ffn_gate_weight"].T
    arrays["L1_attn_wqk"] = np.concatenate([given["L1_attn_Wq"], given["L1_attn_Wk"]], 1)
    arrays["L1_attn_wvg"] = np.concatenate([given["L1_attn_Wv"], given["L1_attn_Wg"]], 1)
    arrays["L1_attn_wgt"], arrays["L1_attn_wo"] = given["L1_attn_Wgt"], given["L1_attn_Wo"]
    row, col = np.arange(P)[:, None], np.arange(P)[None, :]
    arrays["before"] = (row < col).astype(np.float32)
    arrays["upto"] = ((row <= col) / 16).astype(np.float32)
    arrays["after"] = ((row > col) / 16).astype(np.float32)
    arrays["head_mask"] = ((row // RET_D % 2 == np.arange(2)) / 4).astype(np.float32)
    arrays["block_mask"] = ((row // RET_D == col // RET_D) / 4).astype(np.float32)
    heads = np.array([retention_head(p) for p in range(RET_H)])
    of_head = (row % 32 == heads) & (row // 32 != 1)
    arrays["sel"] = np.repeat(of_head[:, :, None], P, 2).astype(ml_dtypes.bfloat16)
    arrays["nsel"] = -arrays["sel"]
    arrays = {k: np.ascontiguousarray(a) for k, a in arrays.items()}
    ins = {k: nc.dram_tensor("in_" + k, a.shape, mybir.dt.from_np(a.dtype), kind="ExternalInput").ap() for k, a in arrays.items()}
    out = nc.dram_tensor("out", (B, T, D), F32, kind="ExternalOutput").ap()
    program(nc, ins, out)
    r = run_bass_kernel_spmd(nc, [{"in_" + k: a for k, a in arrays.items()}], core_ids=[0])
    return r.results[0]["out"]
```
